# Optimizing a Trainium2 kernel written in Bass

```python
import numpy as np
import jax
import jax.numpy as jnp

def _softmax(x, axis=-1):
    return jax.nn.softmax(x, axis=axis)

def _gelu(x):
    return jax.nn.gelu(x, approximate=True)

def _silu(x):
    return jax.nn.silu(x)

def _sigmoid(x):
    return jax.nn.sigmoid(x)

def _layernorm(x, axis=-1, eps=1e-05):
    m = jnp.mean(x, axis=axis, keepdims=True)
    v = jnp.var(x, axis=axis, keepdims=True)
    return (x - m) / jnp.sqrt(v + eps)

def _scatter_add(tgt, idx, src, axis=0):
    return tgt.at[idx].add(src)

def _segment_sum(src, seg, n):
    return jax.ops.segment_sum(src, seg, n)
kernel_name = 'mk_adj_ffn_d2_adj_r2_4f2064'

def setup_inputs(seed: int=0):
    np.random.seed(seed)
    _w = jnp.asarray

    def _rec_inputs():
        import jax
        import jax.numpy as jnp
        _gk = jax.random.key(seed)
        x = -0.0002928 + 1 * jax.random.normal(jax.random.fold_in(_gk, 1), (2048, 512), jnp.float32)
        _a = jax.random.bernoulli(jax.random.fold_in(_gk, 2), 0.0078125, (2048, 2048))
        _af = _a.astype(jnp.float32)
        adj = _af
        return (x, adj)
    x, adj = _rec_inputs()

    def _L0_gnn_setup():
        import jax, jax.numpy as jnp
        import numpy as np
        N = 2048
        D_IN = 512
        H = 16
        DH = D_IN // H
        ALPHA = 0.2
        MASK_VAL = -65500.0
        key = jax.random.key(seed)
        ks = jax.random.split(key, 7)
        x = jax.random.normal(ks[0], (N, D_IN), dtype=jnp.float32)
        adj = jax.random.randint(ks[1], (N, N), 0, 2).astype(jnp.float32)
        s = 1.0 / np.sqrt(D_IN)
        W_seq = jax.random.normal(ks[2], (D_IN, D_IN), dtype=jnp.float32) * s
        a1 = jax.random.normal(ks[3], (DH,), dtype=jnp.float32) / np.sqrt(DH)
        a2 = jax.random.normal(ks[4], (DH,), dtype=jnp.float32) / np.sqrt(DH)
        W_out = jax.random.normal(ks[5], (D_IN, D_IN), dtype=jnp.float32) * s
        b_out = jax.random.normal(ks[6], (D_IN,), dtype=jnp.float32) * 0.01
        return {'x': x, 'adj': adj, 'W_seq': W_seq, 'a1': a1, 'a2': a2, 'W_out': W_out, 'b_out': b_out}
    _L0_gnn_all = _L0_gnn_setup()
    _L0_gnn_in = {k: v for k, v in _L0_gnn_all.items() if k in ('W_seq', 'a1', 'a2', 'W_out', 'b_out')}
    del _L0_gnn_all

    def _L0_ffn_setup():
        import jax, jax.numpy as jnp
        import numpy as np
        TOP_K = 2
        NUM_EXPERTS = 8
        NORM_TOPK_PROB = True
        key = jax.random.key(seed)
        k0, k1, k2, k3, k4 = jax.random.split(key, 5)
        B, S, H, I, E = (2, 256, 512, 384, NUM_EXPERTS)
        scale = 0.02
        return {'hidden_states': jax.random.normal(k0, (B, S, H), dtype=jnp.float32), 'gate_w': jax.random.normal(k1, (H, E), dtype=jnp.float32) * scale, 'w_gate': jax.random.normal(k2, (E, H, I), dtype=jnp.float32) * scale, 'w_up': jax.random.normal(k3, (E, H, I), dtype=jnp.float32) * scale, 'w_down': jax.random.normal(k4, (E, I, H), dtype=jnp.float32) * scale}
    _L0_ffn_all = _L0_ffn_setup()
    _L0_ffn_in = {k: v for k, v in _L0_ffn_all.items() if k in ('gate_w', 'w_gate', 'w_up', 'w_down')}
    del _L0_ffn_all

    def _L1_gnn_setup():
        import jax, jax.numpy as jnp
        import numpy as np
        N = 4096
        D = 512

        def adjacent_mat(adj):
            adj = adj + jnp.eye(adj.shape[0], dtype=adj.dtype)
            deg = jnp.sum(adj, axis=1)
            dinv = jnp.where(deg > 0, deg ** (-0.5), 0.0).astype(adj.dtype)
            return dinv[:, None] * adj * dinv[None, :]
        key = jax.random.key(seed)
        k1, k2 = jax.random.split(key)
        x = jax.random.normal(k1, (N, D), dtype=jnp.float32)
        Coefficient2 = 1e-08 * jnp.ones((N, N), dtype=jnp.float32)
        A = jax.random.uniform(k2, (N, N), dtype=jnp.float32)
        return {'x': x, 'Coefficient2': Coefficient2, 'A': A}
    _L1_gnn_all = _L1_gnn_setup()
    _L1_gnn_in = {k: v for k, v in _L1_gnn_all.items() if k in ()}
    del _L1_gnn_all

    def _L1_ffn_setup():
        import jax, jax.numpy as jnp
        import numpy as np
        E = 8
        K = 2
        CAP_FACTOR = 1.0
        key = jax.random.key(seed)
        ks = jax.random.split(key, 5)
        B, T, C, H = (4, 1024, 512, 2048)
        x = jax.random.normal(ks[0], (B, T, C), dtype=jnp.float32)
        Wr = jax.random.normal(ks[1], (C, E), dtype=jnp.float32) * 0.02
        br = jnp.zeros((E,), jnp.float32)
        W1 = jax.random.normal(ks[2], (E, C, H), dtype=jnp.float32) * 0.02
        b1 = jnp.zeros((E, H), jnp.float32)
        W2 = jax.random.normal(ks[3], (E, H, C), dtype=jnp.float32) * 0.02
        b2 = jnp.zeros((E, C), jnp.float32)
        return {'x': x, 'Wr': Wr, 'br': br, 'W1': W1, 'b1': b1, 'W2': W2, 'b2': b2}
    _L1_ffn_all = _L1_ffn_setup()
    _L1_ffn_in = {k: v for k, v in _L1_ffn_all.items() if k in ('Wr', 'br', 'W1', 'b1', 'W2', 'b2')}
    del _L1_ffn_all
    return {'x': x, 'adj': adj, 'L0_gnn_W_seq': _L0_gnn_in['W_seq'], 'L0_gnn_a1': _L0_gnn_in['a1'], 'L0_gnn_a2': _L0_gnn_in['a2'], 'L0_gnn_W_out': _L0_gnn_in['W_out'], 'L0_gnn_b_out': _L0_gnn_in['b_out'], 'L0_ffn_gate_w': _L0_ffn_in['gate_w'], 'L0_ffn_w_gate': _L0_ffn_in['w_gate'], 'L0_ffn_w_up': _L0_ffn_in['w_up'], 'L0_ffn_w_down': _L0_ffn_in['w_down'], 'L1_ffn_Wr': _L1_ffn_in['Wr'], 'L1_ffn_br': _L1_ffn_in['br'], 'L1_ffn_W1': _L1_ffn_in['W1'], 'L1_ffn_b1': _L1_ffn_in['b1'], 'L1_ffn_W2': _L1_ffn_in['W2'], 'L1_ffn_b2': _L1_ffn_in['b2']}

def reference(x, adj, L0_gnn_W_seq, L0_gnn_a1, L0_gnn_a2, L0_gnn_W_out, L0_gnn_b_out, L0_ffn_gate_w, L0_ffn_w_gate, L0_ffn_w_up, L0_ffn_w_down, L1_ffn_Wr, L1_ffn_br, L1_ffn_W1, L1_ffn_b1, L1_ffn_W2, L1_ffn_b2):
    import jax
    import jax.numpy as jnp

    def _L0_gnn_ref(x, adj, W_seq, a1, a2, W_out, b_out):
        import jax, jax.numpy as jnp
        import numpy as np
        N = 2048
        D_IN = 512
        H = 16
        DH = D_IN // H
        ALPHA = 0.2
        MASK_VAL = -65500.0
        seq = (x @ W_seq).reshape(N, H, DH)
        score1 = jnp.einsum('nhd,d->hn', seq, a1)
        score2 = jnp.einsum('nhd,d->hn', seq, a2)
        scores = score1[:, :, None] + score2[:, None, :]
        scores = jax.nn.leaky_relu(scores, negative_slope=ALPHA)
        scores = scores + (1.0 - adj)[None, :, :] * MASK_VAL
        attn = jax.nn.softmax(scores, axis=-1)
        hidden = jnp.einsum('hij,jhd->ihd', attn, seq).reshape(N, D_IN)
        hidden = hidden @ W_out + b_out
        return jax.nn.elu(hidden)

    def _L0_ffn_ref(hidden_states, gate_w, w_gate, w_up, w_down):
        import jax, jax.numpy as jnp
        import numpy as np
        TOP_K = 2
        NUM_EXPERTS = 8
        NORM_TOPK_PROB = True
        orig_shape = hidden_states.shape
        H = orig_shape[-1]
        x = hidden_states.reshape(-1, H)
        E = gate_w.shape[-1]
        router_logits = x @ gate_w
        routing_probs = jax.nn.softmax(router_logits.astype(jnp.float32), axis=-1)
        routing_weights, selected_experts = jax.lax.top_k(routing_probs, TOP_K)
        if NORM_TOPK_PROB:
            routing_weights = routing_weights / routing_weights.sum(axis=-1, keepdims=True)
        routing_weights = routing_weights.astype(x.dtype)
        cw = (jax.nn.one_hot(selected_experts, E, dtype=x.dtype) * routing_weights[..., None]).sum(axis=1)
        g = jnp.einsum('th,ehi->tei', x, w_gate)
        u = jnp.einsum('th,ehi->tei', x, w_up)
        a = jax.nn.silu(g) * u
        y = jnp.einsum('tei,eih->teh', a, w_down)
        out = jnp.einsum('te,teh->th', cw, y)
        return out.reshape(orig_shape)

    def _L1_gnn_ref(x, Coefficient2, A):
        import jax, jax.numpy as jnp
        import numpy as np
        N = 4096
        D = 512

        def adjacent_mat(adj):
            adj = adj + jnp.eye(adj.shape[0], dtype=adj.dtype)
            deg = jnp.sum(adj, axis=1)
            dinv = jnp.where(deg > 0, deg ** (-0.5), 0.0).astype(adj.dtype)
            return dinv[:, None] * adj * dinv[None, :]
        A_c = jax.lax.stop_gradient(A)
        adj = adjacent_mat((A_c + A_c.T) * 0.5)
        y = Coefficient2 @ adj
        y = y @ x
        return y

    def _L1_ffn_ref(x, Wr, br, W1, b1, W2, b2):
        import jax, jax.numpy as jnp
        import numpy as np
        E = 8
        K = 2
        CAP_FACTOR = 1.0
        B, T, C = x.shape
        N = B * T
        xf = x.reshape(N, C)
        logits = xf @ Wr + br
        topv, topi = jax.lax.top_k(logits, K)
        gates = jax.nn.softmax(topv, axis=-1)
        rw = jnp.zeros((N, E), xf.dtype).at[jnp.arange(N)[:, None], topi].set(gates)
        cap = int(N * K / E * CAP_FACTOR)
        sel = jax.nn.one_hot(topi, E, dtype=jnp.int32).sum(1)
        rank = jnp.cumsum(sel, axis=0) - sel
        keep = (sel > 0) & (rank < cap)
        tok = jnp.broadcast_to(jnp.arange(N, dtype=jnp.int32)[:, None], (N, E))
        eid = jnp.broadcast_to(jnp.arange(E, dtype=jnp.int32)[None, :], (N, E))
        rank_c = jnp.where(keep, rank, cap)
        buf = jnp.full((E, cap), N, dtype=jnp.int32)
        buf = buf.at[eid, rank_c].set(tok, mode='drop')
        xpad = jnp.concatenate([xf, jnp.zeros((1, C), xf.dtype)], axis=0)
        xg = xpad[buf]
        h = jax.nn.gelu(jnp.einsum('ecd,edh->ech', xg, W1) + b1[:, None, :], approximate=False)
        out = jnp.einsum('ech,ehd->ecd', h, W2) + b2[:, None, :]
        rw_pad = jnp.concatenate([rw, jnp.zeros((1, E), rw.dtype)], axis=0)
        w = rw_pad[buf, jnp.arange(E, dtype=jnp.int32)[:, None]]
        weighted = out * w[..., None]
        final = jnp.zeros((N + 1, C), xf.dtype).at[buf.reshape(-1)].add(weighted.reshape(-1, C))
        return final[:N].reshape(B, T, C)
    x = x + _L0_gnn_ref(_layernorm(x, axis=-1), adj, L0_gnn_W_seq, L0_gnn_a1, L0_gnn_a2, L0_gnn_W_out, L0_gnn_b_out)
    x = x + _L0_ffn_ref(_layernorm(x, axis=-1)[None], L0_ffn_gate_w, L0_ffn_w_gate, L0_ffn_w_up, L0_ffn_w_down)[0]
    x = x + _L1_gnn_ref(_layernorm(x, axis=-1), adj, adj)
    x = x + _L1_ffn_ref(_layernorm(x, axis=-1)[None], L1_ffn_Wr, L1_ffn_br, L1_ffn_W1, L1_ffn_b1, L1_ffn_W2, L1_ffn_b2)[0]
    return x

_drawn_inputs = setup_inputs


def setup_inputs(seed=0):
    import zlib

    import numpy as np

    out = dict(_drawn_inputs(seed))
    spreads = {'L1_ffn_br': (0.0, 0.1), 'L1_ffn_b1': (0.0, 0.632), 'L1_ffn_b2': (0.0, 0.345)}
    factors = {'L0_ffn_gate_w': 2.726}
    for name, (base, spread) in spreads.items():
        noise = np.random.default_rng([zlib.crc32(name.encode()), seed]).standard_normal(out[name].shape)
        drawn = base * np.exp(spread * noise) if base else spread * noise
        out[name] = jnp.asarray(drawn.astype(out[name].dtype))
    for name, factor in factors.items():
        out[name] = (out[name] * factor).astype(out[name].dtype)
    return out
```

```python
from contextlib import ExitStack

import concourse.bass as bass
from concourse import mybir

F32 = mybir.dt.float32
F32R = mybir.dt.float32r
BF16 = mybir.dt.bfloat16
U32 = mybir.dt.uint32
I32 = mybir.dt.int32
ALU = mybir.AluOpType
ACT = mybir.ActivationFunctionType
AX = mybir.AxisListType
RMAX = bass.bass_isa.ReduceOp.max

P = 128
N = 2048
D = 512
NT = N // P
KD = D // P
H = 16
DH = D // H
E = 8
TOPK = 2
I0 = 384
KI = I0 // P
BR = 256
NB0 = N * TOPK // BR + E - 1
HID = 2048
CAP = N * TOPK // E
CT = CAP // P
EPS = 1e-5
SLOPE = 0.2
BIG = 1e30
FAR = 1.0e6


START = 3


def rounds(eng, total, period, step, tail=2):
    full = (total - tail) // period
    with eng.Fori(0, full) as i:
        for v in range(period):
            step(period * i + v, v, lambda n: i * (period // n), total)
    for b in range(full * period, total):
        v = b % period
        step(b, v, lambda n, base=b - v: base // n, total - b)


class Chain:

    def __init__(self, eng, sem, passed=None):
        self.eng, self.sem, self.n, self.off, self.passed = eng, sem, 0, 0, passed

    def link(self, ins):
        self.n += 1
        ins.then_inc(self.sem, 1)
        self.eng.wait_ge(self.sem, self.off + self.n)
        if self.passed is not None:
            self.eng.sem_inc(self.passed, 1)

    def loop(self, i, per_round):
        self.off = i * per_round


SPENT = []


def recycle(nc):
    nc.clear_and_free_semaphores(list(SPENT))
    SPENT.clear()
    nc.all_engine_barrier()


class Ctx:

    def __init__(self, nc, stack, tag):
        self.nc, self.stack, self.tag = nc, stack, tag

    def sb(self, name, shape, dt=F32):
        return self.stack.enter_context(self.nc.sbuf_tensor(f"{self.tag}_{name}", shape, dt))

    def ps(self, name, shape, dt=F32):
        return self.stack.enter_context(self.nc.psum_tensor(f"{self.tag}_{name}", shape, dt))

    def sem(self, name):
        s = self.nc.alloc_semaphore(f"{self.tag}_{name}")
        SPENT.append(s)
        return s


def constants(nc, k):
    with ExitStack() as st:
        c = Ctx(nc, st, "const")
        filled, shaped = c.sem("filled"), c.sem("shaped")
        with nc.Block() as block:
            @block.gpsimd
            def _(pool):
                pool.memset(k.ident[:], 0.0).then_inc(filled, 1)
                pool.memset(k.before[:], 1.0).then_inc(filled, 1)
                pool.memset(k.ones[:], 1.0).then_inc(filled, 1)
                pool.memset(k.zeros[:], 0.0).then_inc(filled, 1)
                pool.memset(k.zerob[:], 0.0).then_inc(filled, 1)
                pool.wait_ge(filled, 5)
                pool.affine_select(out=k.ident[:], in_=k.ident[:], compare_op=ALU.not_equal, fill=1.0,
                                   base=0, pattern=[[-1, P]], channel_multiplier=1).then_inc(shaped, 1)
                pool.affine_select(out=k.before[:], in_=k.before[:], compare_op=ALU.is_gt, fill=0.0,
                                   base=0, pattern=[[1, P]], channel_multiplier=-1).then_inc(shaped, 1)
                pool.iota(k.expert_id[:], pattern=[[1, E]], base=0, channel_multiplier=0,
                          allow_small_or_imprecise_dtypes=True).then_inc(shaped, 1)
                pool.iota(k.block_start[:], pattern=[[BR, N // BR]], base=0, channel_multiplier=0,
                          allow_small_or_imprecise_dtypes=True).then_inc(shaped, 1)
                pool.iota(k.block_id[:], pattern=[[1, NB0]], base=0, channel_multiplier=0,
                          allow_small_or_imprecise_dtypes=True).then_inc(shaped, 1)
                pool.wait_ge(shaped, 5)
                pool.tensor_copy(k.identb[:], k.ident[:]).then_inc(shaped, 1)


def norm_stats(nc, tag, x_sb, mean, rstd):
    with ExitStack() as st:
        c = Ctx(nc, st, tag)
        bn = c.sb("bn", [P, NT, 6])
        mv = c.sb("mv", [P, NT, 2])
        var = c.sb("var", [P, NT])
        root = c.sb("root", [P, NT])
        r0 = c.sb("r0", [P, NT])
        t = c.sb("t", [P, NT])
        ch_s, var_ready, root_ready = c.sem("chain"), c.sem("var_ready"), c.sem("root_ready")
        with nc.Block() as block:
            @block.vector
            def _(dve):
                with dve.Fori(0, NT // 2) as i:
                    for u in range(2):
                        dve.bn_stats(bn[:, 2 * i + u, :], x_sb[:, 2 * i + u, :]).then_inc(ch_s, 1)
                dve.wait_ge(ch_s, NT)
                for n in range(NT):
                    dve.bn_aggr(mv[:, n, :], bn[:, n, :]).then_inc(ch_s, 1)
                ch = Chain(dve, ch_s)
                ch.n = 2 * NT
                dve.wait_ge(ch_s, 2 * NT)
                ch.link(dve.tensor_copy(mean[:], mv[:, :, 0]))
                dve.tensor_scalar(var[:], mv[:, :, 1], EPS, None, ALU.add).then_inc(var_ready, 1)
                dve.wait_ge(root_ready, 1)
                ch.link(dve.reciprocal(r0[:], root[:]))
                ch.link(dve.tensor_tensor(t[:], r0[:], r0[:], ALU.mult))
                ch.link(dve.tensor_tensor(t[:], t[:], var[:], ALU.mult))
                ch.link(dve.tensor_scalar(t[:], t[:], -0.5, 1.5, ALU.mult, ALU.add))
                dve.tensor_tensor(rstd[:], r0[:], t[:], ALU.mult).then_inc(ch_s, 1)

            @block.scalar
            def _(act):
                act.wait_ge(var_ready, 1)
                act.activation(root[:], var[:], ACT.Sqrt).then_inc(root_ready, 1)


def project_heads(nc, k, x_sb, mean, rstd, W_seq, a1, a2, seq, s1, s2, adjT, adjT_dram, isolated, iso_row):
    with ExitStack() as st:
        c = Ctx(nc, st, "proj")
        WC = D + 2 * H
        w = c.sb("w", [P, KD, WC])
        w_hi = c.sb("w_hi", [P, KD, WC], F32R)
        w_lo = c.sb("w_lo", [P, KD, WC], F32R)
        a_rows = c.sb("a_rows", [P, 2, DH])
        prod = c.sb("prod", [P, D])
        xn = c.sb("xn", [P, 2, D])
        iso = c.sb("iso", [P, N])
        isob = c.sb("isob", [P, N], BF16)
        isoT = c.sb("isoT", [NT, P])
        hi = [c.sb(f"hi{u}", [P, KD, P], F32R) for u in range(2)]
        lo = [c.sb(f"lo{u}", [P, KD, P], F32R) for u in range(2)]
        xT = [c.ps(f"xT{u}", [P, KD, P]) for u in range(2)]
        out = [c.ps(f"out{u}", [P, D]) for u in range(2)]
        sc = [c.ps(f"sc{u}", [P, 2 * H]) for u in range(2)]
        isoT_ps = c.ps("isoT_ps", [NT, P])
        loaded, w_full, w_split, w_high = c.sem("loaded"), c.sem("w_full"), c.sem("w_split"), c.sem("w_high")
        normed, turned, high, low = c.sem("normed"), c.sem("turned"), c.sem("high"), c.sem("low")
        summed, copied, scored, ch_s = c.sem("summed"), c.sem("copied"), c.sem("scored"), c.sem("chain")
        iso_turned, iso_kept, iso_wrote, iso_in, spilled, iso_cast, filled = (
            c.sem(x) for x in ("iso_turned", "iso_kept", "iso_wrote", "iso_in", "spilled", "iso_cast", "filled"))
        with nc.Block() as block:
            @block.sync
            def _(sp):
                sp.dma_start(w[:, :, 0:D], W_seq.rearrange("(k p) n -> p k n", p=P)).then_inc(loaded, 16)
                sp.dma_start(a_rows[:, 0, :], a1.rearrange("(a d) -> a d", a=1).to_broadcast([P, DH])).then_inc(loaded, 16)
                sp.dma_start(a_rows[:, 1, :], a2.rearrange("(a d) -> a d", a=1).to_broadcast([P, DH])).then_inc(loaded, 16)
                sp.wait_ge(iso_kept, 1)
                sp.dma_start(iso_row.rearrange("a (t p) -> (a t) p", p=P), isoT[:]).then_inc(iso_wrote, 16)
                sp.wait_ge(iso_wrote, 16)
                sp.dma_start(iso[:], iso_row.to_broadcast([P, N])).then_inc(iso_in, 16)
                for q in range(4):
                    sp.dma_start(adjT_dram[512 * q:512 * q + 512, :].rearrange("(t p) n -> p t n", p=P),
                                 adjT[:, 4 * q:4 * q + 4, :]).then_inc(spilled, 16)
                sp.wait_ge(spilled, 64)

            @block.gpsimd
            def _(pool):
                pool.wait_ge(iso_in, 16)
                pool.tensor_copy(isob[:], iso[:]).then_inc(iso_cast, 1)
                pool.wait_ge(iso_cast, 1)
                pool.wait_ge(spilled, 64)
                with pool.Fori(0, NT) as t:
                    pool.tensor_tensor(adjT[:, t, :], adjT[:, t, :], isob[:], ALU.add).then_inc(filled, 1)

            @block.scalar
            def _(act):
                act.sem_inc(copied, START)
                act.wait_ge(w_full, 1)
                act.copy(w_hi[:], w[:]).then_inc(w_high, 1)

                def high_part(t, u):
                    act.wait_ge(summed, START + t - 1)
                    act.wait_ge(turned, START + t + 1)
                    act.copy(hi[u][:], xT[u][:]).then_inc(high, 1)

                def step(t, u, at, left):
                    if left > 1:
                        high_part(t + 1, (u + 1) % 2)
                    act.wait_ge(summed, START + t + 1)
                    act.copy(seq[:, t, :], out[u][:]).then_inc(copied, 1)
                act.wait_ge(turned, START + 1)
                act.copy(hi[0][:], xT[0][:]).then_inc(high, 1)
                rounds(act, NT, 2, step)

            @block.vector
            def _(dve):
                dve.sem_inc(scored, START)
                dve.wait_ge(iso_turned, 1)
                dve.tensor_copy(isoT[:], isoT_ps[:]).then_inc(iso_kept, 1)
                dve.wait_ge(loaded, 48)
                ch = Chain(dve, ch_s)
                for m in range(2):
                    for j in range(KD):
                        ch.link(dve.tensor_tensor(prod[:].rearrange("p (h d) -> p h d", d=DH),
                                                  w[:, j, 0:D].rearrange("p (h d) -> p h d", d=DH),
                                                  a_rows[:, m:m + 1, :].to_broadcast([P, H, DH]), ALU.mult))
                        ch.link(dve.tensor_reduce(w[:, j, D + m * H:D + (m + 1) * H], prod[:].rearrange("p (h d) -> p h d", d=DH),
                                                  AX.X, ALU.add))
                dve.sem_inc(w_full, 1)
                dve.wait_ge(w_high, 1)
                dve.tensor_tensor(w_lo[:], w[:], w_hi[:], ALU.subtract).then_inc(w_split, 1)

                def norm(t, u):
                    dve.tensor_scalar(xn[:, u, :], x_sb[:, t, :], mean[:, bass.ds(t, 1)], rstd[:, bass.ds(t, 1)],
                                      ALU.subtract, ALU.mult).then_inc(normed, 1)

                def low_part(t, u):
                    dve.wait_ge(high, t + 1)
                    dve.tensor_tensor(lo[u][:], xT[u][:], hi[u][:], ALU.subtract).then_inc(low, 1)

                def step(t, u, at, left):
                    if left > 2:
                        dve.wait_ge(turned, START + t + 1)
                        norm(t + 2, u)
                    if left > 1:
                        low_part(t + 1, (u + 1) % 2)
                    dve.wait_ge(summed, START + t + 1)
                    dve.tensor_copy(s1[:, t, :], sc[u][:, 0:H]).then_inc(scored, 1)
                    dve.tensor_copy(s2[:, t, :], sc[u][:, H:2 * H]).then_inc(scored, 1)
                norm(0, 0)
                norm(1, 1)
                low_part(0, 0)
                rounds(dve, NT, 2, step)

            @block.tensor
            def _(pe):
                pe.sem_inc(turned, START)
                pe.sem_inc(summed, START)
                pe.transpose(isoT_ps[:], isolated[:], k.ident[:]).then_inc(iso_turned, 1)

                def turn(t, u):
                    pe.wait_ge(normed, t + 1)
                    for j in range(KD):
                        mm = pe.transpose(xT[u][:, j, :], xn[:, u, j * P:(j + 1) * P], k.ident[:])
                    mm.then_inc(turned, 1)

                def step(t, u, at, left):
                    if left > 1:
                        turn(t + 1, (u + 1) % 2)
                    pe.wait_ge(low, t + 1)
                    pe.wait_ge(copied, START + t - 1)
                    pe.wait_ge(scored, START + 2 * t - 2)
                    terms = [(hi[u][:, j, :], lo[u][:, j, :], w_hi[:, j, :], w_lo[:, j, :]) for j in range(KD)]
                    three_pass(pe, out[u][:], [(a, b, x[:, 0:D], y[:, 0:D]) for a, b, x, y in terms])
                    three_pass(pe, sc[u][:], [(a, b, x[:, D:WC], y[:, D:WC]) for a, b, x, y in terms]).then_inc(summed, 1)
                turn(0, 0)
                pe.wait_ge(w_split, 1)
                rounds(pe, NT, 2, step)


def three_pass(pe, out, terms):
    n = len(terms)
    for j, (ah, al, bh, bl) in enumerate(terms):
        pe.matmul(out, ah, bh, start=(j == 0), stop=False)
        pe.matmul(out, ah, bl, start=False, stop=False)
        mm = pe.matmul(out, al, bh, start=False, stop=(j == n - 1))
    return mm


def transpose_adj(nc, k, adj, adjT, isolated, rowsum, colsum, x, x_sb):
    with ExitStack() as st:
        c = Ctx(nc, st, "adj")
        a = c.sb("a", [P, 2, N])
        ab = c.sb("ab", [P, 2, N], BF16)
        turned_ps = [c.ps(f"turned{u}", [P, NT, P], BF16) for u in range(2)]
        col_ps = c.ps("col_ps", [P, NT])
        loaded = [c.sem(f"loaded{u}") for u in range(2)]
        x_in, cast, turned, kept, ended = (c.sem(x) for x in ("x_in", "cast", "turned", "kept", "ended"))
        passed = c.sem("passed")
        with nc.Block() as block:
            @block.sync
            def _(sp):
                for u in range(2):
                    sp.dma_start(a[:, u, :], adj[u * P:(u + 1) * P, :]).then_inc(loaded[u], 16)
                with sp.Fori(1, NT // 2) as i:
                    for u in range(2):
                        sp.wait_ge(cast, 2 * i + u - 1)
                        sp.sem_inc(passed, 1)
                        sp.dma_start(a[:, u, :], adj[bass.ds((2 * i + u) * P, P), :]).then_inc(loaded[u], 16)
                for q in range(4):
                    sp.dma_start(x_sb[:, 4 * q:4 * q + 4, :],
                                 x[512 * q:512 * q + 512, :].rearrange("(t p) d -> p t d", p=P)).then_inc(x_in, 16)
                sp.wait_ge(x_in, 64)

            @block.scalar
            def _(act):
                def cast_rows(t, u, fills):
                    act.wait_ge(loaded[u], 16 * fills)
                    act.wait_ge(turned, START + t - 1)
                    act.activation(ab[:, u, :], a[:, u, :], ACT.Copy, accum_out=rowsum[:, bass.ds(t, 1)]).then_inc(cast, 1)

                def step(t, u, at, left):
                    if left > 1:
                        cast_rows(t + 1, (u + 1) % 2, at(2) + (u + 1) // 2 + 1)
                act.wait_ge(loaded[0], 16)
                act.activation(ab[:, 0, :], a[:, 0, :], ACT.Copy, accum_out=rowsum[:, 0:1]).then_inc(cast, 1)
                rounds(act, NT, 2, step)

            @block.vector
            def _(dve):
                dve.sem_inc(kept, START)

                def step(t, u, at, left):
                    dve.wait_ge(turned, START + t + 1)
                    dve.tensor_copy(adjT[:, :, bass.ds(t * P, P)], turned_ps[u][:]).then_inc(kept, 1)
                rounds(dve, NT, 2, step)
                dve.wait_ge(cast, NT)
                dve.tensor_scalar(isolated[:], rowsum[:], 0.0, None, ALU.is_equal).then_inc(ended, 1)
                dve.wait_ge(turned, START + NT)
                dve.tensor_copy(colsum[:], col_ps[:]).then_inc(ended, 1)

            @block.tensor
            def _(pe):
                pe.sem_inc(turned, START)

                def step(t, u, at, left):
                    pe.wait_ge(cast, t + 1)
                    pe.wait_ge(kept, START + t - 1)
                    for j in range(NT):
                        pe.transpose(turned_ps[u][:, j, :], ab[:, u, j * P:(j + 1) * P], k.identb[:])
                    for j in range(NT):
                        mm = pe.matmul(col_ps[:, j:j + 1], ab[:, u, j * P:(j + 1) * P], k.ones[:, 0:1], start=False,
                                       stop=False, skip_group_check=True)
                    mm.then_inc(turned, 1)
                pe.matmul(col_ps[:], k.zerob[:], k.zerob[:, 0:NT], start=True, stop=False, skip_group_check=True)
                rounds(pe, NT, 2, step)


def softmax_factors(nc, k, s1, s2, ea, eb, g, ns2, big_s2, s1_rows, rowsum, colsum, dinv):
    with ExitStack() as st:
        c = Ctx(nc, st, "factor")
        top = c.sb("top", [P, H])
        m = c.sb("m", [P, H])
        dif = c.sb("dif", [P, NT, H])
        pos = c.sb("pos", [P, NT, H])
        s1T = c.sb("s1T", [H, N])
        deg, some, root, t = (c.sb(n, [P, NT]) for n in ("deg", "some", "root", "t"))
        s1T_ps = c.ps("s1T_ps", [H, NT, P])
        topped, maxed, difs, turned, kept, wrote = (c.sem(x) for x in ("topped", "maxed", "difs", "turned", "kept", "wrote"))
        ch_s, exps, deg_ready, rooted = c.sem("chain"), c.sem("exps"), c.sem("deg_ready"), c.sem("rooted")
        with nc.Block() as block:
            @block.vector
            def _(dve):
                dve.tensor_reduce(top[:], s2[:].rearrange("p t h -> p h t"), AX.X, ALU.max).then_inc(topped, 1)
                dve.tensor_scalar(ns2[:], s2[:], -1.0, None, ALU.mult).then_inc(ch_s, 1)
                dve.tensor_scalar(big_s2[:], s2[:], BIG, None, ALU.mult).then_inc(ch_s, 1)
                dve.wait_ge(maxed, 1)
                mrow = m[:].rearrange("p (a h) -> p a h", a=1).to_broadcast([P, NT, H])
                dve.tensor_tensor(dif[:], s2[:], mrow, ALU.subtract).then_inc(difs, 1)
                ch = Chain(dve, ch_s)
                ch.n = 2
                dve.wait_ge(ch_s, 2)
                ch.link(dve.tensor_tensor(pos[:], s1[:], mrow, ALU.add))
                dve.tensor_scalar(pos[:], pos[:], 0.0, None, ALU.max).then_inc(difs, 1)
                dve.wait_ge(turned, 1)
                dve.tensor_copy(s1T[:], s1T_ps[:].rearrange("h t p -> h (t p)")).then_inc(kept, 1)
                ch.link(dve.tensor_tensor(deg[:], rowsum[:], colsum[:], ALU.add))
                ch.link(dve.tensor_scalar(deg[:], deg[:], 0.5, 1.0, ALU.mult, ALU.add))
                ch.link(dve.tensor_scalar(some[:], deg[:], 0.0, None, ALU.is_gt))
                dve.tensor_scalar(deg[:], deg[:], 1e-30, None, ALU.max).then_inc(deg_ready, 1)
                dve.wait_ge(rooted, 1)
                ch.link(dve.reciprocal(dinv[:], root[:]))
                ch.link(dve.tensor_tensor(t[:], dinv[:], dinv[:], ALU.mult))
                ch.link(dve.tensor_tensor(t[:], t[:], deg[:], ALU.mult))
                ch.link(dve.tensor_scalar(t[:], t[:], -0.5, 1.5, ALU.mult, ALU.add))
                ch.link(dve.tensor_tensor(dinv[:], dinv[:], t[:], ALU.mult))
                dve.tensor_tensor(dinv[:], dinv[:], some[:], ALU.mult).then_inc(ch_s, 1)

            @block.gpsimd
            def _(pool):
                pool.wait_ge(topped, 1)
                pool.partition_all_reduce(m[:], top[:], P, RMAX).then_inc(maxed, 1)

            @block.scalar
            def _(act):
                act.wait_ge(difs, 1)
                act.activation(ea[:], dif[:], ACT.Exp).then_inc(exps, 1)
                act.activation(eb[:], dif[:], ACT.Exp, scale=SLOPE).then_inc(exps, 1)
                act.wait_ge(difs, 2)
                act.activation(g[:], pos[:], ACT.Exp, scale=-(1.0 - SLOPE)).then_inc(exps, 1)
                act.wait_ge(deg_ready, 1)
                act.activation(root[:], deg[:], ACT.Sqrt).then_inc(rooted, 1)

            @block.tensor
            def _(pe):
                for n in range(NT):
                    mm = pe.transpose(s1T_ps[:, n, :], s1[:, n, :], k.ident[:])
                mm.then_inc(turned, 1)

            @block.sync
            def _(sp):
                sp.wait_ge(kept, 1)
                sp.dma_start(s1_rows, s1T[:]).then_inc(wrote, 16)
                sp.wait_ge(wrote, 16)


def attention(nc, k, adjT, seq, ea, eb, g, ns2, big_s2, s1_rows, tables):
    HB = NT // 2
    HW = N // 2
    C1 = DH + 1
    UNITS = 2 * H
    STEPPED = [j for j in range(NT) if j % 4]
    RD = 4
    with ExitStack() as st:
        c = Ctx(nc, st, "attn")
        s1_row = c.sb("s1_row", [P, 2, N])
        mask = c.sb("mask", [P, NT, HW], BF16)
        step = c.sb("step", [P, RD, HW], BF16)
        vals = c.sb("vals", [P, NT, 2 * C1])
        rest = c.sb("rest", [P, NT, 2 * C1])
        m_parts = c.sb("m_parts", [P, 2, NT, 3, 2 * C1], BF16)
        a_parts = c.sb("a_parts", [P, 2, NT, 3, C1], BF16)
        sums = c.sb("sums", [P, HB, 2 * C1])
        num = c.sb("num", [P, HB, C1])
        inv = c.sb("inv", [P, HB, 1])
        acc = [c.ps(f"acc{u}", [P, HB, 256]) for u in range(2)]
        rows_in = [c.sem(f"rows_in{u}") for u in range(2)]
        stepped, masked = c.sem("stepped"), c.sem("masked")
        mask_used, acc_free = c.sem("mask_used"), c.sem("acc_free")
        parts_ready, ch_p, ch_v = c.sem("parts_ready"), c.sem("pool_chain"), c.sem("dve_chain")
        cleared = c.sem("cleared")
        passed_a, passed_p, passed_s = c.sem("passed_act"), c.sem("passed_pool"), c.sem("passed_sp")
        with nc.Block() as block:
            @block.sync
            def _(sp):
                for u in range(2):
                    sp.dma_start(s1_row[:, u, :], s1_rows[u:u + 1, :].to_broadcast([P, N])).then_inc(rows_in[u], 16)
                for table in tables:
                    sp.dma_start(table.rearrange("(b p) d -> p b d", p=P),
                                 k.zeros[:].rearrange("p (a d) -> p a d", a=1).to_broadcast([P, table.shape[0] // P, D])
                                 ).then_inc(cleared, 16)
                with sp.Fori(1, H // 2) as i:
                    for u in range(2):
                        sp.wait_ge(masked, NT + (2 * i + u - 1) * 2 * NT)
                        sp.sem_inc(passed_s, 1)
                        sp.wait_ge(stepped, (2 * i + u - 1) * 2 * len(STEPPED))
                        sp.sem_inc(passed_s, 1)
                        sp.dma_start(s1_row[:, u, :], s1_rows[bass.ds(2 * i + u, 1), :].to_broadcast([P, N])).then_inc(rows_in[u], 16)
                sp.wait_ge(cleared, 16 * len(tables))

            @block.scalar
            def _(act):
                with act.Fori(0, H // 2) as i:
                    for v in range(4):
                        u, half, n, h = v // 2, v % 2, 4 * i + v, 2 * i + v // 2
                        act.wait_ge(rows_in[u], 16 * (i + 1))
                        for j in range(NT):
                            if j not in STEPPED:
                                continue
                            src = s1_row[:, u, half * HW:(half + 1) * HW]
                            q = STEPPED.index(j)
                            before = STEPPED[q - RD] + (0 if q >= RD else -NT)
                            act.wait_ge(masked, NT + n * NT + before + 1)
                            act.sem_inc(passed_a, 1)
                            act.activation(step[:, q % RD, :], src, ACT.Sigmoid, bias=big_s2[:, j, bass.ds(h, 1)],
                                           scale=BIG).then_inc(stepped, 1)

            @block.gpsimd
            def _(pool):
                ch = Chain(pool, ch_p, passed_p)
                PREP = 7

                def prepare(h, b):
                    v = vals[:].rearrange("p t (w c) -> p t w c", w=2)
                    for w, e in ((0, ea), (1, eb)):
                        f = e[:, :, bass.ds(h, 1)]
                        pool.tensor_tensor(v[:, :, w, 0:DH], seq[:, :, bass.ds(h * DH, DH)],
                                           f.to_broadcast([P, NT, DH]), ALU.mult).then_inc(ch_p, 1)
                        pool.tensor_copy(v[:, :, w, DH:C1], f).then_inc(ch_p, 1)
                    ch.n += 4
                    pool.wait_ge(ch_p, ch.off + ch.n)
                    pool.sem_inc(passed_p, 1)
                    mp = m_parts[:, b]
                    ch.link(pool.tensor_copy(mp[:, :, 0, :], vals[:]))
                    ch.link(pool.tensor_tensor(rest[:], vals[:], mp[:, :, 0, :], ALU.subtract))
                    ch.link(pool.tensor_copy(mp[:, :, 1, :], rest[:]))
                    ch.link(pool.tensor_tensor(mp[:, :, 2, :], rest[:], mp[:, :, 1, :], ALU.subtract))
                    ch.link(pool.tensor_copy(a_parts[:, b], mp[:, :, :, C1:2 * C1]))
                    ch.link(pool.tensor_scalar(mp[:, :, :, C1:2 * C1], a_parts[:, b], -1.0, None, ALU.mult))
                    ch.n += 0
                    pool.sem_inc(parts_ready, 1)

                prepare(0, 0)
                one = ch.n

                def head(h, u):
                    pool.wait_ge(mask_used, NT + 2 * NT * h)
                    pool.sem_inc(passed_p, 1)
                    prepare(h + 1, 1 - u)

                with pool.Fori(0, H // 2 - 1) as i:
                    ch.loop(i, 2 * one)
                    head(2 * i, 0)
                    head(2 * i + 1, 1)
                ch.off = (H // 2 - 2) * 2 * one
                head(H - 2, 0)

            @block.vector
            def _(dve):
                ch = Chain(dve, ch_v)

                def masks(i, v, js):
                    u, half, n, h = (v % 4) // 2, v % 2, 4 * i + v, 2 * i + v // 2
                    if js[0] == 0:
                        dve.wait_ge(rows_in[u], 16 * (i + 1 + v // 4))
                    for j in js:
                        dve.wait_ge(mask_used, n * NT + j + 1)
                        at = adjT[:, j, half * HW:(half + 1) * HW]
                        if j not in STEPPED:
                            dve.scalar_tensor_tensor(out=mask[:, j, :], in0=s1_row[:, u, half * HW:(half + 1) * HW],
                                                     scalar=ns2[:, j, bass.ds(h, 1)], in1=at, op0=ALU.is_gt,
                                                     op1=ALU.mult).then_inc(masked, 1)
                        else:
                            q = STEPPED.index(j)
                            dve.wait_ge(stepped, n * len(STEPPED) + q + 1)
                            dve.tensor_tensor(mask[:, j, :], step[:, q % RD, :], at, ALU.mult).then_inc(masked, 1)

                def combine(i, v):
                    half, n, h = v % 2, 4 * i + v, 2 * i + v // 2
                    dve.wait_ge(mask_used, NT + (n + 1) * NT)
                    dve.tensor_reduce(sums[:], acc[v % 2][:, :, 0:6 * C1].rearrange("p b (s c) -> p b c s", s=3),
                                      AX.X, ALU.add).then_inc(acc_free, 1)
                    dve.wait_ge(acc_free, n + 3)
                    gh = g[:, half * HB:(half + 1) * HB, bass.ds(h, 1)]
                    ch.link(dve.tensor_tensor(num[:], sums[:, :, C1:2 * C1], gh.to_broadcast([P, HB, C1]), ALU.mult))
                    ch.link(dve.tensor_tensor(num[:], num[:], sums[:, :, 0:C1], ALU.add))
                    ch.link(dve.reciprocal(inv[:], num[:, :, DH:C1]))
                    ch.link(dve.tensor_tensor(seq[:, half * HB:(half + 1) * HB, bass.ds(h * DH, DH)], num[:, :, 0:DH],
                                              inv[:].to_broadcast([P, HB, DH]), ALU.mult))

                EARLY = 12
                masks(0, 0, range(0, EARLY))

                def round_(i, last):
                    for v in range(4):
                        masks(i, v, range(EARLY, NT))
                        if not (last and v == 3):
                            masks(i, v + 1, range(0, EARLY))
                        combine(i, v)

                with dve.Fori(0, H // 2 - 1) as i:
                    ch.loop(i, 16)
                    round_(i, False)
                ch.off = (H // 2 - 2) * 16
                round_(H // 2 - 1, True)

            @block.tensor
            def _(pe):
                pe.sem_inc(masked, NT)
                pe.sem_inc(mask_used, NT)
                pe.sem_inc(acc_free, 2)
                with pe.Fori(0, H // 2) as i:
                    for v in range(4):
                        u, half, n, h = v // 2, v % 2, 4 * i + v, 2 * i + v // 2
                        pe.wait_ge(acc_free, n + 1)
                        pe.wait_ge(parts_ready, h + 1)
                        for j in range(NT):
                            pe.wait_ge(masked, NT + n * NT + j + 1)
                            for b in range(HB):
                                o = acc[v % 2][:, b, 0:6 * C1]
                                pe.matmul(o, mask[:, j, b * P:(b + 1) * P], m_parts[:, u, j].rearrange("p s c -> p (s c)"),
                                          start=(j == 0 and b % 2 == 0), stop=(j == NT - 1), skip_group_check=True)
                                mm = pe.matmul(o.rearrange("p (s c) -> p s c", s=3)[:, :, C1:2 * C1],
                                               adjT[:, j, half * HW + b * P:half * HW + (b + 1) * P], a_parts[:, u, j],
                                               start=False, stop=(j == NT - 1), skip_group_check=True)
                            mm.then_inc(mask_used, 1)


class Constants:
    pass


def make_constants(nc, c):
    k = Constants()
    k.ident = c.sb("ident", [P, P])
    k.identb = c.sb("identb", [P, P], BF16)
    k.before = c.sb("before", [P, P], BF16)
    k.ones = c.sb("ones", [P, P], BF16)
    k.zerob = c.sb("zerob", [P, P], BF16)
    k.zeros = c.sb("zeros", [P, D])
    k.expert_id = c.sb("expert_id", [P, E])
    k.block_start = c.sb("block_start", [P, N // BR])
    k.block_id = c.sb("block_id", [P, NB0])
    return k


def project_out(nc, k, hid, x_dram, W_out, b_out, x_sb):
    with ExitStack() as st:
        c = Ctx(nc, st, "outp")
        w = c.sb("w", [P, KD, D])
        w_hi = c.sb("w_hi", [P, KD, D], F32R)
        w_lo = c.sb("w_lo", [P, KD, D], F32R)
        bias = c.sb("bias", [P, D])
        hi = [c.sb(f"hi{u}", [P, KD, P], F32R) for u in range(2)]
        lo = [c.sb(f"lo{u}", [P, KD, P], F32R) for u in range(2)]
        tile = c.sb("tile", [P, 2, D])
        z = c.sb("z", [P, 2, D])
        neg = c.sb("neg", [P, 2, D])
        e = c.sb("e", [P, 2, D])
        xT = [c.ps(f"xT{u}", [P, KD, P]) for u in range(2)]
        out = [c.ps(f"out{u}", [P, D]) for u in range(2)]
        loaded, x_in, w_split, w_high = c.sem("loaded"), c.sem("x_in"), c.sem("w_split"), c.sem("w_high")
        passed = c.sem("passed")
        turned, high, low, summed = c.sem("turned"), c.sem("high"), c.sem("low"), c.sem("summed")
        staged, biased, negated, exped, added = c.sem("staged"), c.sem("biased"), c.sem("negated"), c.sem("exped"), c.sem("added")
        with nc.Block() as block:
            @block.sync
            def _(sp):
                sp.dma_start(w[:], W_out.rearrange("(k p) n -> p k n", p=P)).then_inc(loaded, 16)
                sp.dma_start(bias[:], b_out.rearrange("(a d) -> a d", a=1).to_broadcast([P, D])).then_inc(loaded, 16)
                for q in range(4):
                    sp.dma_start(x_sb[:, 4 * q:4 * q + 4, :],
                                 x_dram[512 * q:512 * q + 512, :].rearrange("(t p) d -> p t d", p=P)).then_inc(x_in, 16)

            @block.gpsimd
            def _(pool):
                def step(t, u, at, left):
                    pool.wait_ge(turned, START + t - 1)
                    pool.sem_inc(passed, 1)
                    pool.tensor_copy(tile[:, u, :], hid[:, t, :]).then_inc(staged, 1)
                for t in range(2):
                    pool.tensor_copy(tile[:, t, :], hid[:, t, :]).then_inc(staged, 1)
                with pool.Fori(1, NT // 2) as i:
                    for u in range(2):
                        step(2 * i + u, u, None, None)

            @block.scalar
            def _(act):
                act.wait_ge(loaded, 32)
                act.copy(w_hi[:], w[:]).then_inc(w_high, 1)

                def high_part(t, u):
                    act.wait_ge(turned, START + t + 1)
                    act.wait_ge(summed, START + t - 1)
                    act.copy(hi[u][:], xT[u][:]).then_inc(high, 1)

                def step(t, u, at, left):
                    if left > 1:
                        high_part(t + 1, (u + 1) % 2)
                    act.wait_ge(negated, t + 1)
                    act.activation(e[:, u, :], neg[:, u, :], ACT.Exp).then_inc(exped, 1)
                act.wait_ge(turned, START + 1)
                act.copy(hi[0][:], xT[0][:]).then_inc(high, 1)
                rounds(act, NT, 2, step)

            @block.vector
            def _(dve):
                dve.wait_ge(w_high, 1)
                dve.tensor_tensor(w_lo[:], w[:], w_hi[:], ALU.subtract).then_inc(w_split, 1)
                dve.wait_ge(x_in, 64)
                dve.sem_inc(biased, START)
                dve.sem_inc(added, START)

                def low_part(t, u):
                    dve.wait_ge(high, t + 1)
                    dve.tensor_tensor(lo[u][:], xT[u][:], hi[u][:], ALU.subtract).then_inc(low, 1)

                def bias_add(t, u):
                    dve.wait_ge(summed, START + t + 1)
                    dve.wait_ge(added, START + 2 * t - 2)
                    dve.tensor_tensor(z[:, u, :], out[u][:], bias[:], ALU.add).then_inc(biased, 1)
                    dve.wait_ge(biased, START + t + 1)
                    dve.tensor_scalar(neg[:, u, :], z[:, u, :], 0.0, None, ALU.min).then_inc(negated, 1)

                def step(t, u, at, left):
                    if left > 2:
                        low_part(t + 2, u)
                    if left > 1:
                        bias_add(t + 1, (u + 1) % 2)
                    x_t = x_sb[:, t, :]
                    dve.wait_ge(exped, t + 1)
                    dve.scalar_tensor_tensor(out=e[:, u, :], in0=e[:, u, :], scalar=-1.0, in1=x_t,
                                             op0=ALU.add, op1=ALU.add).then_inc(added, 1)
                    dve.wait_ge(added, START + 2 * t + 1)
                    dve.scalar_tensor_tensor(out=x_t, in0=z[:, u, :], scalar=0.0, in1=e[:, u, :],
                                             op0=ALU.max, op1=ALU.add).then_inc(added, 1)
                low_part(0, 0)
                low_part(1, 1)
                dve.wait_ge(summed, START + 1)
                dve.tensor_tensor(z[:, 0, :], out[0][:], bias[:], ALU.add).then_inc(biased, 1)
                dve.wait_ge(biased, START + 1)
                dve.tensor_scalar(neg[:, 0, :], z[:, 0, :], 0.0, None, ALU.min).then_inc(negated, 1)
                rounds(dve, NT, 2, step)

            @block.tensor
            def _(pe):
                pe.sem_inc(turned, START)
                pe.sem_inc(summed, START)

                def turn(t, u):
                    pe.wait_ge(staged, t + 1)
                    for j in range(KD):
                        mm = pe.transpose(xT[u][:, j, :], tile[:, u, j * P:(j + 1) * P], k.ident[:])
                    mm.then_inc(turned, 1)

                def step(t, u, at, left):
                    if left > 1:
                        turn(t + 1, (u + 1) % 2)
                    pe.wait_ge(low, t + 1)
                    pe.wait_ge(biased, START + t - 1)
                    three_pass(pe, out[u][:], [(hi[u][:, j, :], lo[u][:, j, :], w_hi[:, j, :], w_lo[:, j, :])
                                               for j in range(KD)]).then_inc(summed, 1)
                turn(0, 0)
                pe.wait_ge(w_split, 1)
                rounds(pe, NT, 2, step)


def route(nc, k, tag, x_sb, mean, rstd, W_r, b_r, xn, put_at, get_from, weight, block_expert):
    capped = block_expert is None
    with ExitStack() as st:
        c = Ctx(nc, st, tag)
        w = c.sb("w", [P, KD, E])
        bias = c.sb("bias", [P, E])
        xT = [c.sb(f"xT{u}", [P, KD, P]) for u in range(2)]
        tile = c.sb("tile", [P, 2, D])
        logits = c.sb("logits", [P, NT, E])
        best = c.sb("best", [P, NT, 8])
        best_id = c.sb("best_id", [P, NT, 8], U32)
        chosen = c.sb("chosen", [P, NT, TOPK])
        hot = [c.sb(f"hot{q}", [P, NT, E]) for q in range(TOPK)]
        sel = c.sb("sel", [P, NT, E], BF16)
        gap = c.sb("gap", [P, NT])
        tail = c.sb("tail", [P, NT])
        before_tile = c.sb("before_tile", [P, NT + 1, E])
        pos = c.sb("pos", [P, NT, E])
        keep = c.sb("keep", [P, NT, E])
        cmp = c.sb("cmp", [P, E, N // BR])
        blocks = c.sb("blocks", [P, E])
        ends = c.sb("ends", [P, E + 1])
        cmpb = c.sb("cmpb", [P, NB0, E])
        blk = c.sb("blk", [P, NB0])
        t = [c.sb(f"t{q}", [P, NT, E]) for q in range(TOPK)]
        slot = c.sb("slot", [P, TOPK, NT])
        kept = c.sb("kept", [P, TOPK, NT])
        far = c.sb("far", [P, TOPK, NT])
        xT_ps = [c.ps(f"xT_ps{u}", [P, KD, P]) for u in range(2)]
        lg_ps = c.ps("lg_ps", [P, NT, E])
        rank_ps = c.ps("rank_ps", [P, NT, E])
        total_ps = c.ps("total_ps", [P, NT, E])
        loaded, normed, turned, copied, scored = (c.sem(x) for x in ("loaded", "normed", "turned", "copied", "scored"))
        chosen_s, ranked, gapped, exped, ch_s = (c.sem(x) for x in ("chosen", "ranked", "gapped", "exped", "chain"))
        staged, passed = c.sem("staged"), c.sem("passed")
        with nc.Block() as block:
            @block.sync
            def _(sp):
                sp.dma_start(w[:], W_r.rearrange("(k p) e -> p k e", p=P)).then_inc(loaded, 16)
                if b_r is not None:
                    sp.dma_start(bias[:], b_r.rearrange("(a d) -> a d", a=1).to_broadcast([P, E])).then_inc(loaded, 16)

            @block.gpsimd
            def _(pool):
                with pool.Fori(0, NT // 2) as i:
                    for u in range(2):
                        pool.wait_ge(normed, 2 * i + u + 1)
                        pool.sem_inc(passed, 1)
                        pool.wait_ge(turned, START + 2 * i)
                        pool.sem_inc(passed, 1)
                        pool.tensor_copy(tile[:, u, :], xn[:, 2 * i + u, :]).then_inc(staged, 1)

            @block.scalar
            def _(act):
                with act.Fori(0, NT // 2) as i:
                    for u in range(2):
                        act.wait_ge(scored, START + 2 * i)
                        act.wait_ge(turned, START + 2 * i + u + 1)
                        act.copy(xT[u][:], xT_ps[u][:]).then_inc(copied, 1)
                act.wait_ge(gapped, 1)
                act.activation(tail[:], gap[:], ACT.Exp).then_inc(exped, 1)

            @block.tensor
            def _(pe):
                pe.sem_inc(turned, START)
                pe.sem_inc(scored, START)
                pe.sem_inc(copied, START)
                pe.wait_ge(loaded, 16 if b_r is None else 32)
                with pe.Fori(0, NT // 2) as i:
                    for u in range(2):
                        pe.wait_ge(staged, 2 * i + u + 1)
                        pe.wait_ge(copied, START + 2 * i)
                        for j in range(KD):
                            mm = pe.transpose(xT_ps[u][:, j, :], tile[:, u, j * P:(j + 1) * P], k.ident[:])
                        mm.then_inc(turned, 1)
                    for u in range(2):
                        pe.wait_ge(copied, START + 2 * i + u + 1)
                        for j in range(KD):
                            mm = pe.matmul(lg_ps[:, 2 * i + u, :], xT[u][:, j, :], w[:, j, :], start=(j == 0), stop=(j == KD - 1))
                        mm.then_inc(scored, 1)
                pe.wait_ge(chosen_s, 1)
                pe.matmul(rank_ps[:], k.before[:], sel[:], start=True, stop=True)
                pe.matmul(total_ps[:], k.ones[:], sel[:], start=True, stop=True).then_inc(ranked, 1)

            @block.vector
            def _(dve):
                with dve.Fori(0, NT // 2) as i:
                    for u in range(2):
                        dve.tensor_scalar(xn[:, 2 * i + u, :], x_sb[:, 2 * i + u, :], mean[:, bass.ds(2 * i + u, 1)],
                                          rstd[:, bass.ds(2 * i + u, 1)], ALU.subtract, ALU.mult).then_inc(normed, 1)
                ch = Chain(dve, ch_s)
                dve.wait_ge(scored, START + NT)
                if b_r is None:
                    ch.link(dve.tensor_copy(logits[:], lg_ps[:]))
                else:
                    ch.link(dve.tensor_tensor(logits[:], lg_ps[:], bias[:].rearrange("p (a e) -> p a e", a=1)
                                              .to_broadcast([P, NT, E]), ALU.add))
                for n in range(NT):
                    dve.max(best[:, n, :], logits[:, n, :]).then_inc(ch_s, 1)
                ch.n += NT
                dve.wait_ge(ch_s, ch.n)
                for n in range(NT):
                    dve.max_index(best_id[:, n, :], best[:, n, :], logits[:, n, :]).then_inc(ch_s, 1)
                ch.n += NT
                dve.wait_ge(ch_s, ch.n)
                ch.link(dve.tensor_copy(chosen[:], best_id[:, :, 0:TOPK]))
                ids = k.expert_id[:].rearrange("p (a e) -> p a e", a=1).to_broadcast([P, NT, E])
                for q in range(TOPK):
                    ch.link(dve.tensor_tensor(hot[q][:], ids, chosen[:, :, q:q + 1].to_broadcast([P, NT, E]), ALU.is_equal))
                dve.tensor_tensor(sel[:], hot[0][:], hot[1][:], ALU.add).then_inc(chosen_s, 1)
                dve.tensor_tensor(gap[:], best[:, :, 1], best[:, :, 0], ALU.subtract).then_inc(gapped, 1)
                dve.wait_ge(exped, 1)
                ch.link(dve.tensor_scalar(gap[:], tail[:], 1.0, None, ALU.add))
                ch.link(dve.reciprocal(weight[:, 0, :], gap[:]))
                ch.link(dve.tensor_tensor(weight[:, 1, :], weight[:, 0, :], tail[:], ALU.mult))
                dve.wait_ge(ranked, 1)
                ch.link(dve.memset(before_tile[:, 0, :], 0.0))
                for n in range(NT):
                    ch.link(dve.tensor_tensor(before_tile[:, n + 1, :], before_tile[:, n, :], total_ps[:, n, :], ALU.add))
                ch.link(dve.tensor_tensor(pos[:], rank_ps[:], before_tile[:, 0:NT, :], ALU.add))
                if capped:
                    ch.link(dve.tensor_scalar(keep[:], pos[:], float(CAP), None, ALU.is_lt))
                    ch.link(dve.tensor_scalar(ends[:, 0:E], k.expert_id[:], float(CAP), None, ALU.mult))
                else:
                    ch.link(dve.tensor_tensor(cmp[:], before_tile[:, NT:NT + 1, :].rearrange("p a e -> p e a").to_broadcast([P, E, N // BR]),
                                              k.block_start[:].rearrange("p (a t) -> p a t", a=1).to_broadcast([P, E, N // BR]), ALU.is_gt))
                    ch.link(dve.tensor_reduce(blocks[:], cmp[:], AX.X, ALU.add))
                    ch.link(dve.memset(ends[:, 0:1], 0.0))
                    for e in range(E):
                        ch.link(dve.tensor_tensor(ends[:, e + 1:e + 2], ends[:, e:e + 1], blocks[:, e:e + 1], ALU.add))
                    ch.link(dve.tensor_tensor(cmpb[:], ends[:, 1:E + 1].rearrange("p (a e) -> p a e", a=1).to_broadcast([P, NB0, E]),
                                              k.block_id[:].rearrange("p (b a) -> p b a", a=1).to_broadcast([P, NB0, E]), ALU.is_le))
                    ch.link(dve.tensor_reduce(blk[:], cmpb[:], AX.X, ALU.add))
                    ch.link(dve.tensor_scalar(block_expert[:], blk[:], float(E - 1), None, ALU.min))
                    ch.link(dve.tensor_scalar(ends[:], ends[:], float(BR), None, ALU.mult))
                ch.link(dve.tensor_tensor(pos[:], pos[:], ends[:, 0:E].rearrange("p (a e) -> p a e", a=1)
                                          .to_broadcast([P, NT, E]), ALU.add))
                for q in range(TOPK):
                    ch.link(dve.tensor_tensor(t[q][:], hot[q][:], pos[:], ALU.mult))
                    ch.link(dve.tensor_reduce(slot[:, q, :], t[q][:], AX.X, ALU.add))
                if capped:
                    for q in range(TOPK):
                        ch.link(dve.tensor_tensor(t[q][:], hot[q][:], keep[:], ALU.mult))
                        ch.link(dve.tensor_reduce(kept[:, q, :], t[q][:], AX.X, ALU.add))
                    ch.link(dve.tensor_tensor(weight[:], weight[:], kept[:], ALU.mult))
                    ch.link(dve.tensor_tensor(slot[:], slot[:], kept[:], ALU.mult))
                    ch.link(dve.tensor_copy(get_from[:], slot[:]))
                    ch.link(dve.tensor_scalar(far[:], kept[:], -FAR, FAR, ALU.mult, ALU.add))
                    ch.link(dve.tensor_tensor(far[:], far[:], slot[:], ALU.add))
                    ch.link(dve.tensor_copy(put_at[:], far[:]))
                else:
                    ch.link(dve.tensor_copy(get_from[:], slot[:]))
                    ch.link(dve.tensor_copy(put_at[:], slot[:]))


def dispatch(nc, tag, xn, put_at, table, rows, x_sb=None, spill=None):
    with ExitStack() as st:
        c = Ctx(nc, st, tag)
        put, stored = c.sem("put"), c.sem("stored")
        with nc.Block() as block:
            if spill is not None:
                @block.sync
                def _(sp):
                    for q in range(4):
                        sp.dma_start(spill[512 * q:512 * q + 512, :].rearrange("(t p) d -> p t d", p=P),
                                     x_sb[:, 4 * q:4 * q + 4, :]).then_inc(stored, 16)
                    sp.wait_ge(stored, 64)

            @block.gpsimd
            def _(pool):
                for n in range(NT):
                    for q in range(TOPK):
                        pool.indirect_dma_start(out=table, out_offset=bass.IndirectOffsetOnAxis(ap=put_at[:, q, n:n + 1], axis=0),
                                                in_=xn[:, n, :], in_offset=None, bounds_check=rows - 1,
                                                oob_is_err=False).then_inc(put, 16)
                pool.wait_ge(put, 16 * NT * TOPK)


def gather_experts(nc, tag, table, get_from, weight, x_sb, out, x_from=None):
    with ExitStack() as st:
        c = Ctx(nc, st, tag)
        R = 4
        y = c.sb("y", [P, R, D])
        got = [c.sem(f"got{r}") for r in range(R)]
        added, stored, x_in = c.sem("added"), c.sem("stored"), c.sem("x_in")
        with nc.Block() as block:
            @block.gpsimd
            def _(pool):
                for n in range(NT * TOPK):
                    if n >= R:
                        pool.wait_ge(added, n - R + 1)
                    pool.indirect_dma_start(out=y[:, n % R, :], out_offset=None, in_=table,
                                            in_offset=bass.IndirectOffsetOnAxis(ap=get_from[:, n % TOPK, n // TOPK:n // TOPK + 1], axis=0)
                                            ).then_inc(got[n % R], 16)

            @block.vector
            def _(dve):
                if x_from is not None:
                    dve.wait_ge(x_in, 64)
                for n in range(NT * TOPK):
                    tile, q = n // TOPK, n % TOPK
                    dve.wait_ge(got[n % R], 16 * (n // R + 1))
                    if n:
                        dve.wait_ge(added, n)
                    dve.scalar_tensor_tensor(out=x_sb[:, tile, :], in0=y[:, n % R, :], scalar=weight[:, q, tile:tile + 1],
                                             in1=x_sb[:, tile, :], op0=ALU.mult, op1=ALU.add).then_inc(added, 1)

            if out is not None:
                @block.sync
                def _(sp):
                    for q in range(4):
                        sp.dma_start(x_sb[:, 4 * q:4 * q + 4, :],
                                     x_from[512 * q:512 * q + 512, :].rearrange("(t p) d -> p t d", p=P)).then_inc(x_in, 16)
                    for q in range(4):
                        sp.wait_ge(added, 8 * q + 8)
                        sp.dma_start(out[512 * q:512 * q + 512, :].rearrange("(t p) d -> p t d", p=P),
                                     x_sb[:, 4 * q:4 * q + 4, :]).then_inc(stored, 16)
                    sp.wait_ge(stored, 64)


def experts_gated(nc, k, block_expert, table, w_gate, w_up, w_down, returned, spare):
    STEPS = NB0 * BR // P
    PERIOD = 4
    with ExitStack() as st:
        c = Ctx(nc, st, "moe0")
        x, y = spare[:, 0:4, :], spare[:, 4:6, :]
        wg, wu = ([c.sb(f"{n}{r}", [P, KD, I0]) for r in range(2)] for n in ("wg", "wu"))
        wd = [c.sb(f"wd{r}", [P, KI, D]) for r in range(2)]
        wg_hi, wg_lo, wu_hi, wu_lo = ([c.sb(f"{n}{r}", [P, KD, I0], F32R) for r in range(2)]
                                      for n in ("wg_hi", "wg_lo", "wu_hi", "wu_lo"))
        wd_hi, wd_lo = ([c.sb(f"{n}{r}", [P, KI, D], F32R) for r in range(2)] for n in ("wd_hi", "wd_lo"))
        x_hi, x_lo = ([c.sb(f"{n}{r}", [P, KD, P], F32R) for r in range(2)] for n in ("x_hi", "x_lo"))
        h_hi, h_lo = ([c.sb(f"{n}{r}", [P, KI, P], F32R) for r in range(2)] for n in ("h_hi", "h_lo"))
        sg = c.sb("sg", [P, 2, I0])
        h = [c.sb(f"h{u}", [P, I0]) for u in range(2)]
        xT_ps = c.ps("xT_ps", [P, KD, P])
        g_ps = [c.ps(f"g_ps{u}", [P, 512]) for u in range(2)]
        u_ps = [c.ps(f"u_ps{u}", [P, 512]) for u in range(2)]
        hT_ps = c.ps("hT_ps", [P, KI, P])
        y_ps = [c.ps(f"y_ps{u}", [P, D]) for u in range(2)]
        w_in = [c.sem(f"w_in{r}") for r in range(2)]
        x_in = [c.sem(f"x_in{r}") for r in range(2)]
        stored = [c.sem(f"stored{u}") for u in range(2)]
        w_high, w_low, turned, x_high, x_split, up, gated, hidden, h_turned, h_high, h_split, down, evac = (
            c.sem(n) for n in ("w_high", "w_low", "turned", "x_high", "x_split", "up", "gated", "hidden", "h_turned",
                               "h_high", "h_split", "down", "evac"))
        passed_s = c.sem("passed_sp")
        raws = [[wg[r], wu[r], wd[r]] for r in range(2)]
        highs = [[wg_hi[r], wu_hi[r], wd_hi[r]] for r in range(2)]
        lows = [[wg_lo[r], wu_lo[r], wd_lo[r]] for r in range(2)]
        with nc.Block() as block:
            @block.sync
            def _(sp):
                sp.sem_inc(stored[0], 16)
                sp.sem_inc(stored[1], 16)

                def load(p, r):
                    ex = sp.value_load(block_expert[0:1, bass.ds(p, 1)], min_val=0, max_val=E - 1)
                    sp.dma_start(x[:, 2 * r:2 * r + 2, :], table[bass.ds(p * BR, BR), :].rearrange("(s q) d -> q s d", q=P)).then_inc(x_in[r], 16)
                    for dst, src in zip(raws[r], (w_gate, w_up, w_down)):
                        sp.dma_start(dst[:], src[bass.ds(ex, 1), :, :].rearrange("a (k q) i -> q (a k) i", q=P)).then_inc(w_in[r], 16)

                def store(b, u):
                    sp.wait_ge(evac, b + 1)
                    sp.sem_inc(passed_s, 1)
                    sp.dma_start(returned[bass.ds(b * P, P), :], y[:, u, :]).then_inc(stored[u], 16)

                load(0, 0)
                load(1, 1)
                with sp.Fori(1, (NB0 - 1) // 2) as i:
                    for r in range(2):
                        sp.wait_ge(w_low, 3 * (2 * i + r - 1))
                        sp.sem_inc(passed_s, 1)
                        sp.wait_ge(turned, 2 * (2 * i + r - 1))
                        sp.sem_inc(passed_s, 1)
                        load(2 * i + r, r)
                        for u in range(2):
                            store(2 * (2 * i + r - 2) + u, u)
                sp.wait_ge(w_low, 3 * (NB0 - 2))
                sp.wait_ge(turned, 2 * (NB0 - 2))
                load(NB0 - 1, 0)
                for b in range(2 * (NB0 - 3), STEPS):
                    store(b, b % 2)
                for u in range(2):
                    sp.wait_ge(stored[u], 16 * (NB0 + 1))

            @block.tensor
            def _(pe):
                def turn_x(b, v, at):
                    pe.wait_ge(x_in[v // 2 % 2], 16 * (at(4) + v // 4 + 1))
                    pe.wait_ge(x_split, b)
                    for j in range(KD):
                        mm = pe.transpose(xT_ps[:, j, :], x[:, v % 4, j * P:(j + 1) * P], k.ident[:])
                    mm.then_inc(turned, 1)

                def up_products(b, v, at):
                    u, r = v % 2, v // 2 % 2
                    pe.wait_ge(x_split, b + 1)
                    if u == 0:
                        pe.wait_ge(w_low, 3 * (at(2) + v // 2) + 2)
                    for dst, hi, lo in ((g_ps, wg_hi, wg_lo), (u_ps, wu_hi, wu_lo)):
                        mm = three_pass(pe, dst[u][:, 0:I0], [(x_hi[u][:, j, :], x_lo[u][:, j, :], hi[r][:, j, :], lo[r][:, j, :])
                                                              for j in range(KD)])
                    mm.then_inc(up, 1)

                def step(b, v, at, left):
                    u, r = v % 2, v // 2 % 2
                    pe.wait_ge(hidden, b + 1)
                    for j in range(KI):
                        mm = pe.transpose(hT_ps[:, j, :], h[u][:, j * P:(j + 1) * P], k.ident[:])
                    mm.then_inc(h_turned, 1)
                    if left > 1:
                        up_products(b + 1, v + 1, at)
                    if left > 2:
                        turn_x(b + 2, v + 2, at)
                    pe.wait_ge(h_split, b + 1)
                    if u == 0:
                        pe.wait_ge(w_low, 3 * (at(2) + v // 2) + 3)
                    three_pass(pe, y_ps[u][:], [(h_hi[u][:, j, :], h_lo[u][:, j, :], wd_hi[r][:, j, :], wd_lo[r][:, j, :])
                                                for j in range(KI)]).then_inc(down, 1)

                turn_x(0, 0, lambda n: 0)
                up_products(0, 0, lambda n: 0)
                turn_x(1, 1, lambda n: 0)
                pe.sem_inc(down, START)
                rounds(pe, STEPS, PERIOD, step)

            @block.scalar
            def _(act):
                def split_w(p, r, n, fills):
                    act.wait_ge(w_in[r], 48 * fills)
                    act.wait_ge(down, START + 2 * p - 2)
                    act.copy(highs[r][n][:], raws[r][n][:]).then_inc(w_high, 1)

                def split_x(b, v):
                    act.wait_ge(turned, b + 1)
                    act.copy(x_hi[v % 2][:], xT_ps[:]).then_inc(x_high, 1)

                def step(b, v, at, left):
                    u = v % 2
                    act.wait_ge(up, b + 1)
                    act.activation(sg[:, u, :], g_ps[u][:, 0:I0], ACT.Silu).then_inc(gated, 1)
                    if left > 1:
                        split_x(b + 1, v + 1)
                    act.wait_ge(h_turned, b + 1)
                    act.wait_ge(down, START + b - 1)
                    act.copy(h_hi[u][:], hT_ps[:]).then_inc(h_high, 1)
                    if left > 2:
                        for n in ((0, 1), (2,))[u]:
                            split_w(at(2) + v // 2 + 1, (v // 2 + 1) % 2, n, at(4) + (v // 2 + 1) // 2 + 1)
                for n in range(3):
                    act.wait_ge(w_in[0], 48)
                    act.copy(highs[0][n][:], raws[0][n][:]).then_inc(w_high, 1)
                    if n == 0:
                        split_x(0, 0)
                rounds(act, STEPS, PERIOD, step)

            @block.vector
            def _(dve):
                def split_w(p, r, n):
                    dve.wait_ge(w_high, 3 * p + n + 1)
                    dve.tensor_tensor(lows[r][n][:], raws[r][n][:], highs[r][n][:], ALU.subtract).then_inc(w_low, 1)

                def split_x(b, v):
                    dve.wait_ge(x_high, b + 1)
                    dve.tensor_tensor(x_lo[v % 2][:], xT_ps[:], x_hi[v % 2][:], ALU.subtract).then_inc(x_split, 1)

                def gate_up(b, v):
                    dve.wait_ge(gated, b + 1)
                    dve.tensor_tensor(h[v % 2][:], sg[:, v % 2, :], u_ps[v % 2][:, 0:I0], ALU.mult).then_inc(hidden, 1)

                def split_h(b, v):
                    dve.wait_ge(h_high, b + 1)
                    dve.tensor_tensor(h_lo[v % 2][:], hT_ps[:], h_hi[v % 2][:], ALU.subtract).then_inc(h_split, 1)

                def split_next(v, at):
                    for n in ((0, 1), (2,))[v % 2]:
                        split_w(at(2) + v // 2 + 1, (v // 2 + 1) % 2, n)

                def step(b, v, at, left):
                    u = v % 2
                    if left > 1:
                        gate_up(b + 1, v + 1)
                    if left > 2:
                        split_x(b + 2, v + 2)
                    dve.wait_ge(down, START + b + 1)
                    dve.wait_ge(stored[u], 16 * (at(2) + v // 2 + 1))
                    dve.tensor_copy(y[:, u, :], y_ps[u][:]).then_inc(evac, 1)
                    if left > 1:
                        split_h(b + 1, v + 1)
                    if left > 3:
                        split_next(v + 1, at)
                split_w(0, 0, 0)
                split_x(0, 0)
                split_w(0, 0, 1)
                split_w(0, 0, 2)
                gate_up(0, 0)
                split_x(1, 1)
                split_h(0, 0)
                split_next(0, lambda n: 0)
                rounds(dve, STEPS, PERIOD, step, 3)


def scale_split(nc, tag, src, norm, z_hi, z_lo, kept_in):
    with ExitStack() as st:
        c = Ctx(nc, st, tag)
        z = c.sb("z", [P, 2, D])
        made, high, low, kept, ready = c.sem("made"), c.sem("high"), c.sem("low"), c.sem("kept"), c.sem("ready")
        if norm is not None:
            mean, rstd, dinv, half_dinv, z_scale = norm
        with nc.Block() as block:
            @block.vector
            def _(dve):
                dve.sem_inc(low, START)
                dve.sem_inc(kept, START)
                if norm is not None:
                    dve.tensor_scalar(half_dinv[:], dinv[:], 0.5, None, ALU.mult).then_inc(ready, 1)
                    dve.tensor_tensor(z_scale[:], rstd[:], dinv[:], ALU.mult).then_inc(ready, 1)
                    dve.wait_ge(ready, 2)
                with dve.Fori(0, NT // 2) as i:
                    for u in range(2):
                        if norm is not None:
                            dve.wait_ge(low, START + 2 * i)
                            dve.wait_ge(kept, START + 2 * i)
                            dve.tensor_scalar(z[:, u, :], src[:, 2 * i + u, :], mean[:, bass.ds(2 * i + u, 1)],
                                              z_scale[:, bass.ds(2 * i + u, 1)], ALU.subtract, ALU.mult).then_inc(made, 1)
                    for u in range(2):
                        z_t = z[:, u, :] if norm is not None else src[:, 2 * i + u, :]
                        dve.wait_ge(high, 2 * i + u + 1)
                        dve.tensor_tensor(z_lo[:, 2 * i + u, :], z_t, z_hi[:, 2 * i + u, :], ALU.subtract).then_inc(low, 1)
                        if norm is not None:
                            dve.tensor_scalar(kept_in[:, 2 * i + u, :], z_t, dinv[:, bass.ds(2 * i + u, 1)], None,
                                              ALU.mult).then_inc(kept, 1)

            @block.scalar
            def _(act):
                with act.Fori(0, NT // 2) as i:
                    for u in range(2):
                        if norm is not None:
                            act.wait_ge(made, 2 * i + u + 1)
                        z_t = z[:, u, :] if norm is not None else src[:, 2 * i + u, :]
                        act.copy(z_hi[:, 2 * i + u, :], z_t).then_inc(high, 1)


def graph_product(nc, tag, adjT_dram, adj, z_hi, z_lo, out, factor):
    HB = NT // 2
    HW = N // 2
    R = 4
    with ExitStack() as st:
        c = Ctx(nc, st, tag)
        a = c.sb("a", [P, R, HW])
        at = c.sb("at", [P, R, HW], BF16)
        s = [c.sb(f"s{r}", [P, HW], F32R) for r in range(R)]
        acc = [c.ps(f"acc{b}", [P, D]) for b in range(HB)]
        loaded = [c.sem(f"loaded{r}") for r in range(R)]
        built, used, summed, read = c.sem("built"), c.sem("used"), c.sem("summed"), c.sem("read")
        with nc.Block() as block:
            @block.sync
            def _(sp):
                for half in range(2):
                    for j in range(NT):
                        if half or j >= R:
                            sp.wait_ge(built, half * NT + j - R + 1)
                        cols = slice(half * HW, (half + 1) * HW)
                        sp.dma_start(at[:, j % R, :], adjT_dram[j * P:(j + 1) * P, cols]).then_inc(loaded[j % R], 16)
                        if adj is not None:
                            sp.dma_start(a[:, j % R, :], adj[j * P:(j + 1) * P, cols]).then_inc(loaded[j % R], 16)

            def build(eng, half):
                for j in range(NT):
                    eng.wait_ge(used, half * NT + j + 1)
                    src = at[:, j % R, :]
                    per = 16 if adj is None else 32
                    eng.wait_ge(loaded[j % R], per * (half * (NT // R) + j // R + 1))
                    if adj is not None:
                        eng.tensor_tensor(s[j % R][:], a[:, j % R, :], src, ALU.add).then_inc(built, 1)
                    else:
                        eng.copy(s[j % R][:], src).then_inc(built, 1)

            @block.vector
            def _(dve):
                def finish(half):
                    for b in range(HB):
                        o = out[:, half * HB + b, :]
                        dve.wait_ge(summed, half * HB + b + 1)
                        if factor is not None:
                            dve.scalar_tensor_tensor(out=o, in0=acc[b][:], scalar=factor[:, half * HB + b:half * HB + b + 1],
                                                     in1=o, op0=ALU.mult, op1=ALU.add).then_inc(read, 1)
                        else:
                            dve.tensor_tensor(o, acc[b][:], o, ALU.add).then_inc(read, 1)
                for half in range(2):
                    if adj is not None:
                        build(dve, half)
                    finish(half)

            if adj is None:
                @block.scalar
                def _(act):
                    with act.Fori(0, 2) as half:
                        build(act, half)

            @block.tensor
            def _(pe):
                pe.sem_inc(used, R)
                pe.sem_inc(read, HB)
                with pe.Fori(0, 2) as half:
                    for j in range(NT):
                        pe.wait_ge(built, half * NT + j + 1)
                        for b in range(HB):
                            if j == 0:
                                pe.wait_ge(read, half * HB + b + 1)
                            lhs = s[j % R][:, b * P:(b + 1) * P]
                            pe.matmul(acc[b][:], lhs, z_hi[:, j, :], start=(j == 0), stop=False)
                            mm = pe.matmul(acc[b][:], lhs, z_lo[:, j, :], start=False, stop=(j == NT - 1))
                            if j == NT - 1:
                                mm.then_inc(summed, 1)
                        if j < NT - 1:
                            mm.then_inc(used, 1)
                    pe.wait_ge(summed, half * HB + HB)
                    pe.sem_inc(used, 1)


def experts_mlp(nc, k, table, W1, b1, W2, b2, returned):
    MC = D // P
    NC = HID // 512
    R = 4
    with ExitStack() as st:
        c = Ctx(nc, st, "moe1")
        raw = c.sb("raw", [P, R, KD, 512])
        w_hi = [c.sb(f"w_hi{u}", [P, KD, 512], F32R) for u in range(2)]
        w_lo = [c.sb(f"w_lo{u}", [P, KD, 512], F32R) for u in range(2)]
        x = c.sb("x", [P, CT, D])
        x_hi = c.sb("x_hi", [P, KD, CAP], F32R)
        x_lo = c.sb("x_lo", [P, KD, CAP], F32R)
        hf = c.sb("hf", [P, 2, CAP])
        h_hi = [c.sb(f"h_hi{m}", [P, CAP], F32R) for m in range(HID // P)]
        h_lo = [c.sb(f"h_lo{m}", [P, CAP], F32R) for m in range(HID // P)]
        b1_rows = c.sb("b1_rows", [P, P])
        b1_col = c.sb("b1_col", [P, E, HID // P])
        b2_row = c.sb("b2_row", [P, 2, D])
        y = c.sb("y", [P, CT, D])
        xT_ps = [c.ps(f"xT_ps{u}", [P, CAP]) for u in range(2)]
        h_ps = [c.ps(f"h_ps{u}", [P, CAP]) for u in range(2)]
        y_ps = [c.ps(f"y_ps{s}", [P, D]) for s in range(CT)]
        raw_in = [c.sem(f"raw_in{r}") for r in range(R)]
        b1_in, x_in, b2_in = c.sem("b1_in"), c.sem("x_in"), c.sem("b2_in")
        w_high, w_low, w_used = c.sem("w_high"), c.sem("w_low"), c.sem("w_used")
        turned, x_high, x_low, b1_turned, b1_ready = (c.sem(n) for n in ("turned", "x_high", "x_low", "b1_turned", "b1_ready"))
        up, act_done, h_high, h_low, down, y_done, stored = (
            c.sem(n) for n in ("up", "act_done", "h_high", "h_low", "down", "y_done", "stored"))
        passed_s, passed_p = c.sem("passed_sp"), c.sem("passed_pool")
        with nc.Block() as block:
            @block.sync
            def _(sp):
                sp.sem_inc(stored, 16)
                sp.dma_start(b1_rows[:], b1.rearrange("e (m p) -> (e m) p", p=P)).then_inc(b1_in, 16)

                def chunk(e, n):
                    src = W1[bass.ds(e, 1), :, n * 512:(n + 1) * 512] if n < NC else \
                        W2[bass.ds(e, 1), (n - NC) * 512:(n - NC + 1) * 512, :]
                    sp.dma_start(raw[:, n % R], src.rearrange("a (k p) i -> p (a k) i", p=P)).then_inc(raw_in[n % R], 16)

                def store(e):
                    sp.wait_ge(y_done, START + CT * (e + 1))
                    sp.sem_inc(passed_s, 1)
                    sp.dma_start(returned[bass.ds(e * CAP, CAP), :].rearrange("(s p) d -> p s d", p=P), y[:]).then_inc(stored, 16)

                def rows(e):
                    sp.dma_start(x[:], table[bass.ds(e * CAP, CAP), :].rearrange("(s p) d -> p s d", p=P)).then_inc(x_in, 16)

                rows(0)
                for n in range(R):
                    chunk(0, n)
                with sp.Fori(0, E - 1) as e:
                    for n in range(R, 2 * NC):
                        sp.wait_ge(w_low, 2 * NC * e + n - R + 1)
                        sp.sem_inc(passed_s, 1)
                        chunk(e, n)
                    sp.wait_ge(turned, KD * (e + 1))
                    sp.sem_inc(passed_s, 1)
                    rows(e + 1)
                    for n in range(R):
                        sp.wait_ge(w_low, 2 * NC * e + 2 * NC + n - R + 1)
                        sp.sem_inc(passed_s, 1)
                        chunk(e + 1, n)
                    store(e)
                for n in range(R, 2 * NC):
                    sp.wait_ge(w_low, 2 * NC * (E - 1) + n - R + 1)
                    chunk(E - 1, n)
                store(E - 1)
                sp.wait_ge(stored, 16 * (E + 1))

            @block.tensor
            def _(pe):
                pe.sem_inc(h_low, START)
                pe.sem_inc(y_done, START)
                pe.sem_inc(w_used, 2)
                pe.sem_inc(act_done, 2)
                pe.wait_ge(b1_in, 16)
                pe.transpose(xT_ps[0][:, 0:P], b1_rows[:], k.ident[:]).then_inc(b1_turned, 1)
                pe.wait_ge(b1_ready, 1)

                def turn_rows(e):
                    pe.wait_ge(x_in, 16 * (e + 1))
                    for j in range(KD):
                        if j >= 2:
                            pe.wait_ge(x_low, KD * e + j - 1)
                        for s in range(CT):
                            mm = pe.transpose(xT_ps[j % 2][:, s * P:(s + 1) * P], x[:, s, j * P:(j + 1) * P], k.ident[:])
                        mm.then_inc(turned, 1)

                def up_chunk(e, n):
                    pe.wait_ge(w_low, 2 * NC * e + n + 1)
                    for m in range(MC):
                        pe.wait_ge(act_done, (HID // P) * e + n * MC + m + 1)
                        cols = slice(m * P, (m + 1) * P)
                        mm = three_pass(pe, h_ps[m % 2][:], [(w_hi[n % 2][:, j, cols], w_lo[n % 2][:, j, cols],
                                                             x_hi[:, j, :], x_lo[:, j, :]) for j in range(KD)])
                        mm.then_inc(up, 1)
                    pe.wait_ge(up, (HID // P) * e + n * MC + MC)
                    pe.sem_inc(w_used, 1)

                def down_chunk(e, n):
                    pe.wait_ge(w_low, 2 * NC * e + NC + n + 1)
                    for m in range(MC):
                        pe.wait_ge(h_low, START + (HID // P) * e + n * MC + m + 1)
                        for s in range(CT):
                            if n == 0 and m == 0:
                                pe.wait_ge(y_done, START + CT * e)
                            for q, (a, b) in enumerate(((h_hi, w_hi), (h_hi, w_lo), (h_lo, w_hi))):
                                mm = pe.matmul(y_ps[s][:], a[n * MC + m][:, s * P:(s + 1) * P], b[(NC + n) % 2][:, m, :],
                                               start=(n == 0 and m == 0 and q == 0), stop=(n == NC - 1 and m == MC - 1 and q == 2))
                    mm.then_inc(down, 1)
                    pe.wait_ge(down, NC * e + n + 1)
                    pe.sem_inc(w_used, 1)

                def expert(e, last):
                    pe.wait_ge(x_low, KD * (e + 1))
                    for n in range(NC):
                        up_chunk(e, n)
                    for n in range(NC):
                        down_chunk(e, n)
                        if n == 1 and not last:
                            turn_rows(e + 1)

                turn_rows(0)
                with pe.Fori(0, E - 1) as e:
                    expert(e, False)
                expert(E - 1, True)

            @block.scalar
            def _(act):
                def w_part(e, n):
                    act.wait_ge(raw_in[n % R], 16 * (2 * e + n // R + 1))
                    act.wait_ge(w_used, 2 * NC * e + n + 1)
                    act.copy(w_hi[n % 2][:], raw[:, n % R]).then_inc(w_high, 1)

                def x_parts(e):
                    for j in range(KD):
                        act.wait_ge(turned, KD * e + j + 1)
                        act.copy(x_hi[:, j, :], xT_ps[j % 2][:]).then_inc(x_high, 1)

                def gelus(e, n):
                    for m in range(MC):
                        g = (HID // P) * e + n * MC + m
                        act.wait_ge(up, g + 1)
                        act.wait_ge(h_low, START + (HID // P) * e + max(n * MC + m - 1, 0))
                        act.activation(hf[:, m % 2, :], h_ps[m % 2][:], ACT.Gelu,
                                       bias=b1_col[:, bass.ds(e, 1), n * MC + m]).then_inc(act_done, 1)
                        act.wait_ge(act_done, g + 3)
                        act.copy(h_hi[n * MC + m][:], hf[:, m % 2, :]).then_inc(h_high, 1)

                x_parts(0)
                w_part(0, 0)
                w_part(0, 1)

                def expert_(e, last):
                    for n in range(NC):
                        gelus(e, n)
                        w_part(e, n + 2)
                    for n in range(NC):
                        if n == 1 and not last:
                            x_parts(e + 1)
                        if n < NC - 2:
                            w_part(e, NC + n + 2)
                        elif not last:
                            w_part(e + 1, n - NC + 2)
                with act.Fori(0, E - 1) as e:
                    expert_(e, False)
                expert_(E - 1, True)

            @block.vector
            def _(dve):
                dve.wait_ge(b1_turned, 1)
                dve.tensor_copy(b1_col[:].rearrange("p e m -> p (e m)"), xT_ps[0][:, 0:P]).then_inc(b1_ready, 1)

                def w_part(e, n):
                    dve.wait_ge(w_high, 2 * NC * e + n + 1)
                    dve.tensor_tensor(w_lo[n % 2][:], raw[:, n % R], w_hi[n % 2][:], ALU.subtract).then_inc(w_low, 1)

                def x_parts(e):
                    for j in range(KD):
                        dve.wait_ge(x_high, KD * e + j + 1)
                        dve.tensor_tensor(x_lo[:, j, :], xT_ps[j % 2][:], x_hi[:, j, :], ALU.subtract).then_inc(x_low, 1)

                def h_parts(e, n):
                    for m in range(MC):
                        dve.wait_ge(h_high, (HID // P) * e + n * MC + m + 1)
                        dve.tensor_tensor(h_lo[n * MC + m][:], hf[:, m % 2, :], h_hi[n * MC + m][:], ALU.subtract).then_inc(h_low, 1)

                def finish(e):
                    dve.wait_ge(down, NC * (e + 1))
                    dve.wait_ge(b2_in, 16 * (e + 1))
                    dve.wait_ge(stored, 16 * e + 16)
                    for s in range(CT):
                        dve.tensor_tensor(y[:, s, :], y_ps[s][:], b2_row[:, 0, :], ALU.add).then_inc(y_done, 1)

                x_parts(0)
                w_part(0, 0)
                w_part(0, 1)

                def expert_(e, last):
                    for n in range(NC):
                        h_parts(e, n)
                        w_part(e, n + 2)
                    for n in range(NC):
                        if n == 1 and not last:
                            x_parts(e + 1)
                        if n < NC - 2:
                            w_part(e, NC + n + 2)
                        elif not last:
                            w_part(e + 1, n - NC + 2)
                    finish(e)
                with dve.Fori(0, E - 1) as e:
                    expert_(e, False)
                expert_(E - 1, True)

            @block.gpsimd
            def _(pool):
                with pool.Fori(0, E) as e:
                    pool.wait_ge(y_done, START + CT * e + 0)
                    pool.sem_inc(passed_p, 1)
                    pool.dma_start(b2_row[:, 0, :], b2[bass.ds(e, 1), :].to_broadcast([P, D])).then_inc(b2_in, 16)


def graph_moe_kernel(nc, x, adj, W_seq, a1, a2, W_out, b_out, gate_w, w_gate, w_up, w_down, Wr, br, W1, b1, W2, b2, out):
    rows0, rows1 = NB0 * BR, E * CAP

    def scratch(name, shape):
        return nc.dram_tensor(name, shape, F32, kind="Internal").ap()
    s1_rows, iso_row = scratch("s1_rows", [H, N]), scratch("iso_row", [1, N])
    sent0, back0 = scratch("sent0", [rows0, D]), scratch("back0", [rows0, D])
    sent1, back1 = scratch("sent1", [rows1, D]), scratch("back1", [rows1, D])
    x3 = scratch("x3", [N, D])

    SPENT.clear()
    adjT_dram = nc.dram_tensor("adjT_dram", [N, N], BF16, kind="Internal").ap()
    with ExitStack() as st:
        c = Ctx(nc, st, "all")
        k = make_constants(nc, c)
        mean, rstd, dinv = c.sb("mean", [P, NT]), c.sb("rstd", [P, NT]), c.sb("dinv", [P, NT])
        put_at, get_from = c.sb("put_at", [P, TOPK, NT], U32), c.sb("get_from", [P, TOPK, NT], U32)
        weight = c.sb("weight", [P, TOPK, NT])
        constants(nc, k)

        with ExitStack() as st1:
            c1 = Ctx(nc, st1, "one")
            seq = c1.sb("seq", [P, NT, D])
            with ExitStack() as st2:
                c2 = Ctx(nc, st2, "gat")
                adjT = c2.sb("adjT", [P, NT, N], BF16)
                isolated, rowsum, colsum = (c2.sb(n, [P, NT]) for n in ("isolated", "rowsum", "colsum"))
                s1, s2, ea, eb, g, ns2, big_s2 = (c2.sb(n, [P, NT, H]) for n in ("s1", "s2", "ea", "eb", "g", "ns2", "big_s2"))
                with ExitStack() as st3:
                    x_in = Ctx(nc, st3, "first").sb("x", [P, NT, D])
                    transpose_adj(nc, k, adj, adjT, isolated, rowsum, colsum, x, x_in)
                    norm_stats(nc, "norm0", x_in, mean, rstd)
                    project_heads(nc, k, x_in, mean, rstd, W_seq, a1, a2, seq, s1, s2, adjT, adjT_dram, isolated, iso_row)
                softmax_factors(nc, k, s1, s2, ea, eb, g, ns2, big_s2, s1_rows, rowsum, colsum, dinv)
                attention(nc, k, adjT, seq, ea, eb, g, ns2, big_s2, s1_rows, [sent0, sent1])
            recycle(nc)
            x_sb = c1.sb("x", [P, NT, D])
            project_out(nc, k, seq, x, W_out, b_out, x_sb)
            norm_stats(nc, "norm1", x_sb, mean, rstd)
            block_expert = c1.sb("block_expert", [P, NB0], I32)
            route(nc, k, "route0", x_sb, mean, rstd, gate_w, None, seq, put_at, get_from, weight, block_expert)
            dispatch(nc, "put0", seq, put_at, sent0, rows0)
            experts_gated(nc, k, block_expert, sent0, w_gate, w_up, w_down, back0, seq)
            gather_experts(nc, "get0", back0, get_from, weight, x_sb, None)
            norm_stats(nc, "norm2", x_sb, mean, rstd)
            recycle(nc)
            with ExitStack() as st2:
                c2 = Ctx(nc, st2, "diffuse")
                half_dinv, z_scale = (c2.sb(n, [P, NT]) for n in ("half_dinv", "z_scale"))
                z_hi, z_lo = c2.sb("z_hi", [P, NT, D], F32R), c2.sb("z_lo", [P, NT, D], F32R)
                scale_split(nc, "split2", x_sb, (mean, rstd, dinv, half_dinv, z_scale), z_hi, z_lo, seq)
                graph_product(nc, "sym", adjT_dram, adj, z_hi, z_lo, seq, half_dinv)
                scale_split(nc, "split3", seq, None, z_hi, z_lo, None)
                graph_product(nc, "prod", adjT_dram, None, z_hi, z_lo, x_sb, None)
            norm_stats(nc, "norm3", x_sb, mean, rstd)
            route(nc, k, "route1", x_sb, mean, rstd, Wr, br, seq, put_at, get_from, weight, None)
            dispatch(nc, "put1", seq, put_at, sent1, rows1, x_sb, x3)
            recycle(nc)
        experts_mlp(nc, k, sent1, W1, b1, W2, b2, back1)
        with ExitStack() as st1:
            x_sb = Ctx(nc, st1, "end").sb("x", [P, NT, D])
            gather_experts(nc, "get1", back1, get_from, weight, x_sb, out, x3)


_INS = ['x', 'adj', 'L0_gnn_W_seq', 'L0_gnn_a1', 'L0_gnn_a2', 'L0_gnn_W_out', 'L0_gnn_b_out', 'L0_ffn_gate_w',
        'L0_ffn_w_gate', 'L0_ffn_w_up', 'L0_ffn_w_down', 'L1_ffn_Wr', 'L1_ffn_br', 'L1_ffn_W1', 'L1_ffn_b1',
        'L1_ffn_W2', 'L1_ffn_b2']
_OUTS = [((2048, 512), 'float32')]


def kernel(**inputs):
    import numpy as _np
    import concourse.bacc as _bacc
    from concourse import mybir as _mybir
    from concourse.bass_utils import run_bass_kernel_spmd as _run

    nc = _bacc.Bacc("TRN2", target_bir_lowering=False, num_devices=1)
    arrays, args = {}, []
    for name in _INS:
        a = _np.ascontiguousarray(inputs[name])
        arrays[f"in_{name}_dram"] = a
        args.append(nc.dram_tensor(f"in_{name}_dram", a.shape, _mybir.dt.from_np(a.dtype), kind="ExternalInput").ap())
    for i, (shape, dtype) in enumerate(_OUTS):
        dt = _mybir.dt.from_np(_np.dtype(dtype))
        args.append(nc.dram_tensor(f"out_{i}_dram", shape, dt, kind="ExternalOutput").ap())
    graph_moe_kernel(nc, *args)
    r = _run(nc, [arrays], core_ids=[0])
    got = tuple(r.results[0][f"out_{i}_dram"] for i in range(len(_OUTS)))
    return got[0]
```

```python
from contextlib import ExitStack

import concourse.bass as bass
from concourse import mybir

F32 = mybir.dt.float32
F32R = mybir.dt.float32r
BF16 = mybir.dt.bfloat16
U32 = mybir.dt.uint32
I32 = mybir.dt.int32
ALU = mybir.AluOpType
ACT = mybir.ActivationFunctionType
AX = mybir.AxisListType
RMAX = bass.bass_isa.ReduceOp.max

P = 128
N = 2048
D = 512
NT = N // P
KD = D // P
H = 16
DH = D // H
E = 8
TOPK = 2
I0 = 384
KI = I0 // P
BR = 256
NB0 = N * TOPK // BR + E - 1
HID = 2048
CAP = N * TOPK // E
CT = CAP // P
WC = D + 2 * H
EPS = 1e-5
SLOPE = 0.2
BIG = 1e30
FAR = 1.0e6


START = 3


def rounds(eng, total, period, step, tail=2):
    full = (total - tail) // period
    with eng.Fori(0, full) as i:
        for v in range(period):
            step(period * i + v, v, lambda n: i * (period // n), total)
    for b in range(full * period, total):
        v = b % period
        step(b, v, lambda n, base=b - v: base // n, total - b)


class Chain:

    def __init__(self, eng, sem, passed=None):
        self.eng, self.sem, self.n, self.off, self.passed = eng, sem, 0, 0, passed

    def link(self, ins):
        self.n += 1
        ins.then_inc(self.sem, 1)
        self.hold()

    def hold(self):
        self.eng.wait_ge(self.sem, self.off + self.n)
        if self.passed is not None:
            self.eng.sem_inc(self.passed, 1)

    def loop(self, i, per_round):
        self.off = i * per_round


SPENT = []


def recycle(nc):
    nc.clear_and_free_semaphores(list(SPENT))
    SPENT.clear()
    nc.all_engine_barrier()


class Ctx:

    def __init__(self, nc, stack, tag):
        self.nc, self.stack, self.tag = nc, stack, tag

    def sb(self, name, shape, dt=F32):
        return self.stack.enter_context(self.nc.sbuf_tensor(f"{self.tag}_{name}", shape, dt))

    def ps(self, name, shape, dt=F32):
        return self.stack.enter_context(self.nc.psum_tensor(f"{self.tag}_{name}", shape, dt))

    def sem(self, name):
        s = self.nc.alloc_semaphore(f"{self.tag}_{name}")
        SPENT.append(s)
        return s


def constants(nc, k):
    with ExitStack() as st:
        c = Ctx(nc, st, "const")
        filled, shaped = c.sem("filled"), c.sem("shaped")
        with nc.Block() as block:
            @block.gpsimd
            def _(pool):
                pool.memset(k.ident[:], 0.0).then_inc(filled, 1)
                pool.memset(k.before[:], 1.0).then_inc(filled, 1)
                pool.memset(k.ones[:], 1.0).then_inc(filled, 1)
                pool.memset(k.zeros[:], 0.0).then_inc(filled, 1)
                pool.memset(k.zerob[:], 0.0).then_inc(filled, 1)
                pool.wait_ge(filled, 5)
                pool.affine_select(out=k.ident[:], in_=k.ident[:], compare_op=ALU.not_equal, fill=1.0,
                                   base=0, pattern=[[-1, P]], channel_multiplier=1).then_inc(shaped, 1)
                pool.affine_select(out=k.before[:], in_=k.before[:], compare_op=ALU.is_gt, fill=0.0,
                                   base=0, pattern=[[1, P]], channel_multiplier=-1).then_inc(shaped, 1)
                pool.iota(k.expert_id[:], pattern=[[1, E]], base=0, channel_multiplier=0,
                          allow_small_or_imprecise_dtypes=True).then_inc(shaped, 1)
                pool.iota(k.block_start[:], pattern=[[BR, N // BR]], base=0, channel_multiplier=0,
                          allow_small_or_imprecise_dtypes=True).then_inc(shaped, 1)
                pool.iota(k.block_id[:], pattern=[[1, NB0]], base=0, channel_multiplier=0,
                          allow_small_or_imprecise_dtypes=True).then_inc(shaped, 1)
                pool.wait_ge(shaped, 5)
                pool.tensor_copy(k.identb[:], k.ident[:]).then_inc(shaped, 1)


def norm_stats(nc, tag, bn, mean, rstd):
    with ExitStack() as st:
        c = Ctx(nc, st, tag)
        mv = c.sb("mv", [P, NT, 2])
        var = c.sb("var", [P, NT])
        root = c.sb("root", [P, NT])
        r0 = c.sb("r0", [P, NT])
        t = c.sb("t", [P, NT])
        ch_s, var_ready, root_ready = c.sem("chain"), c.sem("var_ready"), c.sem("root_ready")
        with nc.Block() as block:
            @block.vector
            def _(dve):
                ch = Chain(dve, ch_s)
                for n in range(NT):
                    dve.bn_aggr(mv[:, n, :], bn[:, n, :]).then_inc(ch_s, 1)
                ch.n = NT
                dve.wait_ge(ch_s, NT)
                ch.link(dve.tensor_copy(mean[:], mv[:, :, 0]))
                dve.tensor_scalar(var[:], mv[:, :, 1], EPS, None, ALU.add).then_inc(var_ready, 1)
                dve.wait_ge(root_ready, 1)
                ch.link(dve.reciprocal(r0[:], root[:]))
                ch.link(dve.tensor_tensor(t[:], r0[:], r0[:], ALU.mult))
                ch.link(dve.tensor_tensor(t[:], t[:], var[:], ALU.mult))
                ch.link(dve.tensor_scalar(t[:], t[:], -0.5, 1.5, ALU.mult, ALU.add))
                dve.tensor_tensor(rstd[:], r0[:], t[:], ALU.mult).then_inc(ch_s, 1)

            @block.scalar
            def _(act):
                act.wait_ge(var_ready, 1)
                act.activation(root[:], var[:], ACT.Sqrt).then_inc(root_ready, 1)


def project_heads(nc, k, x_sb, mean, rstd, w_hi, w_lo, seq, s1, s2, adjT, adjT_dram, isolated, iso_row):
    with ExitStack() as st:
        c = Ctx(nc, st, "proj")
        FILL = 4
        xn = c.sb("xn", [P, 2, D])
        iso = c.sb("iso", [P, N])
        isob = c.sb("isob", [P, N], BF16)
        isoT = c.sb("isoT", [NT, P])
        hi = [c.sb(f"hi{u}", [P, KD, P], F32R) for u in range(2)]
        lo = [c.sb(f"lo{u}", [P, KD, P], F32R) for u in range(2)]
        xT = [c.ps(f"xT{u}", [P, KD, P]) for u in range(2)]
        out = [c.ps(f"out{u}", [P, D]) for u in range(2)]
        sc = [c.ps(f"sc{u}", [P, 2 * H]) for u in range(2)]
        isoT_ps = c.ps("isoT_ps", [NT, P])
        normed, turned, high, low = c.sem("normed"), c.sem("turned"), c.sem("high"), c.sem("low")
        summed, copied, scored = c.sem("summed"), c.sem("copied"), c.sem("scored")
        iso_turned, iso_kept, iso_wrote, iso_in, iso_cast, filled_p, filled_v = (
            c.sem(x) for x in ("iso_turned", "iso_kept", "iso_wrote", "iso_in", "iso_cast", "filled_pool", "filled_dve"))
        spilled = [c.sem(f"spilled{q}") for q in range(4)]
        with nc.Block() as block:
            @block.sync
            def _(sp):
                def spill(q):
                    sp.dma_start(adjT_dram[512 * q:512 * q + 512, :].rearrange("(t p) n -> p t n", p=P),
                                 adjT[:, 4 * q:4 * q + 4, :]).then_inc(spilled[q], 16)
                spill(3)
                sp.wait_ge(iso_kept, 1)
                sp.dma_start(iso_row.rearrange("a (t p) -> (a t) p", p=P), isoT[:]).then_inc(iso_wrote, 16)
                sp.wait_ge(iso_wrote, 16)
                sp.dma_start(iso[:], iso_row.to_broadcast([P, N])).then_inc(iso_in, 16)
                for q in range(3):
                    spill(q)
                for q in range(4):
                    sp.wait_ge(spilled[q], 16)

            @block.gpsimd
            def _(pool):
                pool.wait_ge(iso_cast, 1)
                for t in range(NT - FILL):
                    if t % 4 == 0:
                        pool.wait_ge(spilled[t // 4], 16)
                    pool.tensor_tensor(adjT[:, t, :], adjT[:, t, :], isob[:], ALU.add).then_inc(filled_p, 1)

            @block.scalar
            def _(act):
                act.sem_inc(copied, START)

                def high_part(t, u):
                    act.wait_ge(summed, START + t - 1)
                    act.wait_ge(turned, START + t + 1)
                    act.copy(hi[u][:], xT[u][:]).then_inc(high, 1)

                def step(t, u, at, left):
                    if left > 1:
                        high_part(t + 1, (u + 1) % 2)
                    act.wait_ge(summed, START + t + 1)
                    act.copy(seq[:, t, :], out[u][:]).then_inc(copied, 1)
                act.wait_ge(turned, START + 1)
                act.copy(hi[0][:], xT[0][:]).then_inc(high, 1)
                act.wait_ge(iso_in, 16)
                act.copy(isob[:], iso[:]).then_inc(iso_cast, 1)
                rounds(act, NT, 2, step)

            @block.vector
            def _(dve):
                dve.sem_inc(scored, START)
                dve.wait_ge(iso_turned, 1)
                dve.tensor_copy(isoT[:], isoT_ps[:]).then_inc(iso_kept, 1)

                def norm(t, u):
                    dve.tensor_scalar(xn[:, u, :], x_sb[:, t, :], mean[:, bass.ds(t, 1)], rstd[:, bass.ds(t, 1)],
                                      ALU.subtract, ALU.mult).then_inc(normed, 1)

                def low_part(t, u):
                    dve.wait_ge(high, t + 1)
                    dve.tensor_tensor(lo[u][:], xT[u][:], hi[u][:], ALU.subtract).then_inc(low, 1)

                def step(t, v, at, left):
                    u = v % 2
                    if left > 2:
                        dve.wait_ge(turned, START + t + 1)
                        norm(t + 2, u)
                    if left > 1:
                        low_part(t + 1, (u + 1) % 2)
                    dve.wait_ge(summed, START + t + 1)
                    dve.tensor_copy(s1[:, t, :], sc[u][:, 0:H]).then_inc(scored, 1)
                    dve.tensor_copy(s2[:, t, :], sc[u][:, H:2 * H]).then_inc(scored, 1)
                    if v == 3:
                        dve.wait_ge(iso_cast, 1)
                        dve.wait_ge(spilled[3], 16)
                        a_t = adjT[:, NT - FILL + at(4), :]
                        dve.tensor_tensor(a_t, a_t, isob[:], ALU.add).then_inc(filled_v, 1)
                norm(0, 0)
                norm(1, 1)
                low_part(0, 0)
                rounds(dve, NT, NT // FILL, step)

            @block.tensor
            def _(pe):
                pe.sem_inc(turned, START)
                pe.sem_inc(summed, START)
                pe.transpose(isoT_ps[:], isolated[:], k.ident[:]).then_inc(iso_turned, 1)

                def turn(t, u):
                    pe.wait_ge(normed, t + 1)
                    for j in range(KD):
                        mm = pe.transpose(xT[u][:, j, :], xn[:, u, j * P:(j + 1) * P], k.ident[:])
                    mm.then_inc(turned, 1)

                def step(t, u, at, left):
                    if left > 1:
                        turn(t + 1, (u + 1) % 2)
                    pe.wait_ge(low, t + 1)
                    pe.wait_ge(copied, START + t - 1)
                    pe.wait_ge(scored, START + 2 * t - 2)
                    terms = [(hi[u][:, j, :], lo[u][:, j, :], w_hi[:, j, :], w_lo[:, j, :]) for j in range(KD)]
                    three_pass(pe, out[u][:], [(a, b, x[:, 0:D], y[:, 0:D]) for a, b, x, y in terms])
                    three_pass(pe, sc[u][:], [(a, b, x[:, D:WC], y[:, D:WC]) for a, b, x, y in terms]).then_inc(summed, 1)
                turn(0, 0)
                rounds(pe, NT, 2, step)


def three_pass(pe, out, terms):
    n = len(terms)
    for j, (ah, al, bh, bl) in enumerate(terms):
        pe.matmul(out, ah, bh, start=(j == 0), stop=False)
        pe.matmul(out, ah, bl, start=False, stop=False)
        mm = pe.matmul(out, al, bh, start=False, stop=(j == n - 1))
    return mm


def transpose_adj(nc, k, adj, adjT, isolated, rowsum, colsum, x, x_sb, bn, W_seq, a1, a2, w, w_hi, w_lo):
    with ExitStack() as st:
        c = Ctx(nc, st, "adj")
        a = c.sb("a", [P, 2, N])
        ab = c.sb("ab", [P, 2, N], BF16)
        turned_ps = [c.ps(f"turned{u}", [P, NT, P], BF16) for u in range(2)]
        col_ps = c.ps("col_ps", [P, NT])
        loaded = [c.sem(f"loaded{u}") for u in range(2)]
        a_rows = c.sb("a_rows", [P, 2, DH])
        prod = c.sb("prod", [P, KD, H, DH])
        x_in = [c.sem(f"x_in{q}") for q in range(4)]
        cast, turned, kept, ended, stats = (c.sem(x) for x in ("cast", "turned", "kept", "ended", "stats"))
        w_in, halved, w_full, w_high, w_split = (c.sem(x) for x in ("w_in", "halved", "w_full", "w_high", "w_split"))
        passed = c.sem("passed")
        with nc.Block() as block:
            @block.sync
            def _(sp):
                for u in range(2):
                    sp.dma_start(a[:, u, :], adj[u * P:(u + 1) * P, :]).then_inc(loaded[u], 16)
                sp.dma_start(w[:, :, 0:D], W_seq.rearrange("(k p) n -> p k n", p=P)).then_inc(w_in, 16)
                sp.dma_start(a_rows[:, 0, :], a1.rearrange("(a d) -> a d", a=1).to_broadcast([P, DH])).then_inc(w_in, 16)
                sp.dma_start(a_rows[:, 1, :], a2.rearrange("(a d) -> a d", a=1).to_broadcast([P, DH])).then_inc(w_in, 16)
                with sp.Fori(1, NT // 2) as i:
                    for u in range(2):
                        sp.wait_ge(cast, 2 * i + u - 1)
                        sp.sem_inc(passed, 1)
                        sp.dma_start(a[:, u, :], adj[bass.ds((2 * i + u) * P, P), :]).then_inc(loaded[u], 16)
                for q in range(4):
                    sp.dma_start(x_sb[:, 4 * q:4 * q + 4, :],
                                 x[512 * q:512 * q + 512, :].rearrange("(t p) d -> p t d", p=P)).then_inc(x_in[q], 16)

            @block.gpsimd
            def _(pool):
                pool.wait_ge(w_in, 48)
                ch = Chain(pool, halved)
                for m in range(2):
                    for j in range(KD):
                        ch.link(pool.tensor_tensor(prod[:, j], w[:, j, 0:D].rearrange("p (h d) -> p h d", d=DH),
                                                   a_rows[:, m:m + 1, :].to_broadcast([P, H, DH]), ALU.mult))
                    width = DH // 2
                    while width > 1:
                        ch.link(pool.tensor_tensor(prod[:, :, :, 0:width], prod[:, :, :, 0:width],
                                                   prod[:, :, :, width:2 * width], ALU.add))
                        width //= 2
                    ch.link(pool.tensor_tensor(w[:, :, D + m * H:D + (m + 1) * H], prod[:, :, :, 0], prod[:, :, :, 1], ALU.add))
                pool.sem_inc(w_full, 1)

            @block.scalar
            def _(act):
                def cast_rows(t, u, fills):
                    act.wait_ge(loaded[u], 16 * fills)
                    act.wait_ge(turned, START + t - 1)
                    act.activation(ab[:, u, :], a[:, u, :], ACT.Copy, accum_out=rowsum[:, bass.ds(t, 1)]).then_inc(cast, 1)

                def step(t, u, at, left):
                    if left > 1:
                        cast_rows(t + 1, (u + 1) % 2, at(2) + (u + 1) // 2 + 1)
                act.wait_ge(loaded[0], 16)
                act.activation(ab[:, 0, :], a[:, 0, :], ACT.Copy, accum_out=rowsum[:, 0:1]).then_inc(cast, 1)
                rounds(act, NT, 2, step)
                act.wait_ge(w_full, 1)
                act.copy(w_hi[:], w[:]).then_inc(w_high, 1)

            @block.vector
            def _(dve):
                dve.sem_inc(kept, START)

                def step(t, u, at, left):
                    dve.wait_ge(turned, START + t + 1)
                    dve.tensor_copy(adjT[:, :, bass.ds(t * P, P)], turned_ps[u][:]).then_inc(kept, 1)
                rounds(dve, NT, 2, step)
                dve.wait_ge(cast, NT)
                dve.tensor_scalar(isolated[:], rowsum[:], 0.0, None, ALU.is_equal).then_inc(ended, 1)
                dve.wait_ge(turned, START + NT)
                dve.tensor_copy(colsum[:], col_ps[:]).then_inc(ended, 1)
                dve.wait_ge(w_high, 1)
                dve.tensor_tensor(w_lo[:], w[:], w_hi[:], ALU.subtract).then_inc(w_split, 1)
                for n in range(NT):
                    if n % 4 == 0:
                        dve.wait_ge(x_in[n // 4], 16)
                    dve.bn_stats(bn[:, n, :], x_sb[:, n, :]).then_inc(stats, 1)

            @block.tensor
            def _(pe):
                pe.sem_inc(turned, START)

                def step(t, u, at, left):
                    pe.wait_ge(cast, t + 1)
                    pe.wait_ge(kept, START + t - 1)
                    for j in range(NT):
                        pe.transpose(turned_ps[u][:, j, :], ab[:, u, j * P:(j + 1) * P], k.identb[:])
                    for j in range(NT):
                        mm = pe.matmul(col_ps[:, j:j + 1], ab[:, u, j * P:(j + 1) * P], k.ones[:, 0:1], start=False,
                                       stop=False, skip_group_check=True)
                    mm.then_inc(turned, 1)
                pe.matmul(col_ps[:], k.zerob[:], k.zerob[:, 0:NT], start=True, stop=False, skip_group_check=True)
                rounds(pe, NT, 2, step)


def softmax_factors(nc, k, s1, s2, ea, eb, g, ns2, big_s2, s1_rows, rowsum, colsum, dinv):
    with ExitStack() as st:
        c = Ctx(nc, st, "factor")
        top = c.sb("top", [P, H])
        m = c.sb("m", [P, H])
        dif = c.sb("dif", [P, NT, H])
        pos = c.sb("pos", [P, NT, H])
        s1T = c.sb("s1T", [H, N])
        deg, some, root, t = (c.sb(n, [P, NT]) for n in ("deg", "some", "root", "t"))
        s1T_ps = c.ps("s1T_ps", [H, NT, P])
        topped, maxed, difs, turned, kept, wrote = (c.sem(x) for x in ("topped", "maxed", "difs", "turned", "kept", "wrote"))
        ch_s, exps, deg_ready, rooted = c.sem("chain"), c.sem("exps"), c.sem("deg_ready"), c.sem("rooted")
        with nc.Block() as block:
            @block.vector
            def _(dve):
                dve.tensor_reduce(top[:], s2[:].rearrange("p t h -> p h t"), AX.X, ALU.max).then_inc(topped, 1)
                dve.tensor_scalar(ns2[:], s2[:], -1.0, None, ALU.mult).then_inc(ch_s, 1)
                dve.tensor_scalar(big_s2[:], s2[:], BIG, None, ALU.mult).then_inc(ch_s, 1)
                dve.wait_ge(maxed, 1)
                mrow = m[:].rearrange("p (a h) -> p a h", a=1).to_broadcast([P, NT, H])
                dve.tensor_tensor(dif[:], s2[:], mrow, ALU.subtract).then_inc(difs, 1)
                ch = Chain(dve, ch_s)
                ch.n = 2
                dve.wait_ge(ch_s, 2)
                ch.link(dve.tensor_tensor(pos[:], s1[:], mrow, ALU.add))
                dve.tensor_scalar(pos[:], pos[:], 0.0, None, ALU.max).then_inc(difs, 1)
                dve.wait_ge(turned, 1)
                dve.tensor_copy(s1T[:], s1T_ps[:].rearrange("h t p -> h (t p)")).then_inc(kept, 1)
                ch.link(dve.tensor_tensor(deg[:], rowsum[:], colsum[:], ALU.add))
                ch.link(dve.tensor_scalar(deg[:], deg[:], 0.5, 1.0, ALU.mult, ALU.add))
                ch.link(dve.tensor_scalar(some[:], deg[:], 0.0, None, ALU.is_gt))
                dve.tensor_scalar(deg[:], deg[:], 1e-30, None, ALU.max).then_inc(deg_ready, 1)
                dve.wait_ge(rooted, 1)
                ch.link(dve.reciprocal(dinv[:], root[:]))
                ch.link(dve.tensor_tensor(t[:], dinv[:], dinv[:], ALU.mult))
                ch.link(dve.tensor_tensor(t[:], t[:], deg[:], ALU.mult))
                ch.link(dve.tensor_scalar(t[:], t[:], -0.5, 1.5, ALU.mult, ALU.add))
                ch.link(dve.tensor_tensor(dinv[:], dinv[:], t[:], ALU.mult))
                dve.tensor_tensor(dinv[:], dinv[:], some[:], ALU.mult).then_inc(ch_s, 1)

            @block.gpsimd
            def _(pool):
                pool.wait_ge(topped, 1)
                pool.partition_all_reduce(m[:], top[:], P, RMAX).then_inc(maxed, 1)

            @block.scalar
            def _(act):
                act.wait_ge(difs, 1)
                act.activation(ea[:], dif[:], ACT.Exp).then_inc(exps, 1)
                act.activation(eb[:], dif[:], ACT.Exp, scale=SLOPE).then_inc(exps, 1)
                act.wait_ge(difs, 2)
                act.activation(g[:], pos[:], ACT.Exp, scale=-(1.0 - SLOPE)).then_inc(exps, 1)
                act.wait_ge(deg_ready, 1)
                act.activation(root[:], deg[:], ACT.Sqrt).then_inc(rooted, 1)

            @block.tensor
            def _(pe):
                for n in range(NT):
                    mm = pe.transpose(s1T_ps[:, n, :], s1[:, n, :], k.ident[:])
                mm.then_inc(turned, 1)

            @block.sync
            def _(sp):
                sp.wait_ge(kept, 1)
                sp.dma_start(s1_rows, s1T[:]).then_inc(wrote, 16)
                sp.wait_ge(wrote, 16)


def attention(nc, k, adjT, seq, ea, eb, g, ns2, big_s2, s1_rows, tables):
    HB = NT // 2
    HW = N // 2
    C1 = DH + 1
    UNITS = 2 * H
    STEPPED = [j for j in range(NT) if j % 4]
    RD = 4
    with ExitStack() as st:
        c = Ctx(nc, st, "attn")
        s1_row = c.sb("s1_row", [P, 2, N])
        mask = c.sb("mask", [P, NT, HW], BF16)
        step = c.sb("step", [P, RD, HW], BF16)
        vals = c.sb("vals", [P, NT, 2 * C1])
        rest = c.sb("rest", [P, NT, 2 * C1])
        m_parts = c.sb("m_parts", [P, 2, NT, 3, 2 * C1], BF16)
        a_parts = c.sb("a_parts", [P, 2, NT, 3, C1], BF16)
        sums = c.sb("sums", [P, HB, 2 * C1])
        num = c.sb("num", [P, HB, C1])
        inv = c.sb("inv", [P, HB, 1])
        acc = [c.ps(f"acc{u}", [P, HB, 256]) for u in range(2)]
        rows_in = [c.sem(f"rows_in{u}") for u in range(2)]
        stepped, masked = c.sem("stepped"), c.sem("masked")
        mask_used, acc_free = c.sem("mask_used"), c.sem("acc_free")
        parts_ready, ch_p, ch_v, ch_first = (c.sem(n) for n in ("parts_ready", "pool_chain", "dve_chain", "first_chain"))
        cleared = c.sem("cleared")
        passed_a, passed_p, passed_s = c.sem("passed_act"), c.sem("passed_pool"), c.sem("passed_sp")

        LINKS = 10

        def prepare(ch, h, b):
            v = vals[:].rearrange("p t (w c) -> p t w c", w=2)
            for w, e in ((0, ea), (1, eb)):
                f = e[:, :, bass.ds(h, 1)]
                ch.eng.tensor_tensor(v[:, :, w, 0:DH], seq[:, :, bass.ds(h * DH, DH)],
                                     f.to_broadcast([P, NT, DH]), ALU.mult).then_inc(ch.sem, 1)
                ch.eng.tensor_copy(v[:, :, w, DH:C1], f).then_inc(ch.sem, 1)
            ch.n += 4
            ch.hold()
            mp = m_parts[:, b]
            ch.link(ch.eng.tensor_copy(mp[:, :, 0, :], vals[:]))
            ch.link(ch.eng.tensor_tensor(rest[:], vals[:], mp[:, :, 0, :], ALU.subtract))
            ch.link(ch.eng.tensor_copy(mp[:, :, 1, :], rest[:]))
            ch.link(ch.eng.tensor_tensor(mp[:, :, 2, :], rest[:], mp[:, :, 1, :], ALU.subtract))
            ch.link(ch.eng.tensor_copy(a_parts[:, b], mp[:, :, :, C1:2 * C1]))
            ch.link(ch.eng.tensor_scalar(mp[:, :, :, C1:2 * C1], a_parts[:, b], -1.0, None, ALU.mult))

        with nc.Block() as block:
            @block.sync
            def _(sp):
                for u in range(2):
                    sp.dma_start(s1_row[:, u, :], s1_rows[u:u + 1, :].to_broadcast([P, N])).then_inc(rows_in[u], 16)
                for table in tables:
                    sp.dma_start(table.rearrange("(b p) d -> p b d", p=P),
                                 k.zeros[:].rearrange("p (a d) -> p a d", a=1).to_broadcast([P, table.shape[0] // P, D])
                                 ).then_inc(cleared, 16)
                with sp.Fori(1, H // 2) as i:
                    for u in range(2):
                        sp.wait_ge(masked, NT + (2 * i + u - 1) * 2 * NT)
                        sp.sem_inc(passed_s, 1)
                        sp.wait_ge(stepped, (2 * i + u - 1) * 2 * len(STEPPED))
                        sp.sem_inc(passed_s, 1)
                        sp.dma_start(s1_row[:, u, :], s1_rows[bass.ds(2 * i + u, 1), :].to_broadcast([P, N])).then_inc(rows_in[u], 16)
                sp.wait_ge(cleared, 16 * len(tables))

            @block.scalar
            def _(act):
                with act.Fori(0, H // 2) as i:
                    for v in range(4):
                        u, half, n, h = v // 2, v % 2, 4 * i + v, 2 * i + v // 2
                        act.wait_ge(rows_in[u], 16 * (i + 1))
                        for j in range(NT):
                            if j not in STEPPED:
                                continue
                            src = s1_row[:, u, half * HW:(half + 1) * HW]
                            q = STEPPED.index(j)
                            before = STEPPED[q - RD] + (0 if q >= RD else -NT)
                            act.wait_ge(masked, NT + n * NT + before + 1)
                            act.sem_inc(passed_a, 1)
                            act.activation(step[:, q % RD, :], src, ACT.Sigmoid, bias=big_s2[:, j, bass.ds(h, 1)],
                                           scale=BIG).then_inc(stepped, 1)

            @block.gpsimd
            def _(pool):
                ch = Chain(pool, ch_p, passed_p)
                pool.wait_ge(parts_ready, 1)


                def head(h, u):
                    pool.wait_ge(mask_used, NT + 2 * NT * h)
                    pool.sem_inc(passed_p, 1)
                    prepare(ch, h + 1, 1 - u)
                    pool.sem_inc(parts_ready, 1)

                with pool.Fori(0, H // 2 - 1) as i:
                    ch.loop(i, 2 * LINKS)
                    head(2 * i, 0)
                    head(2 * i + 1, 1)
                assert ch.n == 2 * LINKS
                ch.off = (H // 2 - 2) * 2 * LINKS
                head(H - 2, 0)

            @block.vector
            def _(dve):
                ch = Chain(dve, ch_v)

                def masks(i, v, js):
                    u, half, n, h = (v % 4) // 2, v % 2, 4 * i + v, 2 * i + v // 2
                    if js[0] == 0:
                        dve.wait_ge(rows_in[u], 16 * (i + 1 + v // 4))
                    for j in js:
                        dve.wait_ge(mask_used, n * NT + j + 1)
                        at = adjT[:, j, half * HW:(half + 1) * HW]
                        if j not in STEPPED:
                            dve.scalar_tensor_tensor(out=mask[:, j, :], in0=s1_row[:, u, half * HW:(half + 1) * HW],
                                                     scalar=ns2[:, j, bass.ds(h, 1)], in1=at, op0=ALU.is_gt,
                                                     op1=ALU.mult).then_inc(masked, 1)
                        else:
                            q = STEPPED.index(j)
                            dve.wait_ge(stepped, n * len(STEPPED) + q + 1)
                            dve.tensor_tensor(mask[:, j, :], step[:, q % RD, :], at, ALU.mult).then_inc(masked, 1)

                def combine(i, v):
                    half, n, h = v % 2, 4 * i + v, 2 * i + v // 2
                    dve.wait_ge(mask_used, NT + (n + 1) * NT)
                    dve.tensor_reduce(sums[:], acc[v % 2][:, :, 0:6 * C1].rearrange("p b (s c) -> p b c s", s=3),
                                      AX.X, ALU.add).then_inc(acc_free, 1)
                    dve.wait_ge(acc_free, n + 3)
                    gh = g[:, half * HB:(half + 1) * HB, bass.ds(h, 1)]
                    ch.link(dve.tensor_tensor(num[:], sums[:, :, C1:2 * C1], gh.to_broadcast([P, HB, C1]), ALU.mult))
                    ch.link(dve.tensor_tensor(num[:], num[:], sums[:, :, 0:C1], ALU.add))
                    ch.link(dve.reciprocal(inv[:], num[:, :, DH:C1]))
                    ch.link(dve.tensor_tensor(seq[:, half * HB:(half + 1) * HB, bass.ds(h * DH, DH)], num[:, :, 0:DH],
                                              inv[:].to_broadcast([P, HB, DH]), ALU.mult))

                prepare(Chain(dve, ch_first), 0, 0)
                dve.sem_inc(parts_ready, 1)
                EARLY = 12
                masks(0, 0, range(0, EARLY))

                def round_(i, last):
                    for v in range(4):
                        masks(i, v, range(EARLY, NT))
                        if not (last and v == 3):
                            masks(i, v + 1, range(0, EARLY))
                        combine(i, v)

                with dve.Fori(0, H // 2 - 1) as i:
                    ch.loop(i, 16)
                    round_(i, False)
                ch.off = (H // 2 - 2) * 16
                round_(H // 2 - 1, True)

            @block.tensor
            def _(pe):
                pe.sem_inc(masked, NT)
                pe.sem_inc(mask_used, NT)
                pe.sem_inc(acc_free, 2)
                with pe.Fori(0, H // 2) as i:
                    for v in range(4):
                        u, half, n, h = v // 2, v % 2, 4 * i + v, 2 * i + v // 2
                        pe.wait_ge(acc_free, n + 1)
                        pe.wait_ge(parts_ready, h + 1)
                        for j in range(NT):
                            pe.wait_ge(masked, NT + n * NT + j + 1)
                            for b in range(HB):
                                o = acc[v % 2][:, b, 0:6 * C1]
                                pe.matmul(o, mask[:, j, b * P:(b + 1) * P], m_parts[:, u, j].rearrange("p s c -> p (s c)"),
                                          start=(j == 0 and b % 2 == 0), stop=(j == NT - 1), skip_group_check=True)
                                mm = pe.matmul(o.rearrange("p (s c) -> p s c", s=3)[:, :, C1:2 * C1],
                                               adjT[:, j, half * HW + b * P:half * HW + (b + 1) * P], a_parts[:, u, j],
                                               start=False, stop=(j == NT - 1), skip_group_check=True)
                            mm.then_inc(mask_used, 1)


class Constants:
    pass


def make_constants(nc, c):
    k = Constants()
    k.ident = c.sb("ident", [P, P])
    k.identb = c.sb("identb", [P, P], BF16)
    k.before = c.sb("before", [P, P], BF16)
    k.ones = c.sb("ones", [P, P], BF16)
    k.zerob = c.sb("zerob", [P, P], BF16)
    k.zeros = c.sb("zeros", [P, D])
    k.expert_id = c.sb("expert_id", [P, E])
    k.block_start = c.sb("block_start", [P, N // BR])
    k.block_id = c.sb("block_id", [P, NB0])
    return k


def project_out(nc, k, hid, x_dram, W_out, b_out, x_sb, bn):
    with ExitStack() as st:
        c = Ctx(nc, st, "outp")
        w = c.sb("w", [P, KD, D])
        w_hi = c.sb("w_hi", [P, KD, D], F32R)
        w_lo = c.sb("w_lo", [P, KD, D], F32R)
        bias = c.sb("bias", [P, D])
        hi = [c.sb(f"hi{u}", [P, KD, P], F32R) for u in range(2)]
        lo = [c.sb(f"lo{u}", [P, KD, P], F32R) for u in range(2)]
        tile = c.sb("tile", [P, 2, D])
        z = c.sb("z", [P, 2, D])
        neg = c.sb("neg", [P, 2, D])
        e = c.sb("e", [P, 2, D])
        xT = [c.ps(f"xT{u}", [P, KD, P]) for u in range(2)]
        out = [c.ps(f"out{u}", [P, D]) for u in range(2)]
        loaded, x_in, w_split, w_high = c.sem("loaded"), c.sem("x_in"), c.sem("w_split"), c.sem("w_high")
        passed, stats = c.sem("passed"), c.sem("stats")
        turned, high, low, summed = c.sem("turned"), c.sem("high"), c.sem("low"), c.sem("summed")
        staged, biased, negated, exped, added = c.sem("staged"), c.sem("biased"), c.sem("negated"), c.sem("exped"), c.sem("added")
        with nc.Block() as block:
            @block.sync
            def _(sp):
                sp.dma_start(w[:], W_out.rearrange("(k p) n -> p k n", p=P)).then_inc(loaded, 16)
                sp.dma_start(bias[:], b_out.rearrange("(a d) -> a d", a=1).to_broadcast([P, D])).then_inc(loaded, 16)
                for q in range(4):
                    sp.dma_start(x_sb[:, 4 * q:4 * q + 4, :],
                                 x_dram[512 * q:512 * q + 512, :].rearrange("(t p) d -> p t d", p=P)).then_inc(x_in, 16)

            @block.gpsimd
            def _(pool):
                def step(t, u, at, left):
                    pool.wait_ge(turned, START + t - 1)
                    pool.sem_inc(passed, 1)
                    pool.tensor_copy(tile[:, u, :], hid[:, t, :]).then_inc(staged, 1)
                for t in range(2):
                    pool.tensor_copy(tile[:, t, :], hid[:, t, :]).then_inc(staged, 1)
                with pool.Fori(1, NT // 2) as i:
                    for u in range(2):
                        step(2 * i + u, u, None, None)

            @block.scalar
            def _(act):
                act.wait_ge(loaded, 32)
                act.copy(w_hi[:], w[:]).then_inc(w_high, 1)

                def high_part(t, u):
                    act.wait_ge(turned, START + t + 1)
                    act.wait_ge(summed, START + t - 1)
                    act.copy(hi[u][:], xT[u][:]).then_inc(high, 1)

                def step(t, u, at, left):
                    if left > 1:
                        high_part(t + 1, (u + 1) % 2)
                    act.wait_ge(negated, t + 1)
                    act.activation(e[:, u, :], neg[:, u, :], ACT.Exp).then_inc(exped, 1)
                act.wait_ge(turned, START + 1)
                act.copy(hi[0][:], xT[0][:]).then_inc(high, 1)
                rounds(act, NT, 2, step)

            @block.vector
            def _(dve):
                dve.wait_ge(w_high, 1)
                dve.tensor_tensor(w_lo[:], w[:], w_hi[:], ALU.subtract).then_inc(w_split, 1)
                dve.sem_inc(biased, START)
                dve.sem_inc(added, START)

                def low_part(t, u):
                    dve.wait_ge(high, t + 1)
                    dve.tensor_tensor(lo[u][:], xT[u][:], hi[u][:], ALU.subtract).then_inc(low, 1)

                def bias_add(t, u):
                    dve.wait_ge(summed, START + t + 1)
                    dve.wait_ge(added, START + 2 * t - 2)
                    dve.tensor_tensor(z[:, u, :], out[u][:], bias[:], ALU.add).then_inc(biased, 1)
                    dve.wait_ge(biased, START + t + 1)
                    dve.tensor_scalar(neg[:, u, :], z[:, u, :], 0.0, None, ALU.min).then_inc(negated, 1)

                def step(t, u, at, left):
                    if left > 2:
                        low_part(t + 2, u)
                    if left > 1:
                        bias_add(t + 1, (u + 1) % 2)
                    x_t = x_sb[:, t, :]
                    dve.wait_ge(exped, t + 1)
                    dve.scalar_tensor_tensor(out=e[:, u, :], in0=e[:, u, :], scalar=-1.0, in1=x_t,
                                             op0=ALU.add, op1=ALU.add).then_inc(added, 1)
                    dve.wait_ge(added, START + 2 * t + 1)
                    dve.scalar_tensor_tensor(out=x_t, in0=z[:, u, :], scalar=0.0, in1=e[:, u, :],
                                             op0=ALU.max, op1=ALU.add).then_inc(added, 1)
                    dve.wait_ge(added, START + 2 * t + 2)
                    dve.bn_stats(bn[:, t, :], x_t).then_inc(stats, 1)
                low_part(0, 0)
                low_part(1, 1)
                dve.wait_ge(summed, START + 1)
                dve.tensor_tensor(z[:, 0, :], out[0][:], bias[:], ALU.add).then_inc(biased, 1)
                dve.wait_ge(biased, START + 1)
                dve.tensor_scalar(neg[:, 0, :], z[:, 0, :], 0.0, None, ALU.min).then_inc(negated, 1)
                dve.wait_ge(x_in, 64)
                rounds(dve, NT, 2, step)

            @block.tensor
            def _(pe):
                pe.sem_inc(turned, START)
                pe.sem_inc(summed, START)

                def turn(t, u):
                    pe.wait_ge(staged, t + 1)
                    for j in range(KD):
                        mm = pe.transpose(xT[u][:, j, :], tile[:, u, j * P:(j + 1) * P], k.ident[:])
                    mm.then_inc(turned, 1)

                def step(t, u, at, left):
                    if left > 1:
                        turn(t + 1, (u + 1) % 2)
                    pe.wait_ge(low, t + 1)
                    pe.wait_ge(biased, START + t - 1)
                    three_pass(pe, out[u][:], [(hi[u][:, j, :], lo[u][:, j, :], w_hi[:, j, :], w_lo[:, j, :])
                                               for j in range(KD)]).then_inc(summed, 1)
                turn(0, 0)
                pe.wait_ge(w_split, 1)
                rounds(pe, NT, 2, step)


def route(nc, k, tag, x_sb, mean, rstd, W_r, b_r, xn, put_at, get_from, weight, block_expert):
    capped = block_expert is None
    R = 4
    with ExitStack() as st:
        c = Ctx(nc, st, tag)
        w = c.sb("w", [P, KD, E])
        bias = c.sb("bias", [P, E])
        xT = [c.sb(f"xT{u}", [P, KD, P]) for u in range(2)]
        tile = c.sb("tile", [P, R, D])
        logits = c.sb("logits", [P, NT, E])
        best = c.sb("best", [P, NT, 8])
        best_id = c.sb("best_id", [P, NT, 8], U32)
        chosen = c.sb("chosen", [P, NT, TOPK])
        hot = [c.sb(f"hot{q}", [P, NT, E]) for q in range(TOPK)]
        sel = c.sb("sel", [P, NT, E], BF16)
        gap = c.sb("gap", [P, NT])
        tail = c.sb("tail", [P, NT])
        before_tile = c.sb("before_tile", [P, NT + 1, E])
        pos = c.sb("pos", [P, NT, E])
        keep = c.sb("keep", [P, NT, E])
        cmp = c.sb("cmp", [P, E, N // BR])
        blocks = c.sb("blocks", [P, E])
        ends = c.sb("ends", [P, E + 1])
        cmpb = c.sb("cmpb", [P, NB0, E])
        blk = c.sb("blk", [P, NB0])
        t = [c.sb(f"t{q}", [P, NT, E]) for q in range(TOPK)]
        slot = c.sb("slot", [P, TOPK, NT])
        kept = c.sb("kept", [P, TOPK, NT])
        far = c.sb("far", [P, TOPK, NT])
        xT_ps = [c.ps(f"xT_ps{u}", [P, KD, P]) for u in range(2)]
        lg_ps = c.ps("lg_ps", [P, NT, E])
        rank_ps = c.ps("rank_ps", [P, NT, E])
        total_ps = c.ps("total_ps", [P, NT, E])
        loaded, normed, turned, copied, scored = (c.sem(x) for x in ("loaded", "normed", "turned", "copied", "scored"))
        chosen_s, ranked, gapped, exped, ch_s = (c.sem(x) for x in ("chosen", "ranked", "gapped", "exped", "chain"))
        kept_xn = c.sem("kept_xn")
        with nc.Block() as block:
            @block.sync
            def _(sp):
                sp.dma_start(w[:], W_r.rearrange("(k p) e -> p k e", p=P)).then_inc(loaded, 16)
                if b_r is not None:
                    sp.dma_start(bias[:], b_r.rearrange("(a d) -> a d", a=1).to_broadcast([P, E])).then_inc(loaded, 16)

            @block.scalar
            def _(act):
                with act.Fori(0, NT // R) as i:
                    for v in range(R):
                        act.wait_ge(normed, R * i + v + 1)
                        act.copy(xn[:, R * i + v, :], tile[:, v, :]).then_inc(kept_xn, 1)
                        act.wait_ge(scored, START + R * i + v // 2 * 2)
                        act.wait_ge(turned, START + R * i + v + 1)
                        act.copy(xT[v % 2][:], xT_ps[v % 2][:]).then_inc(copied, 1)
                act.wait_ge(gapped, 1)
                act.activation(tail[:], gap[:], ACT.Exp).then_inc(exped, 1)

            @block.tensor
            def _(pe):
                pe.sem_inc(turned, START)
                pe.sem_inc(scored, START)
                pe.sem_inc(copied, START)
                pe.wait_ge(loaded, 16 if b_r is None else 32)

                def turn(i, v):
                    pe.wait_ge(normed, R * i + v + 1)
                    pe.wait_ge(copied, START + R * i + v // 2 * 2)
                    for j in range(KD):
                        mm = pe.transpose(xT_ps[v % 2][:, j, :], tile[:, v, j * P:(j + 1) * P], k.ident[:])
                    mm.then_inc(turned, 1)

                def score(i, v):
                    pe.wait_ge(copied, START + R * i + v + 1)
                    for j in range(KD):
                        mm = pe.matmul(lg_ps[:, R * i + v, :], xT[v % 2][:, j, :], w[:, j, :], start=(j == 0), stop=(j == KD - 1))
                    mm.then_inc(scored, 1)
                with pe.Fori(0, NT // R) as i:
                    for v in range(0, R, 2):
                        turn(i, v)
                        turn(i, v + 1)
                        score(i, v)
                        score(i, v + 1)
                pe.wait_ge(chosen_s, 1)
                pe.matmul(rank_ps[:], k.before[:], sel[:], start=True, stop=True)
                pe.matmul(total_ps[:], k.ones[:], sel[:], start=True, stop=True).then_inc(ranked, 1)

            @block.vector
            def _(dve):
                dve.sem_inc(kept_xn, R)
                with dve.Fori(0, NT // R) as i:
                    for v in range(R):
                        dve.wait_ge(turned, START + R * i + max(v - R + 1, 1 - START))
                        dve.wait_ge(kept_xn, R * i + v + 1)
                        dve.tensor_scalar(tile[:, v, :], x_sb[:, R * i + v, :], mean[:, bass.ds(R * i + v, 1)],
                                          rstd[:, bass.ds(R * i + v, 1)], ALU.subtract, ALU.mult).then_inc(normed, 1)
                ch = Chain(dve, ch_s)
                dve.wait_ge(scored, START + NT)
                if b_r is None:
                    ch.link(dve.tensor_copy(logits[:], lg_ps[:]))
                else:
                    ch.link(dve.tensor_tensor(logits[:], lg_ps[:], bias[:].rearrange("p (a e) -> p a e", a=1)
                                              .to_broadcast([P, NT, E]), ALU.add))
                for n in range(NT):
                    dve.max(best[:, n, :], logits[:, n, :]).then_inc(ch_s, 1)
                ch.n += NT
                dve.wait_ge(ch_s, ch.n)
                for n in range(NT):
                    dve.max_index(best_id[:, n, :], best[:, n, :], logits[:, n, :]).then_inc(ch_s, 1)
                ch.n += NT
                dve.wait_ge(ch_s, ch.n)
                ch.link(dve.tensor_copy(chosen[:], best_id[:, :, 0:TOPK]))
                ids = k.expert_id[:].rearrange("p (a e) -> p a e", a=1).to_broadcast([P, NT, E])
                for q in range(TOPK):
                    ch.link(dve.tensor_tensor(hot[q][:], ids, chosen[:, :, q:q + 1].to_broadcast([P, NT, E]), ALU.is_equal))
                dve.tensor_tensor(sel[:], hot[0][:], hot[1][:], ALU.add).then_inc(chosen_s, 1)
                dve.tensor_tensor(gap[:], best[:, :, 1], best[:, :, 0], ALU.subtract).then_inc(gapped, 1)
                dve.wait_ge(exped, 1)
                ch.link(dve.tensor_scalar(gap[:], tail[:], 1.0, None, ALU.add))
                ch.link(dve.reciprocal(weight[:, 0, :], gap[:]))
                ch.link(dve.tensor_tensor(weight[:, 1, :], weight[:, 0, :], tail[:], ALU.mult))
                dve.wait_ge(ranked, 1)
                ch.link(dve.memset(before_tile[:, 0, :], 0.0))
                for n in range(NT):
                    ch.link(dve.tensor_tensor(before_tile[:, n + 1, :], before_tile[:, n, :], total_ps[:, n, :], ALU.add))
                ch.link(dve.tensor_tensor(pos[:], rank_ps[:], before_tile[:, 0:NT, :], ALU.add))
                if capped:
                    ch.link(dve.tensor_scalar(keep[:], pos[:], float(CAP), None, ALU.is_lt))
                    ch.link(dve.tensor_scalar(ends[:, 0:E], k.expert_id[:], float(CAP), None, ALU.mult))
                else:
                    ch.link(dve.tensor_tensor(cmp[:], before_tile[:, NT:NT + 1, :].rearrange("p a e -> p e a").to_broadcast([P, E, N // BR]),
                                              k.block_start[:].rearrange("p (a t) -> p a t", a=1).to_broadcast([P, E, N // BR]), ALU.is_gt))
                    ch.link(dve.tensor_reduce(blocks[:], cmp[:], AX.X, ALU.add))
                    ch.link(dve.memset(ends[:, 0:1], 0.0))
                    for e in range(E):
                        ch.link(dve.tensor_tensor(ends[:, e + 1:e + 2], ends[:, e:e + 1], blocks[:, e:e + 1], ALU.add))
                    ch.link(dve.tensor_tensor(cmpb[:], ends[:, 1:E + 1].rearrange("p (a e) -> p a e", a=1).to_broadcast([P, NB0, E]),
                                              k.block_id[:].rearrange("p (b a) -> p b a", a=1).to_broadcast([P, NB0, E]), ALU.is_le))
                    ch.link(dve.tensor_reduce(blk[:], cmpb[:], AX.X, ALU.add))
                    ch.link(dve.tensor_scalar(block_expert[:], blk[:], float(E - 1), None, ALU.min))
                    ch.link(dve.tensor_scalar(ends[:], ends[:], float(BR), None, ALU.mult))
                ch.link(dve.tensor_tensor(pos[:], pos[:], ends[:, 0:E].rearrange("p (a e) -> p a e", a=1)
                                          .to_broadcast([P, NT, E]), ALU.add))
                for q in range(TOPK):
                    ch.link(dve.tensor_tensor(t[q][:], hot[q][:], pos[:], ALU.mult))
                    ch.link(dve.tensor_reduce(slot[:, q, :], t[q][:], AX.X, ALU.add))
                if capped:
                    for q in range(TOPK):
                        ch.link(dve.tensor_tensor(t[q][:], hot[q][:], keep[:], ALU.mult))
                        ch.link(dve.tensor_reduce(kept[:, q, :], t[q][:], AX.X, ALU.add))
                    ch.link(dve.tensor_tensor(weight[:], weight[:], kept[:], ALU.mult))
                    ch.link(dve.tensor_tensor(slot[:], slot[:], kept[:], ALU.mult))
                    ch.link(dve.tensor_copy(get_from[:], slot[:]))
                    ch.link(dve.tensor_scalar(far[:], kept[:], -FAR, FAR, ALU.mult, ALU.add))
                    ch.link(dve.tensor_tensor(far[:], far[:], slot[:], ALU.add))
                    ch.link(dve.tensor_copy(put_at[:], far[:]))
                else:
                    ch.link(dve.tensor_copy(get_from[:], slot[:]))
                    ch.link(dve.tensor_copy(put_at[:], slot[:]))


def dispatch(nc, tag, xn, put_at, table, rows, x_sb=None, spill=None):
    with ExitStack() as st:
        c = Ctx(nc, st, tag)
        put, stored = c.sem("put"), c.sem("stored")
        with nc.Block() as block:
            if spill is not None:
                @block.sync
                def _(sp):
                    for q in range(4):
                        sp.dma_start(spill[512 * q:512 * q + 512, :].rearrange("(t p) d -> p t d", p=P),
                                     x_sb[:, 4 * q:4 * q + 4, :]).then_inc(stored, 16)
                    sp.wait_ge(stored, 64)

            @block.gpsimd
            def _(pool):
                for n in range(NT):
                    for q in range(TOPK):
                        pool.indirect_dma_start(out=table, out_offset=bass.IndirectOffsetOnAxis(ap=put_at[:, q, n:n + 1], axis=0),
                                                in_=xn[:, n, :], in_offset=None, bounds_check=rows - 1,
                                                oob_is_err=False).then_inc(put, 16)
                pool.wait_ge(put, 16 * NT * TOPK)


def gather_experts(nc, tag, table, get_from, weight, x_sb, bn=None, out=None, x_from=None):
    with ExitStack() as st:
        c = Ctx(nc, st, tag)
        R = 8
        y = c.sb("y", [P, R, D])
        got = [c.sem(f"got{r}") for r in range(R)]
        added, stored, x_in, stats = (c.sem(n) for n in ("added", "stored", "x_in", "stats"))
        with nc.Block() as block:
            @block.gpsimd
            def _(pool):
                for n in range(NT * TOPK):
                    if n >= R:
                        pool.wait_ge(added, n - R + 1)
                    pool.indirect_dma_start(out=y[:, n % R, :], out_offset=None, in_=table,
                                            in_offset=bass.IndirectOffsetOnAxis(ap=get_from[:, n % TOPK, n // TOPK:n // TOPK + 1], axis=0)
                                            ).then_inc(got[n % R], 16)

            @block.vector
            def _(dve):
                if x_from is not None:
                    dve.wait_ge(x_in, 64)
                for n in range(NT * TOPK):
                    tile, q = n // TOPK, n % TOPK
                    dve.wait_ge(got[n % R], 16 * (n // R + 1))
                    if n:
                        dve.wait_ge(added, n)
                    dve.scalar_tensor_tensor(out=x_sb[:, tile, :], in0=y[:, n % R, :], scalar=weight[:, q, tile:tile + 1],
                                             in1=x_sb[:, tile, :], op0=ALU.mult, op1=ALU.add).then_inc(added, 1)
                    if bn is not None and q == TOPK - 1:
                        dve.wait_ge(added, n + 1)
                        dve.bn_stats(bn[:, tile, :], x_sb[:, tile, :]).then_inc(stats, 1)

            if out is not None:
                @block.sync
                def _(sp):
                    for q in range(4):
                        sp.dma_start(x_sb[:, 4 * q:4 * q + 4, :],
                                     x_from[512 * q:512 * q + 512, :].rearrange("(t p) d -> p t d", p=P)).then_inc(x_in, 16)
                    for q in range(4):
                        sp.wait_ge(added, 8 * q + 8)
                        sp.dma_start(out[512 * q:512 * q + 512, :].rearrange("(t p) d -> p t d", p=P),
                                     x_sb[:, 4 * q:4 * q + 4, :]).then_inc(stored, 16)
                    sp.wait_ge(stored, 64)


def experts_gated(nc, k, block_expert, table, w_gate, w_up, w_down, returned, spare):
    STEPS = NB0 * BR // P
    PERIOD = 4
    with ExitStack() as st:
        c = Ctx(nc, st, "moe0")
        x, y = spare[:, 0:4, :], spare[:, 4:6, :]
        wg, wu = ([c.sb(f"{n}{r}", [P, KD, I0]) for r in range(2)] for n in ("wg", "wu"))
        wd = [c.sb(f"wd{r}", [P, KI, D]) for r in range(2)]
        wg_hi, wg_lo, wu_hi, wu_lo = ([c.sb(f"{n}{r}", [P, KD, I0], F32R) for r in range(2)]
                                      for n in ("wg_hi", "wg_lo", "wu_hi", "wu_lo"))
        wd_hi, wd_lo = ([c.sb(f"{n}{r}", [P, KI, D], F32R) for r in range(2)] for n in ("wd_hi", "wd_lo"))
        x_hi, x_lo = ([c.sb(f"{n}{r}", [P, KD, P], F32R) for r in range(2)] for n in ("x_hi", "x_lo"))
        h_hi, h_lo = ([c.sb(f"{n}{r}", [P, KI, P], F32R) for r in range(2)] for n in ("h_hi", "h_lo"))
        sg = c.sb("sg", [P, 2, I0])
        h = [c.sb(f"h{u}", [P, I0]) for u in range(2)]
        xT_ps = c.ps("xT_ps", [P, KD, P])
        g_ps = [c.ps(f"g_ps{u}", [P, 512]) for u in range(2)]
        u_ps = [c.ps(f"u_ps{u}", [P, 512]) for u in range(2)]
        hT_ps = c.ps("hT_ps", [P, KI, P])
        y_ps = [c.ps(f"y_ps{u}", [P, D]) for u in range(2)]
        w_in = [c.sem(f"w_in{r}") for r in range(2)]
        x_in = [c.sem(f"x_in{r}") for r in range(2)]
        stored = [c.sem(f"stored{u}") for u in range(2)]
        w_high, w_low, turned, x_high, x_split, up, gated, hidden, h_turned, h_high, h_split, down, evac = (
            c.sem(n) for n in ("w_high", "w_low", "turned", "x_high", "x_split", "up", "gated", "hidden", "h_turned",
                               "h_high", "h_split", "down", "evac"))
        passed_s = c.sem("passed_sp")
        raws = [[wg[r], wu[r], wd[r]] for r in range(2)]
        highs = [[wg_hi[r], wu_hi[r], wd_hi[r]] for r in range(2)]
        lows = [[wg_lo[r], wu_lo[r], wd_lo[r]] for r in range(2)]
        with nc.Block() as block:
            @block.sync
            def _(sp):
                sp.sem_inc(stored[0], 16)
                sp.sem_inc(stored[1], 16)

                def load(p, r):
                    ex = sp.value_load(block_expert[0:1, bass.ds(p, 1)], min_val=0, max_val=E - 1)
                    sp.dma_start(x[:, 2 * r:2 * r + 2, :], table[bass.ds(p * BR, BR), :].rearrange("(s q) d -> q s d", q=P)).then_inc(x_in[r], 16)
                    for dst, src in zip(raws[r], (w_gate, w_up, w_down)):
                        sp.dma_start(dst[:], src[bass.ds(ex, 1), :, :].rearrange("a (k q) i -> q (a k) i", q=P)).then_inc(w_in[r], 16)

                def store(b, u):
                    sp.wait_ge(evac, b + 1)
                    sp.sem_inc(passed_s, 1)
                    sp.dma_start(returned[bass.ds(b * P, P), :], y[:, u, :]).then_inc(stored[u], 16)

                load(0, 0)
                load(1, 1)
                with sp.Fori(1, (NB0 - 1) // 2) as i:
                    for r in range(2):
                        sp.wait_ge(w_low, 3 * (2 * i + r - 1))
                        sp.sem_inc(passed_s, 1)
                        sp.wait_ge(turned, 2 * (2 * i + r - 1))
                        sp.sem_inc(passed_s, 1)
                        load(2 * i + r, r)
                        for u in range(2):
                            store(2 * (2 * i + r - 2) + u, u)
                sp.wait_ge(w_low, 3 * (NB0 - 2))
                sp.wait_ge(turned, 2 * (NB0 - 2))
                load(NB0 - 1, 0)
                for b in range(2 * (NB0 - 3), STEPS):
                    store(b, b % 2)
                for u in range(2):
                    sp.wait_ge(stored[u], 16 * (NB0 + 1))

            @block.tensor
            def _(pe):
                def turn_x(b, v, at):
                    pe.wait_ge(x_in[v // 2 % 2], 16 * (at(4) + v // 4 + 1))
                    pe.wait_ge(x_split, b)
                    for j in range(KD):
                        mm = pe.transpose(xT_ps[:, j, :], x[:, v % 4, j * P:(j + 1) * P], k.ident[:])
                    mm.then_inc(turned, 1)

                def up_products(b, v, at):
                    u, r = v % 2, v // 2 % 2
                    pe.wait_ge(x_split, b + 1)
                    if u == 0:
                        pe.wait_ge(w_low, 3 * (at(2) + v // 2) + 2)
                    for dst, hi, lo in ((g_ps, wg_hi, wg_lo), (u_ps, wu_hi, wu_lo)):
                        mm = three_pass(pe, dst[u][:, 0:I0], [(x_hi[u][:, j, :], x_lo[u][:, j, :], hi[r][:, j, :], lo[r][:, j, :])
                                                              for j in range(KD)])
                    mm.then_inc(up, 1)

                def step(b, v, at, left):
                    u, r = v % 2, v // 2 % 2
                    pe.wait_ge(hidden, b + 1)
                    for j in range(KI):
                        mm = pe.transpose(hT_ps[:, j, :], h[u][:, j * P:(j + 1) * P], k.ident[:])
                    mm.then_inc(h_turned, 1)
                    if left > 1:
                        up_products(b + 1, v + 1, at)
                    if left > 2:
                        turn_x(b + 2, v + 2, at)
                    pe.wait_ge(h_split, b + 1)
                    if u == 0:
                        pe.wait_ge(w_low, 3 * (at(2) + v // 2) + 3)
                    three_pass(pe, y_ps[u][:], [(h_hi[u][:, j, :], h_lo[u][:, j, :], wd_hi[r][:, j, :], wd_lo[r][:, j, :])
                                                for j in range(KI)]).then_inc(down, 1)

                turn_x(0, 0, lambda n: 0)
                up_products(0, 0, lambda n: 0)
                turn_x(1, 1, lambda n: 0)
                pe.sem_inc(down, START)
                rounds(pe, STEPS, PERIOD, step)

            @block.scalar
            def _(act):
                def split_w(p, r, n, fills):
                    act.wait_ge(w_in[r], 48 * fills)
                    act.wait_ge(down, START + 2 * p - 2)
                    act.copy(highs[r][n][:], raws[r][n][:]).then_inc(w_high, 1)

                def split_x(b, v):
                    act.wait_ge(turned, b + 1)
                    act.copy(x_hi[v % 2][:], xT_ps[:]).then_inc(x_high, 1)

                def step(b, v, at, left):
                    u = v % 2
                    act.wait_ge(up, b + 1)
                    act.activation(sg[:, u, :], g_ps[u][:, 0:I0], ACT.Silu).then_inc(gated, 1)
                    if left > 1:
                        split_x(b + 1, v + 1)
                    act.wait_ge(h_turned, b + 1)
                    act.wait_ge(down, START + b - 1)
                    act.copy(h_hi[u][:], hT_ps[:]).then_inc(h_high, 1)
                    if left > 2:
                        for n in ((0, 1), (2,))[u]:
                            split_w(at(2) + v // 2 + 1, (v // 2 + 1) % 2, n, at(4) + (v // 2 + 1) // 2 + 1)
                for n in range(3):
                    act.wait_ge(w_in[0], 48)
                    act.copy(highs[0][n][:], raws[0][n][:]).then_inc(w_high, 1)
                    if n == 0:
                        split_x(0, 0)
                rounds(act, STEPS, PERIOD, step)

            @block.vector
            def _(dve):
                def split_w(p, r, n):
                    dve.wait_ge(w_high, 3 * p + n + 1)
                    dve.tensor_tensor(lows[r][n][:], raws[r][n][:], highs[r][n][:], ALU.subtract).then_inc(w_low, 1)

                def split_x(b, v):
                    dve.wait_ge(x_high, b + 1)
                    dve.tensor_tensor(x_lo[v % 2][:], xT_ps[:], x_hi[v % 2][:], ALU.subtract).then_inc(x_split, 1)

                def gate_up(b, v):
                    dve.wait_ge(gated, b + 1)
                    dve.tensor_tensor(h[v % 2][:], sg[:, v % 2, :], u_ps[v % 2][:, 0:I0], ALU.mult).then_inc(hidden, 1)

                def split_h(b, v):
                    dve.wait_ge(h_high, b + 1)
                    dve.tensor_tensor(h_lo[v % 2][:], hT_ps[:], h_hi[v % 2][:], ALU.subtract).then_inc(h_split, 1)

                def split_next(v, at):
                    for n in ((0, 1), (2,))[v % 2]:
                        split_w(at(2) + v // 2 + 1, (v // 2 + 1) % 2, n)

                def step(b, v, at, left):
                    u = v % 2
                    if left > 1:
                        gate_up(b + 1, v + 1)
                    if left > 2:
                        split_x(b + 2, v + 2)
                    dve.wait_ge(down, START + b + 1)
                    dve.wait_ge(stored[u], 16 * (at(2) + v // 2 + 1))
                    dve.tensor_copy(y[:, u, :], y_ps[u][:]).then_inc(evac, 1)
                    if left > 1:
                        split_h(b + 1, v + 1)
                    if left > 3:
                        split_next(v + 1, at)
                split_w(0, 0, 0)
                split_x(0, 0)
                split_w(0, 0, 1)
                split_w(0, 0, 2)
                gate_up(0, 0)
                split_x(1, 1)
                split_h(0, 0)
                split_next(0, lambda n: 0)
                rounds(dve, STEPS, PERIOD, step, 3)


def graph_product(nc, tag, adjT_dram, adj, src, norm, z_hi, z_lo, out, bn):
    HB = NT // 2
    HW = N // 2
    R = 4
    with ExitStack() as st:
        c = Ctx(nc, st, tag)
        a = c.sb("a", [P, R, HW])
        at = c.sb("at", [P, R, HW], BF16)
        s = [c.sb(f"s{r}", [P, HW], F32R) for r in range(R)]
        acc = [c.ps(f"acc{b}", [P, D]) for b in range(HB)]
        loaded = [c.sem(f"loaded{r}") for r in range(R)]
        built, used, summed, read, stats = (c.sem(n) for n in ("built", "used", "summed", "read", "stats"))
        scales, made, high, low, kept = (c.sem(n) for n in ("scales", "made", "high", "low", "kept"))
        if norm is not None:
            mean, rstd, dinv = norm
            z = c.sb("z", [P, R, D])
            half_dinv, z_scale = c.sb("half_dinv", [P, NT]), c.sb("z_scale", [P, NT])

        def z_tile(j):
            return z[:, j % R, :] if norm is not None else src[:, j, :]

        with nc.Block() as block:
            @block.sync
            def _(sp):
                for half in range(2):
                    for j in range(NT):
                        if half or j >= R:
                            sp.wait_ge(built, half * NT + j - R + 1)
                        cols = slice(half * HW, (half + 1) * HW)
                        sp.dma_start(at[:, j % R, :], adjT_dram[j * P:(j + 1) * P, cols]).then_inc(loaded[j % R], 16)
                        if adj is not None:
                            sp.dma_start(a[:, j % R, :], adj[j * P:(j + 1) * P, cols]).then_inc(loaded[j % R], 16)

            def build(eng, half, j):
                eng.wait_ge(used, half * NT + j + 1)
                per = 16 if adj is None else 32
                eng.wait_ge(loaded[j % R], per * (half * (NT // R) + j // R + 1))
                if adj is not None:
                    eng.tensor_tensor(s[j % R][:], a[:, j % R, :], at[:, j % R, :], ALU.add).then_inc(built, 1)
                else:
                    eng.copy(s[j % R][:], at[:, j % R, :]).then_inc(built, 1)

            @block.vector
            def _(dve):
                def make(j):
                    if j >= R:
                        dve.wait_ge(low, j - R + 1)
                        dve.wait_ge(kept, j - R + 1)
                    dve.tensor_scalar(z_tile(j), src[:, j, :], mean[:, j:j + 1], z_scale[:, j:j + 1],
                                      ALU.subtract, ALU.mult).then_inc(made, 1)

                def finish(half):
                    for b in range(HB):
                        o = out[:, half * HB + b, :]
                        dve.wait_ge(summed, half * HB + b + 1)
                        if norm is not None:
                            dve.scalar_tensor_tensor(out=o, in0=acc[b][:], scalar=half_dinv[:, half * HB + b:half * HB + b + 1],
                                                     in1=o, op0=ALU.mult, op1=ALU.add).then_inc(read, 1)
                        else:
                            dve.tensor_tensor(o, acc[b][:], o, ALU.add).then_inc(read, 1)
                    if bn is not None:
                        dve.wait_ge(read, (half + 2) * HB)
                        for b in range(HB):
                            dve.bn_stats(bn[:, half * HB + b, :], out[:, half * HB + b, :]).then_inc(stats, 1)

                if norm is not None:
                    dve.tensor_scalar(half_dinv[:], dinv[:], 0.5, None, ALU.mult).then_inc(scales, 1)
                    dve.tensor_tensor(z_scale[:], rstd[:], dinv[:], ALU.mult).then_inc(scales, 1)
                    dve.wait_ge(scales, 2)
                    make(0)
                    make(1)
                for j in range(NT):
                    if adj is not None:
                        build(dve, 0, j)
                    if norm is not None and j + 2 < NT:
                        make(j + 2)
                    dve.wait_ge(high, j + 1)
                    dve.tensor_tensor(z_lo[:, j, :], z_tile(j), z_hi[:, j, :], ALU.subtract).then_inc(low, 1)
                if norm is not None:
                    dve.wait_ge(kept, NT)
                finish(0)
                if adj is not None:
                    for j in range(NT):
                        build(dve, 1, j)
                finish(1)

            @block.scalar
            def _(act):
                for j in range(NT):
                    if norm is not None:
                        act.wait_ge(made, j + 1)
                    act.copy(z_hi[:, j, :], z_tile(j)).then_inc(high, 1)
                    if norm is not None:
                        act.activation(out[:, j, :], z_tile(j), ACT.Copy, scale=dinv[:, j:j + 1]).then_inc(kept, 1)
                    if adj is None:
                        build(act, 0, j)
                if adj is None:
                    for j in range(NT):
                        build(act, 1, j)

            @block.tensor
            def _(pe):
                pe.sem_inc(used, R)
                pe.sem_inc(read, HB)
                with pe.Fori(0, 2) as half:
                    for j in range(NT):
                        pe.wait_ge(built, half * NT + j + 1)
                        pe.wait_ge(low, j + 1)
                        for b in range(HB):
                            if j == 0:
                                pe.wait_ge(read, half * HB + b + 1)
                            lhs = s[j % R][:, b * P:(b + 1) * P]
                            pe.matmul(acc[b][:], lhs, z_hi[:, j, :], start=(j == 0), stop=False)
                            mm = pe.matmul(acc[b][:], lhs, z_lo[:, j, :], start=False, stop=(j == NT - 1))
                            if j == NT - 1:
                                mm.then_inc(summed, 1)
                        if j < NT - 1:
                            mm.then_inc(used, 1)
                    pe.wait_ge(summed, half * HB + HB)
                    pe.sem_inc(used, 1)


def experts_mlp(nc, k, table, W1, b1, W2, b2, returned):
    MC = D // P
    NC = HID // 512
    R = 4
    with ExitStack() as st:
        c = Ctx(nc, st, "moe1")
        raw = c.sb("raw", [P, R, KD, 512])
        w_hi = [c.sb(f"w_hi{u}", [P, KD, 512], F32R) for u in range(2)]
        w_lo = [c.sb(f"w_lo{u}", [P, KD, 512], F32R) for u in range(2)]
        x = c.sb("x", [P, CT, D])
        x_hi = c.sb("x_hi", [P, KD, CAP], F32R)
        x_lo = c.sb("x_lo", [P, KD, CAP], F32R)
        hf = c.sb("hf", [P, 2, CAP])
        h_hi = [c.sb(f"h_hi{m}", [P, CAP], F32R) for m in range(HID // P)]
        h_lo = [c.sb(f"h_lo{m}", [P, CAP], F32R) for m in range(HID // P)]
        b1_rows = c.sb("b1_rows", [P, P])
        b1_col = c.sb("b1_col", [P, E, HID // P])
        b2_row = c.sb("b2_row", [P, 2, D])
        y = c.sb("y", [P, CT, D])
        xT_ps = [c.ps(f"xT_ps{u}", [P, CAP]) for u in range(2)]
        h_ps = [c.ps(f"h_ps{u}", [P, CAP]) for u in range(2)]
        y_ps = [c.ps(f"y_ps{s}", [P, D]) for s in range(CT)]
        raw_in = [c.sem(f"raw_in{r}") for r in range(R)]
        b1_in, x_in, b2_in = c.sem("b1_in"), c.sem("x_in"), c.sem("b2_in")
        w_high, w_low = c.sem("w_high"), c.sem("w_low")
        turned, x_high, x_low, b1_turned, b1_ready = (c.sem(n) for n in ("turned", "x_high", "x_low", "b1_turned", "b1_ready"))
        up, act_done, h_high, h_low, down, y_done, stored = (
            c.sem(n) for n in ("up", "act_done", "h_high", "h_low", "down", "y_done", "stored"))
        passed_s, passed_p = c.sem("passed_sp"), c.sem("passed_pool")
        with nc.Block() as block:
            @block.sync
            def _(sp):
                sp.sem_inc(stored, 16)
                sp.dma_start(b1_rows[:], b1.rearrange("e (m p) -> (e m) p", p=P)).then_inc(b1_in, 16)

                def chunk(e, n):
                    src = W1[bass.ds(e, 1), :, n * 512:(n + 1) * 512] if n < NC else \
                        W2[bass.ds(e, 1), (n - NC) * 512:(n - NC + 1) * 512, :]
                    sp.dma_start(raw[:, n % R], src.rearrange("a (k p) i -> p (a k) i", p=P)).then_inc(raw_in[n % R], 16)

                def store(e):
                    sp.wait_ge(y_done, START + CT * (e + 1))
                    sp.sem_inc(passed_s, 1)
                    sp.dma_start(returned[bass.ds(e * CAP, CAP), :].rearrange("(s p) d -> p s d", p=P), y[:]).then_inc(stored, 16)

                def rows(e):
                    sp.dma_start(x[:], table[bass.ds(e * CAP, CAP), :].rearrange("(s p) d -> p s d", p=P)).then_inc(x_in, 16)

                rows(0)
                for n in range(R):
                    chunk(0, n)
                with sp.Fori(0, E - 1) as e:
                    for n in range(R, 2 * NC):
                        sp.wait_ge(w_low, 2 * NC * e + n - R + 1)
                        sp.sem_inc(passed_s, 1)
                        chunk(e, n)
                    sp.wait_ge(turned, KD * (e + 1))
                    sp.sem_inc(passed_s, 1)
                    rows(e + 1)
                    for n in range(R):
                        sp.wait_ge(w_low, 2 * NC * e + 2 * NC + n - R + 1)
                        sp.sem_inc(passed_s, 1)
                        chunk(e + 1, n)
                    store(e)
                for n in range(R, 2 * NC):
                    sp.wait_ge(w_low, 2 * NC * (E - 1) + n - R + 1)
                    chunk(E - 1, n)
                store(E - 1)
                sp.wait_ge(stored, 16 * (E + 1))

            @block.tensor
            def _(pe):
                pe.sem_inc(h_low, START)
                pe.sem_inc(y_done, START)
                pe.sem_inc(act_done, 2)
                pe.wait_ge(b1_in, 16)
                pe.transpose(xT_ps[0][:, 0:P], b1_rows[:], k.ident[:]).then_inc(b1_turned, 1)
                pe.wait_ge(b1_ready, 1)

                def turn_rows(e):
                    pe.wait_ge(x_in, 16 * (e + 1))
                    for j in range(KD):
                        if j >= 2:
                            pe.wait_ge(x_low, KD * e + j - 1)
                        for s in range(CT):
                            mm = pe.transpose(xT_ps[j % 2][:, s * P:(s + 1) * P], x[:, s, j * P:(j + 1) * P], k.ident[:])
                        mm.then_inc(turned, 1)

                def up_chunk(e, n):
                    pe.wait_ge(w_low, 2 * NC * e + n + 1)
                    for m in range(MC):
                        pe.wait_ge(act_done, (HID // P) * e + n * MC + m + 1)
                        cols = slice(m * P, (m + 1) * P)
                        mm = three_pass(pe, h_ps[m % 2][:], [(w_hi[n % 2][:, j, cols], w_lo[n % 2][:, j, cols],
                                                             x_hi[:, j, :], x_lo[:, j, :]) for j in range(KD)])
                        mm.then_inc(up, 1)

                def down_chunk(e, n):
                    pe.wait_ge(w_low, 2 * NC * e + NC + n + 1)
                    for m in range(MC):
                        pe.wait_ge(h_low, START + (HID // P) * e + n * MC + m + 1)
                        for s in range(CT):
                            if n == 0 and m == 0:
                                pe.wait_ge(y_done, START + CT * e)
                            for q, (a, b) in enumerate(((h_hi, w_hi), (h_hi, w_lo), (h_lo, w_hi))):
                                mm = pe.matmul(y_ps[s][:], a[n * MC + m][:, s * P:(s + 1) * P], b[(NC + n) % 2][:, m, :],
                                               start=(n == 0 and m == 0 and q == 0), stop=(n == NC - 1 and m == MC - 1 and q == 2))
                    mm.then_inc(down, 1)

                def expert(e, last):
                    pe.wait_ge(x_low, KD * (e + 1))
                    for n in range(NC):
                        up_chunk(e, n)
                    for n in range(NC):
                        down_chunk(e, n)
                        if n == 1 and not last:
                            turn_rows(e + 1)

                turn_rows(0)
                with pe.Fori(0, E - 1) as e:
                    expert(e, False)
                expert(E - 1, True)

            @block.scalar
            def _(act):
                def w_part(e, n):
                    act.wait_ge(raw_in[n % R], 16 * (2 * e + n // R + 1))
                    if n >= NC + 2:
                        act.wait_ge(down, NC * e + n - NC - 1)
                    elif n >= 2:
                        act.wait_ge(up, (HID // P) * e + (n - 1) * MC)
                    elif not (isinstance(e, int) and e == 0):
                        act.wait_ge(down, NC * (e - 1) + NC + n - 1)
                    act.copy(w_hi[n % 2][:], raw[:, n % R]).then_inc(w_high, 1)

                def x_parts(e):
                    for j in range(KD):
                        act.wait_ge(turned, KD * e + j + 1)
                        act.copy(x_hi[:, j, :], xT_ps[j % 2][:]).then_inc(x_high, 1)

                def gelus(e, n):
                    for m in range(MC):
                        g = (HID // P) * e + n * MC + m
                        act.wait_ge(up, g + 1)
                        act.wait_ge(h_low, START + (HID // P) * e + max(n * MC + m - 1, 0))
                        act.activation(hf[:, m % 2, :], h_ps[m % 2][:], ACT.Gelu,
                                       bias=b1_col[:, bass.ds(e, 1), n * MC + m]).then_inc(act_done, 1)
                        act.wait_ge(act_done, g + 3)
                        act.copy(h_hi[n * MC + m][:], hf[:, m % 2, :]).then_inc(h_high, 1)

                x_parts(0)
                w_part(0, 0)
                w_part(0, 1)

                def expert_(e, last):
                    for n in range(NC):
                        gelus(e, n)
                        w_part(e, n + 2)
                    for n in range(NC):
                        if n == 1 and not last:
                            x_parts(e + 1)
                        if n < NC - 2:
                            w_part(e, NC + n + 2)
                        elif not last:
                            w_part(e + 1, n - NC + 2)
                with act.Fori(0, E - 1) as e:
                    expert_(e, False)
                expert_(E - 1, True)

            @block.vector
            def _(dve):
                dve.wait_ge(b1_turned, 1)
                dve.tensor_copy(b1_col[:].rearrange("p e m -> p (e m)"), xT_ps[0][:, 0:P]).then_inc(b1_ready, 1)

                def w_part(e, n):
                    dve.wait_ge(w_high, 2 * NC * e + n + 1)
                    dve.tensor_tensor(w_lo[n % 2][:], raw[:, n % R], w_hi[n % 2][:], ALU.subtract).then_inc(w_low, 1)

                def x_parts(e):
                    for j in range(KD):
                        dve.wait_ge(x_high, KD * e + j + 1)
                        dve.tensor_tensor(x_lo[:, j, :], xT_ps[j % 2][:], x_hi[:, j, :], ALU.subtract).then_inc(x_low, 1)

                def h_parts(e, n):
                    for m in range(MC):
                        dve.wait_ge(h_high, (HID // P) * e + n * MC + m + 1)
                        dve.tensor_tensor(h_lo[n * MC + m][:], hf[:, m % 2, :], h_hi[n * MC + m][:], ALU.subtract).then_inc(h_low, 1)

                def finish(e):
                    dve.wait_ge(down, NC * (e + 1))
                    dve.wait_ge(b2_in, 16 * (e + 1))
                    dve.wait_ge(stored, 16 * e + 16)
                    for s in range(CT):
                        dve.tensor_tensor(y[:, s, :], y_ps[s][:], b2_row[:, 0, :], ALU.add).then_inc(y_done, 1)

                x_parts(0)
                w_part(0, 0)
                w_part(0, 1)

                def expert_(e, last):
                    for n in range(NC):
                        h_parts(e, n)
                        w_part(e, n + 2)
                    for n in range(NC):
                        if n == 1 and not last:
                            x_parts(e + 1)
                        if n < NC - 2:
                            w_part(e, NC + n + 2)
                        elif not last:
                            w_part(e + 1, n - NC + 2)
                    finish(e)
                with dve.Fori(0, E - 1) as e:
                    expert_(e, False)
                expert_(E - 1, True)

            @block.gpsimd
            def _(pool):
                with pool.Fori(0, E) as e:
                    pool.wait_ge(y_done, START + CT * e + 0)
                    pool.sem_inc(passed_p, 1)
                    pool.dma_start(b2_row[:, 0, :], b2[bass.ds(e, 1), :].to_broadcast([P, D])).then_inc(b2_in, 16)


def graph_moe_kernel(nc, x, adj, W_seq, a1, a2, W_out, b_out, gate_w, w_gate, w_up, w_down, Wr, br, W1, b1, W2, b2, out):
    rows0, rows1 = NB0 * BR, E * CAP

    def scratch(name, shape):
        return nc.dram_tensor(name, shape, F32, kind="Internal").ap()
    s1_rows, iso_row = scratch("s1_rows", [H, N]), scratch("iso_row", [1, N])
    sent0, back0 = scratch("sent0", [rows0, D]), scratch("back0", [rows0, D])
    sent1, back1 = scratch("sent1", [rows1, D]), scratch("back1", [rows1, D])
    x3 = scratch("x3", [N, D])

    SPENT.clear()
    adjT_dram = nc.dram_tensor("adjT_dram", [N, N], BF16, kind="Internal").ap()
    with ExitStack() as st:
        c = Ctx(nc, st, "all")
        k = make_constants(nc, c)
        mean, rstd, dinv = c.sb("mean", [P, NT]), c.sb("rstd", [P, NT]), c.sb("dinv", [P, NT])
        bn = c.sb("bn", [P, NT, 6])
        put_at, get_from = c.sb("put_at", [P, TOPK, NT], U32), c.sb("get_from", [P, TOPK, NT], U32)
        weight = c.sb("weight", [P, TOPK, NT])
        constants(nc, k)

        with ExitStack() as st1:
            c1 = Ctx(nc, st1, "one")
            seq = c1.sb("seq", [P, NT, D])
            with ExitStack() as st2:
                c2 = Ctx(nc, st2, "gat")
                adjT = c2.sb("adjT", [P, NT, N], BF16)
                isolated, rowsum, colsum = (c2.sb(n, [P, NT]) for n in ("isolated", "rowsum", "colsum"))
                s1, s2, ea, eb, g, ns2, big_s2 = (c2.sb(n, [P, NT, H]) for n in ("s1", "s2", "ea", "eb", "g", "ns2", "big_s2"))
                with ExitStack() as st3:
                    c3 = Ctx(nc, st3, "first")
                    x_in, w = c3.sb("x", [P, NT, D]), c3.sb("w", [P, KD, WC])
                    w_hi, w_lo = c3.sb("w_hi", [P, KD, WC], F32R), c3.sb("w_lo", [P, KD, WC], F32R)
                    transpose_adj(nc, k, adj, adjT, isolated, rowsum, colsum, x, x_in, bn, W_seq, a1, a2, w, w_hi, w_lo)
                    norm_stats(nc, "norm0", bn, mean, rstd)
                    project_heads(nc, k, x_in, mean, rstd, w_hi, w_lo, seq, s1, s2, adjT, adjT_dram, isolated, iso_row)
                softmax_factors(nc, k, s1, s2, ea, eb, g, ns2, big_s2, s1_rows, rowsum, colsum, dinv)
                attention(nc, k, adjT, seq, ea, eb, g, ns2, big_s2, s1_rows, [sent0, sent1])
            recycle(nc)
            x_sb = c1.sb("x", [P, NT, D])
            project_out(nc, k, seq, x, W_out, b_out, x_sb, bn)
            norm_stats(nc, "norm1", bn, mean, rstd)
            block_expert = c1.sb("block_expert", [P, NB0], I32)
            route(nc, k, "route0", x_sb, mean, rstd, gate_w, None, seq, put_at, get_from, weight, block_expert)
            dispatch(nc, "put0", seq, put_at, sent0, rows0)
            experts_gated(nc, k, block_expert, sent0, w_gate, w_up, w_down, back0, seq)
            gather_experts(nc, "get0", back0, get_from, weight, x_sb, bn)
            norm_stats(nc, "norm2", bn, mean, rstd)
            recycle(nc)
            with ExitStack() as st2:
                c2 = Ctx(nc, st2, "diffuse")
                z_hi, z_lo = c2.sb("z_hi", [P, NT, D], F32R), c2.sb("z_lo", [P, NT, D], F32R)
                graph_product(nc, "sym", adjT_dram, adj, x_sb, (mean, rstd, dinv), z_hi, z_lo, seq, None)
                graph_product(nc, "prod", adjT_dram, None, seq, None, z_hi, z_lo, x_sb, bn)
            norm_stats(nc, "norm3", bn, mean, rstd)
            route(nc, k, "route1", x_sb, mean, rstd, Wr, br, seq, put_at, get_from, weight, None)
            dispatch(nc, "put1", seq, put_at, sent1, rows1, x_sb, x3)
            recycle(nc)
        experts_mlp(nc, k, sent1, W1, b1, W2, b2, back1)
        with ExitStack() as st1:
            x_sb = Ctx(nc, st1, "end").sb("x", [P, NT, D])
            gather_experts(nc, "get1", back1, get_from, weight, x_sb, out=out, x_from=x3)


_INS = ['x', 'adj', 'L0_gnn_W_seq', 'L0_gnn_a1', 'L0_gnn_a2', 'L0_gnn_W_out', 'L0_gnn_b_out', 'L0_ffn_gate_w',
        'L0_ffn_w_gate', 'L0_ffn_w_up', 'L0_ffn_w_down', 'L1_ffn_Wr', 'L1_ffn_br', 'L1_ffn_W1', 'L1_ffn_b1',
        'L1_ffn_W2', 'L1_ffn_b2']
_OUTS = [((2048, 512), 'float32')]


def kernel(**inputs):
    import numpy as _np
    import concourse.bacc as _bacc
    from concourse import mybir as _mybir
    from concourse.bass_utils import run_bass_kernel_spmd as _run

    nc = _bacc.Bacc("TRN2", target_bir_lowering=False, num_devices=1)
    arrays, args = {}, []
    for name in _INS:
        a = _np.ascontiguousarray(inputs[name])
        arrays[f"in_{name}_dram"] = a
        args.append(nc.dram_tensor(f"in_{name}_dram", a.shape, _mybir.dt.from_np(a.dtype), kind="ExternalInput").ap())
    for i, (shape, dtype) in enumerate(_OUTS):
        dt = _mybir.dt.from_np(_np.dtype(dtype))
        args.append(nc.dram_tensor(f"out_{i}_dram", shape, dt, kind="ExternalOutput").ap())
    graph_moe_kernel(nc, *args)
    r = _run(nc, [arrays], core_ids=[0])
    got = tuple(r.results[0][f"out_{i}_dram"] for i in range(len(_OUTS)))
    return got[0]
```

```python
from contextlib import ExitStack

import concourse.bass as bass
from concourse import mybir

F32 = mybir.dt.float32
F32R = mybir.dt.float32r
BF16 = mybir.dt.bfloat16
U32 = mybir.dt.uint32
I32 = mybir.dt.int32
ALU = mybir.AluOpType
ACT = mybir.ActivationFunctionType
AX = mybir.AxisListType
RMAX = bass.bass_isa.ReduceOp.max

P = 128
N = 2048
D = 512
NT = N // P
KD = D // P
H = 16
DH = D // H
E = 8
TOPK = 2
I0 = 384
KI = I0 // P
BR = 256
NB0 = N * TOPK // BR + E - 1
HID = 2048
CAP = N * TOPK // E
CT = CAP // P
WC = D + 2 * H
EPS = 1e-5
SLOPE = 0.2
BIG = 1e20
FAR = 1.0e6


SENT = 16 * NT * TOPK

START = 3


def rounds(eng, total, period, step, tail=2, head=0):
    full = (total - tail) // period

    def plain(first, last):
        for b in range(first, last):
            v = b % period
            step(b, v, lambda n, base=b - v: base // n, total - b)
    plain(0, head * period)
    with eng.Fori(head, full) as i:
        for v in range(period):
            step(period * i + v, v, lambda n: i * (period // n), total)
    plain(full * period, total)


FOURS = [slice(n, n + 4) for n in range(0, NT, 4)]
GROUPS = [slice(0, 2), slice(2, 4)] + FOURS[1:]
GROUP_OF = [g for g, tiles in enumerate(GROUPS) for _ in range(tiles.start, tiles.stop)]


def members(tiles):
    return range(tiles.start, tiles.stop)


class Chain:

    def __init__(self, eng, sem, passed=None):
        self.eng, self.sem, self.n, self.off, self.passed = eng, sem, 0, 0, passed

    def link(self, ins):
        self.n += 1
        ins.then_inc(self.sem, 1)
        self.hold()

    def hold(self):
        self.eng.wait_ge(self.sem, self.off + self.n)
        if self.passed is not None:
            self.eng.sem_inc(self.passed, 1)

    def loop(self, i, per_round):
        self.off = i * per_round


SPENT = []


def recycle(nc):
    nc.clear_and_free_semaphores(list(SPENT))
    SPENT.clear()
    nc.all_engine_barrier()


class Ctx:

    def __init__(self, nc, stack, tag):
        self.nc, self.stack, self.tag = nc, stack, tag

    def sb(self, name, shape, dt=F32):
        return self.stack.enter_context(self.nc.sbuf_tensor(f"{self.tag}_{name}", shape, dt))

    def ps(self, name, shape, dt=F32):
        return self.stack.enter_context(self.nc.psum_tensor(f"{self.tag}_{name}", shape, dt))

    def sem(self, name):
        s = self.nc.alloc_semaphore(f"{self.tag}_{name}")
        SPENT.append(s)
        return s


def constants(nc, k):
    with ExitStack() as st:
        c = Ctx(nc, st, "const")
        filled, shaped = c.sem("filled"), c.sem("shaped")
        with nc.Block() as block:
            @block.gpsimd
            def _(pool):
                pool.memset(k.ident[:], 0.0).then_inc(filled, 1)
                pool.memset(k.before[:], 1.0).then_inc(filled, 1)
                pool.memset(k.ones[:], 1.0).then_inc(filled, 1)
                pool.memset(k.zeros[:], 0.0).then_inc(filled, 1)
                pool.memset(k.zerob[:], 0.0).then_inc(filled, 1)
                pool.wait_ge(filled, 5)
                pool.affine_select(out=k.ident[:], in_=k.ident[:], compare_op=ALU.not_equal, fill=1.0,
                                   base=0, pattern=[[-1, P]], channel_multiplier=1).then_inc(shaped, 1)
                pool.affine_select(out=k.before[:], in_=k.before[:], compare_op=ALU.is_gt, fill=0.0,
                                   base=0, pattern=[[1, P]], channel_multiplier=-1).then_inc(shaped, 1)
                pool.iota(k.expert_id[:], pattern=[[1, E]], base=0, channel_multiplier=0,
                          allow_small_or_imprecise_dtypes=True).then_inc(shaped, 1)
                pool.iota(k.block_start[:], pattern=[[BR, N // BR]], base=0, channel_multiplier=0,
                          allow_small_or_imprecise_dtypes=True).then_inc(shaped, 1)
                pool.iota(k.block_id[:], pattern=[[1, NB0]], base=0, channel_multiplier=0,
                          allow_small_or_imprecise_dtypes=True).then_inc(shaped, 1)
                pool.wait_ge(shaped, 5)
                pool.tensor_copy(k.identb[:], k.ident[:]).then_inc(shaped, 1)


def newton_rsqrt(ch, out, root, value, t):
    ch.link(ch.eng.reciprocal(out, root))
    ch.link(ch.eng.tensor_tensor(t, out, out, ALU.mult))
    ch.link(ch.eng.tensor_tensor(t, t, value, ALU.mult))
    ch.link(ch.eng.tensor_scalar(t, t, -0.5, 1.5, ALU.mult, ALU.add))
    ch.link(ch.eng.tensor_tensor(out, out, t, ALU.mult))


def norm_stats(nc, tag, bn, mean, rstd):
    with ExitStack() as st:
        c = Ctx(nc, st, tag)
        mv = c.sb("mv", [P, NT, 2])
        var = c.sb("var", [P, NT])
        root = c.sb("root", [P, NT])
        t = c.sb("t", [P, NT])
        ch_s, var_ready, root_ready = c.sem("chain"), c.sem("var_ready"), c.sem("root_ready")
        with nc.Block() as block:
            @block.vector
            def _(dve):
                ch = Chain(dve, ch_s)
                for n in range(NT):
                    dve.bn_aggr(mv[:, n, :], bn[:, n, :]).then_inc(ch_s, 1)
                ch.n = NT
                dve.wait_ge(ch_s, NT)
                ch.link(dve.tensor_copy(mean[:], mv[:, :, 0]))
                dve.tensor_scalar(var[:], mv[:, :, 1], EPS, None, ALU.add).then_inc(var_ready, 1)
                dve.wait_ge(root_ready, 1)
                newton_rsqrt(ch, rstd[:], root[:], var[:], t[:])

            @block.scalar
            def _(act):
                act.wait_ge(var_ready, 1)
                act.activation(root[:], var[:], ACT.Sqrt).then_inc(root_ready, 1)


def project_heads(nc, k, x_sb, mean, rstd, w_hi, w_lo, seq, s1, s2, adjT, adjT_dram, isolated, iso_row):
    with ExitStack() as st:
        c = Ctx(nc, st, "proj")
        FILL = 4
        xn = c.sb("xn", [P, 2, D])
        isob = c.sb("isob", [P, N], BF16)
        isoT = c.sb("isoT", [NT, P], BF16)
        hi = [c.sb(f"hi{u}", [P, KD, P], F32R) for u in range(2)]
        lo = [c.sb(f"lo{u}", [P, KD, P], F32R) for u in range(2)]
        xT = [c.ps(f"xT{u}", [P, KD, P]) for u in range(2)]
        out = [c.ps(f"out{u}", [P, D]) for u in range(2)]
        sc = [c.ps(f"sc{u}", [P, 2 * H]) for u in range(2)]
        isoT_ps = c.ps("isoT_ps", [NT, P])
        normed, turned, high, low = c.sem("normed"), c.sem("turned"), c.sem("high"), c.sem("low")
        summed, copied, scored = c.sem("summed"), c.sem("copied"), c.sem("scored")
        iso_turned, iso_kept, iso_wrote, iso_in, filled_p, filled_v = (
            c.sem(x) for x in ("iso_turned", "iso_kept", "iso_wrote", "iso_in", "filled_pool", "filled_dve"))
        spilled = [c.sem(f"spilled{q}") for q in range(4)]
        with nc.Block() as block:
            @block.sync
            def _(sp):
                def spill(q):
                    sp.dma_start(adjT_dram[512 * q:512 * q + 512, :].rearrange("(t p) n -> p t n", p=P),
                                 adjT[:, 4 * q:4 * q + 4, :]).then_inc(spilled[q], 16)
                spill(3)
                sp.wait_ge(iso_kept, 1)
                sp.dma_start(iso_row.rearrange("a (t p) -> (a t) p", p=P), isoT[:]).then_inc(iso_wrote, 16)
                sp.wait_ge(iso_wrote, 16)
                sp.dma_start(isob[:], iso_row.to_broadcast([P, N])).then_inc(iso_in, 16)
                for q in range(3):
                    spill(q)
                for q in range(4):
                    sp.wait_ge(spilled[q], 16)

            @block.gpsimd
            def _(pool):
                pool.wait_ge(iso_in, 16)
                for t in range(NT - FILL):
                    if t % 4 == 0:
                        pool.wait_ge(spilled[t // 4], 16)
                    pool.tensor_tensor(adjT[:, t, :], adjT[:, t, :], isob[:], ALU.add).then_inc(filled_p, 1)

            @block.scalar
            def _(act):
                act.sem_inc(copied, START)

                def high_part(t, u):
                    act.wait_ge(summed, START + t - 1)
                    act.wait_ge(turned, START + t + 1)
                    act.copy(hi[u][:], xT[u][:]).then_inc(high, 1)

                def step(t, u, at, left):
                    if left > 1:
                        high_part(t + 1, (u + 1) % 2)
                    act.wait_ge(summed, START + t + 1)
                    act.copy(seq[:, t, :], out[u][:]).then_inc(copied, 1)
                act.wait_ge(turned, START + 1)
                act.copy(hi[0][:], xT[0][:]).then_inc(high, 1)
                rounds(act, NT, 2, step)

            @block.vector
            def _(dve):
                dve.sem_inc(scored, START)
                dve.wait_ge(iso_turned, 1)
                dve.tensor_copy(isoT[:], isoT_ps[:]).then_inc(iso_kept, 1)

                def norm(t, u):
                    dve.tensor_scalar(xn[:, u, :], x_sb[:, t, :], mean[:, bass.ds(t, 1)], rstd[:, bass.ds(t, 1)],
                                      ALU.subtract, ALU.mult).then_inc(normed, 1)

                def low_part(t, u):
                    dve.wait_ge(high, t + 1)
                    dve.tensor_tensor(lo[u][:], xT[u][:], hi[u][:], ALU.subtract).then_inc(low, 1)

                def step(t, v, at, left):
                    u = v % 2
                    if left > 2:
                        dve.wait_ge(turned, START + t + 1)
                        norm(t + 2, u)
                    if left > 1:
                        low_part(t + 1, (u + 1) % 2)
                    dve.wait_ge(summed, START + t + 1)
                    dve.tensor_copy(s1[:, t, :], sc[u][:, 0:H]).then_inc(scored, 1)
                    dve.tensor_copy(s2[:, t, :], sc[u][:, H:2 * H]).then_inc(scored, 1)
                    if v == 3:
                        dve.wait_ge(iso_in, 16)
                        dve.wait_ge(spilled[3], 16)
                        a_t = adjT[:, NT - FILL + at(4), :]
                        dve.tensor_tensor(a_t, a_t, isob[:], ALU.add).then_inc(filled_v, 1)
                norm(0, 0)
                norm(1, 1)
                low_part(0, 0)
                rounds(dve, NT, NT // FILL, step)

            @block.tensor
            def _(pe):
                pe.sem_inc(turned, START)
                pe.sem_inc(summed, START)
                pe.transpose(isoT_ps[:], isolated[:], k.ident[:]).then_inc(iso_turned, 1)

                def turn(t, u):
                    pe.wait_ge(normed, t + 1)
                    for j in range(KD):
                        mm = pe.transpose(xT[u][:, j, :], xn[:, u, j * P:(j + 1) * P], k.ident[:])
                    mm.then_inc(turned, 1)

                def step(t, u, at, left):
                    if left > 1:
                        turn(t + 1, (u + 1) % 2)
                    pe.wait_ge(low, t + 1)
                    pe.wait_ge(copied, START + t - 1)
                    pe.wait_ge(scored, START + 2 * t - 2)
                    terms = [(hi[u][:, j, :], lo[u][:, j, :], w_hi[:, j, :], w_lo[:, j, :]) for j in range(KD)]
                    three_pass(pe, out[u][:], [(a, b, x[:, 0:D], y[:, 0:D]) for a, b, x, y in terms])
                    three_pass(pe, sc[u][:], [(a, b, x[:, D:WC], y[:, D:WC]) for a, b, x, y in terms]).then_inc(summed, 1)
                turn(0, 0)
                rounds(pe, NT, 2, step)


def three_pass(pe, out, terms):
    n = len(terms)
    for j, (ah, al, bh, bl) in enumerate(terms):
        pe.matmul(out, ah, bh, start=(j == 0), stop=False)
        pe.matmul(out, ah, bl, start=False, stop=False)
        mm = pe.matmul(out, al, bh, start=False, stop=(j == n - 1))
    return mm


def transpose_adj(nc, k, adj, adjT, isolated, rowsum, colsum, x, x_sb, bn, W_seq, a1, a2, w, w_hi, w_lo):
    with ExitStack() as st:
        c = Ctx(nc, st, "adj")
        a = c.sb("a", [P, 2, N])
        ab = c.sb("ab", [P, 2, N], BF16)
        turned_ps = [c.ps(f"turned{u}", [P, NT, P], BF16) for u in range(2)]
        col_ps = c.ps("col_ps", [P, NT])
        loaded = [c.sem(f"loaded{u}") for u in range(2)]
        a_rows = c.sb("a_rows", [P, 2, DH])
        prod = c.sb("prod", [P, KD, H, DH])
        x_in = [c.sem(f"x_in{q}") for q in range(4)]
        cast, turned, kept, ended, stats = (c.sem(x) for x in ("cast", "turned", "kept", "ended", "stats"))
        w_in, halved, w_full, w_high, w_split = (c.sem(x) for x in ("w_in", "halved", "w_full", "w_high", "w_split"))
        passed = c.sem("passed")
        with nc.Block() as block:
            @block.sync
            def _(sp):
                for u in range(2):
                    sp.dma_start(a[:, u, :], adj[u * P:(u + 1) * P, :]).then_inc(loaded[u], 16)
                sp.dma_start(w[:, :, 0:D], W_seq.rearrange("(k p) n -> p k n", p=P)).then_inc(w_in, 16)
                sp.dma_start(a_rows[:, 0, :], a1.rearrange("(a d) -> a d", a=1).to_broadcast([P, DH])).then_inc(w_in, 16)
                sp.dma_start(a_rows[:, 1, :], a2.rearrange("(a d) -> a d", a=1).to_broadcast([P, DH])).then_inc(w_in, 16)
                with sp.Fori(1, NT // 2) as i:
                    for u in range(2):
                        sp.wait_ge(cast, 2 * i + u - 1)
                        sp.sem_inc(passed, 1)
                        sp.dma_start(a[:, u, :], adj[bass.ds((2 * i + u) * P, P), :]).then_inc(loaded[u], 16)
                for q in range(4):
                    sp.dma_start(x_sb[:, 4 * q:4 * q + 4, :],
                                 x[512 * q:512 * q + 512, :].rearrange("(t p) d -> p t d", p=P)).then_inc(x_in[q], 16)

            @block.gpsimd
            def _(pool):
                pool.wait_ge(w_in, 48)
                ch = Chain(pool, halved)
                for m in range(2):
                    for j in range(KD):
                        ch.link(pool.tensor_tensor(prod[:, j], w[:, j, 0:D].rearrange("p (h d) -> p h d", d=DH),
                                                   a_rows[:, m:m + 1, :].to_broadcast([P, H, DH]), ALU.mult))
                    width = DH // 2
                    while width > 1:
                        ch.link(pool.tensor_tensor(prod[:, :, :, 0:width], prod[:, :, :, 0:width],
                                                   prod[:, :, :, width:2 * width], ALU.add))
                        width //= 2
                    ch.link(pool.tensor_tensor(w[:, :, D + m * H:D + (m + 1) * H], prod[:, :, :, 0], prod[:, :, :, 1], ALU.add))
                pool.sem_inc(w_full, 1)

            @block.scalar
            def _(act):
                def cast_rows(t, u, fills):
                    act.wait_ge(loaded[u], 16 * fills)
                    act.wait_ge(turned, START + t - 1)
                    act.activation(ab[:, u, :], a[:, u, :], ACT.Copy, accum_out=rowsum[:, bass.ds(t, 1)]).then_inc(cast, 1)

                def step(t, u, at, left):
                    if left > 1:
                        cast_rows(t + 1, (u + 1) % 2, at(2) + (u + 1) // 2 + 1)
                act.wait_ge(loaded[0], 16)
                act.activation(ab[:, 0, :], a[:, 0, :], ACT.Copy, accum_out=rowsum[:, 0:1]).then_inc(cast, 1)
                rounds(act, NT, 2, step)
                act.wait_ge(w_full, 1)
                act.copy(w_hi[:], w[:]).then_inc(w_high, 1)

            @block.vector
            def _(dve):
                dve.sem_inc(kept, START)

                def step(t, u, at, left):
                    dve.wait_ge(turned, START + t + 1)
                    dve.tensor_copy(adjT[:, :, bass.ds(t * P, P)], turned_ps[u][:]).then_inc(kept, 1)
                rounds(dve, NT, 2, step)
                dve.wait_ge(cast, NT)
                dve.tensor_scalar(isolated[:], rowsum[:], 0.0, None, ALU.is_equal).then_inc(ended, 1)
                dve.wait_ge(turned, START + NT)
                dve.tensor_copy(colsum[:], col_ps[:]).then_inc(ended, 1)
                for n in range(NT):
                    if n % 4 == 0:
                        dve.wait_ge(x_in[n // 4], 16)
                    if n == 4:
                        dve.wait_ge(w_high, 1)
                        dve.tensor_tensor(w_lo[:], w[:], w_hi[:], ALU.subtract).then_inc(w_split, 1)
                    dve.bn_stats(bn[:, n, :], x_sb[:, n, :]).then_inc(stats, 1)

            @block.tensor
            def _(pe):
                pe.sem_inc(turned, START)

                def step(t, u, at, left):
                    pe.wait_ge(cast, t + 1)
                    pe.wait_ge(kept, START + t - 1)
                    for j in range(NT):
                        pe.transpose(turned_ps[u][:, j, :], ab[:, u, j * P:(j + 1) * P], k.identb[:])
                    for j in range(NT):
                        mm = pe.matmul(col_ps[:, j:j + 1], ab[:, u, j * P:(j + 1) * P], k.ones[:, 0:1], start=False,
                                       stop=False, skip_group_check=True)
                    mm.then_inc(turned, 1)
                pe.matmul(col_ps[:], k.zerob[:], k.zerob[:, 0:NT], start=True, stop=False, skip_group_check=True)
                rounds(pe, NT, 2, step)


def softmax_factors(nc, k, s1, s2, ea, eb, g, ns2, big_s2, s1_rows, rowsum, colsum, dinv):
    with ExitStack() as st:
        c = Ctx(nc, st, "factor")
        top = c.sb("top", [P, H])
        m = c.sb("m", [P, H])
        dif = c.sb("dif", [P, NT, H])
        pos = c.sb("pos", [P, NT, H])
        s1T = c.sb("s1T", [H, N])
        deg, some, root, t = (c.sb(n, [P, NT]) for n in ("deg", "some", "root", "t"))
        s1T_ps = c.ps("s1T_ps", [H, NT, P])
        topped, maxed, difs, turned, kept, wrote = (c.sem(x) for x in ("topped", "maxed", "difs", "turned", "kept", "wrote"))
        ch_s, exps, deg_ready, rooted = c.sem("chain"), c.sem("exps"), c.sem("deg_ready"), c.sem("rooted")
        with nc.Block() as block:
            @block.vector
            def _(dve):
                dve.tensor_reduce(top[:], s2[:].rearrange("p t h -> p h t"), AX.X, ALU.max).then_inc(topped, 1)
                dve.tensor_scalar(ns2[:], s2[:], -1.0, None, ALU.mult).then_inc(ch_s, 1)
                dve.tensor_scalar(big_s2[:], s2[:], BIG, None, ALU.mult).then_inc(ch_s, 1)
                dve.wait_ge(maxed, 1)
                mrow = m[:].rearrange("p (a h) -> p a h", a=1).to_broadcast([P, NT, H])
                dve.tensor_tensor(dif[:], s2[:], mrow, ALU.subtract).then_inc(difs, 1)
                ch = Chain(dve, ch_s)
                ch.n = 2
                dve.wait_ge(ch_s, 2)
                ch.link(dve.tensor_tensor(pos[:], s1[:], mrow, ALU.add))
                dve.tensor_scalar(pos[:], pos[:], 0.0, None, ALU.max).then_inc(difs, 1)
                dve.wait_ge(turned, 1)
                dve.tensor_copy(s1T[:], s1T_ps[:].rearrange("h t p -> h (t p)")).then_inc(kept, 1)
                ch.link(dve.tensor_tensor(deg[:], rowsum[:], colsum[:], ALU.add))
                ch.link(dve.tensor_scalar(deg[:], deg[:], 0.5, 1.0, ALU.mult, ALU.add))
                ch.link(dve.tensor_scalar(some[:], deg[:], 0.0, None, ALU.is_gt))
                dve.tensor_scalar(deg[:], deg[:], 1e-30, None, ALU.max).then_inc(deg_ready, 1)
                dve.wait_ge(rooted, 1)
                newton_rsqrt(ch, dinv[:], root[:], deg[:], t[:])
                dve.tensor_tensor(dinv[:], dinv[:], some[:], ALU.mult).then_inc(ch_s, 1)

            @block.gpsimd
            def _(pool):
                pool.wait_ge(topped, 1)
                pool.partition_all_reduce(m[:], top[:], P, RMAX).then_inc(maxed, 1)

            @block.scalar
            def _(act):
                act.wait_ge(difs, 1)
                act.activation(ea[:], dif[:], ACT.Exp).then_inc(exps, 1)
                act.activation(eb[:], dif[:], ACT.Exp, scale=SLOPE).then_inc(exps, 1)
                act.wait_ge(difs, 2)
                act.activation(g[:], pos[:], ACT.Exp, scale=-(1.0 - SLOPE)).then_inc(exps, 1)
                act.wait_ge(deg_ready, 1)
                act.activation(root[:], deg[:], ACT.Sqrt).then_inc(rooted, 1)

            @block.tensor
            def _(pe):
                for n in range(NT):
                    mm = pe.transpose(s1T_ps[:, n, :], s1[:, n, :], k.ident[:])
                mm.then_inc(turned, 1)

            @block.sync
            def _(sp):
                sp.wait_ge(kept, 1)
                sp.dma_start(s1_rows, s1T[:]).then_inc(wrote, 16)
                sp.wait_ge(wrote, 16)


def attention(nc, k, adjT, seq, ea, eb, g, ns2, big_s2, s1_rows, tables):
    HB = NT // 2
    HW = N // 2
    C1 = DH + 1
    STEPPED = [j for j in range(NT) if j % 4]
    RD = 4
    with ExitStack() as st:
        c = Ctx(nc, st, "attn")
        s1_row = c.sb("s1_row", [P, 2, N])
        mask = c.sb("mask", [P, NT, HW], BF16)
        step = c.sb("step", [P, RD, HW], BF16)
        vals = c.sb("vals", [P, NT, 2 * C1])
        rest = c.sb("rest", [P, NT, 2 * C1])
        m_parts = c.sb("m_parts", [P, 2, NT, 3, 2 * C1], BF16)
        a_parts = c.sb("a_parts", [P, 2, NT, 3, C1], BF16)
        sums = c.sb("sums", [P, HB, 2 * C1])
        num = c.sb("num", [P, HB, C1])
        inv = c.sb("inv", [P, HB, 1])
        acc = [c.ps(f"acc{u}", [P, HB, 256]) for u in range(2)]
        rows_in = [c.sem(f"rows_in{u}") for u in range(2)]
        stepped, masked = c.sem("stepped"), c.sem("masked")
        mask_used, acc_free = c.sem("mask_used"), c.sem("acc_free")
        parts_ready, ch_p, ch_v, ch_first = (c.sem(n) for n in ("parts_ready", "pool_chain", "dve_chain", "first_chain"))
        cleared = c.sem("cleared")
        passed_a, passed_p, passed_s = c.sem("passed_act"), c.sem("passed_pool"), c.sem("passed_sp")

        LINKS = 10

        def prepare(ch, h, b):
            v = vals[:].rearrange("p t (w c) -> p t w c", w=2)
            for w, e in ((0, ea), (1, eb)):
                f = e[:, :, bass.ds(h, 1)]
                ch.eng.tensor_tensor(v[:, :, w, 0:DH], seq[:, :, bass.ds(h * DH, DH)],
                                     f.to_broadcast([P, NT, DH]), ALU.mult).then_inc(ch.sem, 1)
                ch.eng.tensor_copy(v[:, :, w, DH:C1], f).then_inc(ch.sem, 1)
            ch.n += 4
            ch.hold()
            mp = m_parts[:, b]
            ch.link(ch.eng.tensor_copy(mp[:, :, 0, :], vals[:]))
            ch.link(ch.eng.tensor_tensor(rest[:], vals[:], mp[:, :, 0, :], ALU.subtract))
            ch.link(ch.eng.tensor_copy(mp[:, :, 1, :], rest[:]))
            ch.link(ch.eng.tensor_tensor(mp[:, :, 2, :], rest[:], mp[:, :, 1, :], ALU.subtract))
            ch.link(ch.eng.tensor_copy(a_parts[:, b], mp[:, :, :, C1:2 * C1]))
            ch.link(ch.eng.tensor_scalar(mp[:, :, :, C1:2 * C1], a_parts[:, b], -1.0, None, ALU.mult))

        with nc.Block() as block:
            @block.sync
            def _(sp):
                for u in range(2):
                    sp.dma_start(s1_row[:, u, :], s1_rows[u:u + 1, :].to_broadcast([P, N])).then_inc(rows_in[u], 16)
                for table in tables:
                    sp.dma_start(table.rearrange("(b p) d -> p b d", p=P),
                                 k.zeros[:].rearrange("p (a d) -> p a d", a=1).to_broadcast([P, table.shape[0] // P, D])
                                 ).then_inc(cleared, 16)
                with sp.Fori(1, H // 2) as i:
                    for u in range(2):
                        sp.wait_ge(masked, NT + (2 * i + u - 1) * 2 * NT)
                        sp.sem_inc(passed_s, 1)
                        sp.wait_ge(stepped, (2 * i + u - 1) * 2 * len(STEPPED))
                        sp.sem_inc(passed_s, 1)
                        sp.dma_start(s1_row[:, u, :], s1_rows[bass.ds(2 * i + u, 1), :].to_broadcast([P, N])).then_inc(rows_in[u], 16)
                sp.wait_ge(cleared, 16 * len(tables))

            @block.scalar
            def _(act):
                with act.Fori(0, H // 2) as i:
                    for v in range(4):
                        u, half, n, h = v // 2, v % 2, 4 * i + v, 2 * i + v // 2
                        act.wait_ge(rows_in[u], 16 * (i + 1))
                        for j in range(NT):
                            if j not in STEPPED:
                                continue
                            src = s1_row[:, u, half * HW:(half + 1) * HW]
                            q = STEPPED.index(j)
                            before = STEPPED[q - RD] + (0 if q >= RD else -NT)
                            act.wait_ge(masked, NT + n * NT + before + 1)
                            act.sem_inc(passed_a, 1)
                            act.activation(step[:, q % RD, :], src, ACT.Sigmoid, bias=big_s2[:, j, bass.ds(h, 1)],
                                           scale=BIG).then_inc(stepped, 1)

            @block.gpsimd
            def _(pool):
                ch = Chain(pool, ch_p, passed_p)
                pool.wait_ge(parts_ready, 1)


                def head(h, u):
                    pool.wait_ge(mask_used, NT + 2 * NT * h)
                    pool.sem_inc(passed_p, 1)
                    prepare(ch, h + 1, 1 - u)
                    pool.sem_inc(parts_ready, 1)

                with pool.Fori(0, H // 2 - 1) as i:
                    ch.loop(i, 2 * LINKS)
                    head(2 * i, 0)
                    head(2 * i + 1, 1)
                assert ch.n == 2 * LINKS
                ch.off = (H // 2 - 2) * 2 * LINKS
                head(H - 2, 0)

            @block.vector
            def _(dve):
                ch = Chain(dve, ch_v)

                def masks(i, v, js):
                    u, half, n, h = (v % 4) // 2, v % 2, 4 * i + v, 2 * i + v // 2
                    if js[0] == 0:
                        dve.wait_ge(rows_in[u], 16 * (i + 1 + v // 4))
                    for j in js:
                        dve.wait_ge(mask_used, n * NT + j + 1)
                        at = adjT[:, j, half * HW:(half + 1) * HW]
                        if j not in STEPPED:
                            dve.scalar_tensor_tensor(out=mask[:, j, :], in0=s1_row[:, u, half * HW:(half + 1) * HW],
                                                     scalar=ns2[:, j, bass.ds(h, 1)], in1=at, op0=ALU.is_gt,
                                                     op1=ALU.mult).then_inc(masked, 1)
                        else:
                            q = STEPPED.index(j)
                            dve.wait_ge(stepped, n * len(STEPPED) + q + 1)
                            dve.tensor_tensor(mask[:, j, :], step[:, q % RD, :], at, ALU.mult).then_inc(masked, 1)

                def combine(i, v):
                    half, n, h = v % 2, 4 * i + v, 2 * i + v // 2
                    dve.wait_ge(mask_used, NT + (n + 1) * NT)
                    dve.tensor_reduce(sums[:], acc[v % 2][:, :, 0:6 * C1].rearrange("p b (s c) -> p b c s", s=3),
                                      AX.X, ALU.add).then_inc(acc_free, 1)
                    dve.wait_ge(acc_free, n + 3)
                    gh = g[:, half * HB:(half + 1) * HB, bass.ds(h, 1)]
                    ch.link(dve.tensor_tensor(num[:], sums[:, :, C1:2 * C1], gh.to_broadcast([P, HB, C1]), ALU.mult))
                    ch.link(dve.tensor_tensor(num[:], num[:], sums[:, :, 0:C1], ALU.add))
                    ch.link(dve.reciprocal(inv[:], num[:, :, DH:C1]))
                    ch.link(dve.tensor_tensor(seq[:, half * HB:(half + 1) * HB, bass.ds(h * DH, DH)], num[:, :, 0:DH],
                                              inv[:].to_broadcast([P, HB, DH]), ALU.mult))

                prepare(Chain(dve, ch_first), 0, 0)
                dve.sem_inc(parts_ready, 1)
                EARLY = 12
                masks(0, 0, range(0, EARLY))

                def round_(i, last):
                    for v in range(4):
                        masks(i, v, range(EARLY, NT))
                        if not (last and v == 3):
                            masks(i, v + 1, range(0, EARLY))
                        combine(i, v)

                with dve.Fori(0, H // 2 - 1) as i:
                    ch.loop(i, 16)
                    round_(i, False)
                ch.off = (H // 2 - 2) * 16
                round_(H // 2 - 1, True)

            @block.tensor
            def _(pe):
                pe.sem_inc(masked, NT)
                pe.sem_inc(mask_used, NT)
                pe.sem_inc(acc_free, 2)
                with pe.Fori(0, H // 2) as i:
                    for v in range(4):
                        u, half, n, h = v // 2, v % 2, 4 * i + v, 2 * i + v // 2
                        pe.wait_ge(acc_free, n + 1)
                        pe.wait_ge(parts_ready, h + 1)
                        for j in range(NT):
                            pe.wait_ge(masked, NT + n * NT + j + 1)
                            for b in range(HB):
                                o = acc[v % 2][:, b, 0:6 * C1]
                                pe.matmul(o, mask[:, j, b * P:(b + 1) * P], m_parts[:, u, j].rearrange("p s c -> p (s c)"),
                                          start=(j == 0 and b % 2 == 0), stop=(j == NT - 1), skip_group_check=True)
                                mm = pe.matmul(o.rearrange("p (s c) -> p s c", s=3)[:, :, C1:2 * C1],
                                               adjT[:, j, half * HW + b * P:half * HW + (b + 1) * P], a_parts[:, u, j],
                                               start=False, stop=(j == NT - 1), skip_group_check=True)
                            mm.then_inc(mask_used, 1)


class Constants:
    pass


def make_constants(nc, c):
    k = Constants()
    k.ident = c.sb("ident", [P, P])
    k.identb = c.sb("identb", [P, P], BF16)
    k.before = c.sb("before", [P, P], BF16)
    k.ones = c.sb("ones", [P, P], BF16)
    k.zerob = c.sb("zerob", [P, P], BF16)
    k.zeros = c.sb("zeros", [P, D])
    k.expert_id = c.sb("expert_id", [P, E])
    k.block_start = c.sb("block_start", [P, N // BR])
    k.block_id = c.sb("block_id", [P, NB0])
    return k


def project_out(nc, k, hid, x_dram, W_out, b_out, x_sb, bn):
    with ExitStack() as st:
        c = Ctx(nc, st, "outp")
        w = c.sb("w", [P, KD, D])
        w_hi = c.sb("w_hi", [P, KD, D], F32R)
        w_lo = c.sb("w_lo", [P, KD, D], F32R)
        bias = c.sb("bias", [P, D])
        hi = [c.sb(f"hi{u}", [P, KD, P], F32R) for u in range(2)]
        lo = [c.sb(f"lo{u}", [P, KD, P], F32R) for u in range(2)]
        tile = c.sb("tile", [P, 2, D])
        z = c.sb("z", [P, 2, D])
        neg = c.sb("neg", [P, 2, D])
        e = c.sb("e", [P, 2, D])
        xT = [c.ps(f"xT{u}", [P, KD, P]) for u in range(2)]
        out = [c.ps(f"out{u}", [P, D]) for u in range(2)]
        loaded, x_in, w_split, w_high = c.sem("loaded"), c.sem("x_in"), c.sem("w_split"), c.sem("w_high")
        passed, stats = c.sem("passed"), c.sem("stats")
        turned, high, low, summed = c.sem("turned"), c.sem("high"), c.sem("low"), c.sem("summed")
        staged, biased, negated, exped, added = c.sem("staged"), c.sem("biased"), c.sem("negated"), c.sem("exped"), c.sem("added")
        with nc.Block() as block:
            @block.sync
            def _(sp):
                sp.dma_start(w[:], W_out.rearrange("(k p) n -> p k n", p=P)).then_inc(loaded, 16)
                sp.dma_start(bias[:], b_out.rearrange("(a d) -> a d", a=1).to_broadcast([P, D])).then_inc(loaded, 16)
                for q in range(4):
                    sp.dma_start(x_sb[:, 4 * q:4 * q + 4, :],
                                 x_dram[512 * q:512 * q + 512, :].rearrange("(t p) d -> p t d", p=P)).then_inc(x_in, 16)

            @block.gpsimd
            def _(pool):
                def step(t, u, at, left):
                    pool.wait_ge(turned, START + t - 1)
                    pool.sem_inc(passed, 1)
                    pool.tensor_copy(tile[:, u, :], hid[:, t, :]).then_inc(staged, 1)
                for t in range(2):
                    pool.tensor_copy(tile[:, t, :], hid[:, t, :]).then_inc(staged, 1)
                with pool.Fori(1, NT // 2) as i:
                    for u in range(2):
                        step(2 * i + u, u, None, None)

            @block.scalar
            def _(act):
                act.wait_ge(loaded, 32)
                act.copy(w_hi[:], w[:]).then_inc(w_high, 1)

                def high_part(t, u):
                    act.wait_ge(turned, START + t + 1)
                    act.wait_ge(summed, START + t - 1)
                    act.copy(hi[u][:], xT[u][:]).then_inc(high, 1)

                def step(t, u, at, left):
                    if left > 1:
                        high_part(t + 1, (u + 1) % 2)
                    act.wait_ge(negated, t + 1)
                    act.activation(e[:, u, :], neg[:, u, :], ACT.Exp).then_inc(exped, 1)
                act.wait_ge(turned, START + 1)
                act.copy(hi[0][:], xT[0][:]).then_inc(high, 1)
                for t in range(NT):
                    step(t, t % 2, None, NT - t)

            @block.vector
            def _(dve):
                dve.wait_ge(w_high, 1)
                dve.tensor_tensor(w_lo[:], w[:], w_hi[:], ALU.subtract).then_inc(w_split, 1)
                dve.sem_inc(biased, START)
                dve.sem_inc(added, START)

                def low_part(t, u):
                    dve.wait_ge(high, t + 1)
                    dve.tensor_tensor(lo[u][:], xT[u][:], hi[u][:], ALU.subtract).then_inc(low, 1)

                def bias_add(t, u):
                    dve.wait_ge(summed, START + t + 1)
                    dve.wait_ge(added, START + 2 * t - 2)
                    dve.tensor_tensor(z[:, u, :], out[u][:], bias[:], ALU.add).then_inc(biased, 1)
                    dve.wait_ge(biased, START + t + 1)
                    dve.tensor_scalar(neg[:, u, :], z[:, u, :], 0.0, None, ALU.min).then_inc(negated, 1)

                def take_stats(t):
                    dve.wait_ge(added, START + 2 * t + 2)
                    dve.bn_stats(bn[:, t, :], x_sb[:, t, :]).then_inc(stats, 1)

                def step(t, u, at, left):
                    if left > 2:
                        low_part(t + 2, u)
                    if left > 1:
                        bias_add(t + 1, (u + 1) % 2)
                    if not (isinstance(t, int) and t == 0):
                        take_stats(t - 1)
                    x_t = x_sb[:, t, :]
                    dve.wait_ge(exped, t + 1)
                    dve.scalar_tensor_tensor(out=e[:, u, :], in0=e[:, u, :], scalar=-1.0, in1=x_t,
                                             op0=ALU.add, op1=ALU.add).then_inc(added, 1)
                    dve.wait_ge(added, START + 2 * t + 1)
                    dve.scalar_tensor_tensor(out=x_t, in0=z[:, u, :], scalar=0.0, in1=e[:, u, :],
                                             op0=ALU.max, op1=ALU.add).then_inc(added, 1)
                low_part(0, 0)
                low_part(1, 1)
                dve.wait_ge(summed, START + 1)
                dve.tensor_tensor(z[:, 0, :], out[0][:], bias[:], ALU.add).then_inc(biased, 1)
                dve.wait_ge(biased, START + 1)
                dve.tensor_scalar(neg[:, 0, :], z[:, 0, :], 0.0, None, ALU.min).then_inc(negated, 1)
                dve.wait_ge(x_in, 64)
                rounds(dve, NT, 2, step, head=1)
                take_stats(NT - 1)

            @block.tensor
            def _(pe):
                pe.sem_inc(turned, START)
                pe.sem_inc(summed, START)

                def turn(t, u):
                    pe.wait_ge(staged, t + 1)
                    for j in range(KD):
                        mm = pe.transpose(xT[u][:, j, :], tile[:, u, j * P:(j + 1) * P], k.ident[:])
                    mm.then_inc(turned, 1)

                def step(t, u, at, left):
                    if left > 1:
                        turn(t + 1, (u + 1) % 2)
                    pe.wait_ge(low, t + 1)
                    pe.wait_ge(biased, START + t - 1)
                    three_pass(pe, out[u][:], [(hi[u][:, j, :], lo[u][:, j, :], w_hi[:, j, :], w_lo[:, j, :])
                                               for j in range(KD)]).then_inc(summed, 1)
                turn(0, 0)
                pe.wait_ge(w_split, 1)
                rounds(pe, NT, 2, step)


def route(nc, k, tag, x_sb, mean, rstd, W_r, b_r, xn, put_at, get_from, weight, block_expert, table=None, spill=None):
    capped = block_expert is None
    NG = len(GROUPS)
    G = max(g.stop - g.start for g in GROUPS)
    with ExitStack() as st:
        c = Ctx(nc, st, tag)
        w = c.sb("w", [P, KD, E])
        bias = c.sb("bias", [P, E])
        xT = [c.sb(f"xT{u}", [P, KD, G, P]) for u in range(2)]
        lgT = c.sb("lgT", [E, NT, P])
        logits = c.sb("logits", [P, NT, E])
        best = c.sb("best", [P, NT, 8])
        best_id = c.sb("best_id", [P, NT, 8], U32)
        chosen = c.sb("chosen", [P, NT, TOPK])
        hot = [c.sb(f"hot{q}", [P, NT, E]) for q in range(TOPK)]
        sel = c.sb("sel", [P, NT, E], BF16)
        gap = c.sb("gap", [P, NT])
        tail = c.sb("tail", [P, NT])
        before_tile = c.sb("before_tile", [P, NT + 1, E])
        pos = c.sb("pos", [P, NT, E])
        keep = c.sb("keep", [P, NT, E])
        cmp = c.sb("cmp", [P, E, N // BR])
        blocks = c.sb("blocks", [P, E])
        ends = c.sb("ends", [P, E + 1])
        cmpb = c.sb("cmpb", [P, NB0, E])
        blk = c.sb("blk", [P, NB0])
        t = [c.sb(f"t{q}", [P, NT, E]) for q in range(TOPK)]
        slot = c.sb("slot", [P, TOPK, NT])
        kept = c.sb("kept", [P, TOPK, NT])
        far = c.sb("far", [P, TOPK, NT])
        xT_ps = [c.ps(f"xT_ps{u}", [P, KD, P]) for u in range(2)]
        lgT_ps = [c.ps(f"lgT_ps{u}", [E, G, P]) for u in range(2)]
        lg_ps = c.ps("lg_ps", [P, NT, E])
        rank_ps = c.ps("rank_ps", [P, NT, E])
        total_ps = c.ps("total_ps", [P, NT, E])
        loaded, stored, normed, turned, copied, scored, score_kept, backed = (
            c.sem(x) for x in ("loaded", "stored", "normed", "turned", "copied", "scored", "score_kept", "backed"))
        chosen_s, ranked, placed, put, gapped, exped, ch_s = (
            c.sem(x) for x in ("chosen", "ranked", "placed", "put", "gapped", "exped", "chain"))
        with nc.Block() as block:
            @block.sync
            def _(sp):
                sp.dma_start(w[:], W_r.rearrange("(k p) e -> p k e", p=P)).then_inc(loaded, 16)
                if b_r is not None:
                    sp.dma_start(bias[:], b_r.rearrange("(a d) -> a d", a=1).to_broadcast([P, E])).then_inc(loaded, 16)
                if spill is not None:
                    for q in range(4):
                        sp.dma_start(spill[512 * q:512 * q + 512, :].rearrange("(t p) d -> p t d", p=P),
                                     x_sb[:, 4 * q:4 * q + 4, :]).then_inc(stored, 16)
                    sp.wait_ge(stored, 64)

            if capped:
                @block.gpsimd
                def _(pool):
                    for g in range(NG):
                        pool.wait_ge(placed, g + 1)
                        dispatch(pool, xn, put_at, table, put, members(GROUPS[g]))
                    pool.wait_ge(put, SENT)

            @block.scalar
            def _(act):
                def keep_scores(g):
                    act.wait_ge(scored, g + 1)
                    act.copy(lgT[:, GROUPS[g], :], lgT_ps[g % 2][:, 0:len(members(GROUPS[g])), :]).then_inc(score_kept, 1)

                for n in range(NT):
                    g = GROUP_OF[n]
                    if n == GROUPS[g].start and g:
                        keep_scores(g - 1)
                    act.wait_ge(turned, n + 1)
                    if g >= 2:
                        act.wait_ge(scored, g - 1)
                    act.copy(xT[g % 2][:, :, n - GROUPS[g].start, :], xT_ps[n % 2][:]).then_inc(copied, 1)
                keep_scores(NG - 1)
                act.wait_ge(gapped, 1)
                act.activation(tail[:], gap[:], ACT.Exp).then_inc(exped, 1)

            @block.tensor
            def _(pe):
                def turn(g):
                    for n in members(GROUPS[g]):
                        pe.wait_ge(normed, n + 1)
                        if n >= 2:
                            pe.wait_ge(copied, n - 1)
                        for j in range(KD):
                            mm = pe.transpose(xT_ps[n % 2][:, j, :], xn[:, n, j * P:(j + 1) * P], k.ident[:])
                        mm.then_inc(turned, 1)

                def score(g):
                    pe.wait_ge(copied, GROUPS[g].stop)
                    if g >= 2:
                        pe.wait_ge(score_kept, g - 1)
                    for j in range(KD):
                        mm = pe.matmul(lgT_ps[g % 2][:, 0:len(members(GROUPS[g])), :], w[:, j, :], xT[g % 2][:, j, 0:len(members(GROUPS[g])), :], start=(j == 0), stop=(j == KD - 1))
                    mm.then_inc(scored, 1)

                def rank(g):
                    pe.wait_ge(chosen_s, g + 1)
                    tiles = GROUPS[g]
                    pe.matmul(rank_ps[:, tiles, :], k.before[:], sel[:, tiles, :], start=True, stop=True)
                    pe.matmul(total_ps[:, tiles, :], k.ones[:], sel[:, tiles, :], start=True, stop=True).then_inc(ranked, 1)

                def turn_back(g):
                    pe.wait_ge(score_kept, g + 1)
                    for n in members(GROUPS[g]):
                        mm = pe.transpose(lg_ps[:, n, :], lgT[:, n, :], k.ident[0:E, 0:E])
                    mm.then_inc(backed, 1)

                pe.wait_ge(loaded, 16 if b_r is None else 32)
                for stage in range(NG + 3):
                    for work, behind in ((rank, 3), (turn_back, 2), (score, 1), (turn, 0)):
                        if 0 <= stage - behind < NG:
                            work(stage - behind)

            @block.vector
            def _(dve):
                for n in range(NT):
                    dve.tensor_scalar(xn[:, n, :], x_sb[:, n, :], mean[:, n:n + 1], rstd[:, n:n + 1],
                                      ALU.subtract, ALU.mult).then_inc(normed, 1)
                ch = Chain(dve, ch_s)
                ch.link(dve.memset(before_tile[:, 0, :], 0.0))
                if capped:
                    ch.link(dve.tensor_scalar(ends[:, 0:E], k.expert_id[:], float(CAP), None, ALU.mult))
                if b_r is not None:
                    dve.wait_ge(loaded, 32)

                def spread(row, n):
                    return row.rearrange("p (a e) -> p a e", a=1).to_broadcast([P, n, E])

                def choose(g):
                    tiles = GROUPS[g]
                    dve.wait_ge(backed, g + 1)
                    if b_r is None:
                        ch.link(dve.tensor_copy(logits[:, tiles, :], lg_ps[:, tiles, :]))
                    else:
                        ch.link(dve.tensor_tensor(logits[:, tiles, :], lg_ps[:, tiles, :], spread(bias[:], len(members(GROUPS[g]))), ALU.add))
                    for n in members(GROUPS[g]):
                        dve.max(best[:, n, :], logits[:, n, :]).then_inc(ch_s, 1)
                    ch.n += len(members(GROUPS[g]))
                    ch.hold()
                    for n in members(GROUPS[g]):
                        dve.max_index(best_id[:, n, :], best[:, n, :], logits[:, n, :]).then_inc(ch_s, 1)
                    ch.n += len(members(GROUPS[g]))
                    ch.hold()
                    ch.link(dve.tensor_copy(chosen[:, tiles, :], best_id[:, tiles, 0:TOPK]))
                    for q in range(TOPK):
                        dve.tensor_tensor(hot[q][:, tiles, :], spread(k.expert_id[:], len(members(GROUPS[g]))),
                                          chosen[:, tiles, q:q + 1].to_broadcast([P, len(members(GROUPS[g])), E]), ALU.is_equal).then_inc(ch_s, 1)
                    ch.n += TOPK
                    ch.hold()
                    dve.tensor_tensor(sel[:, tiles, :], hot[0][:, tiles, :], hot[1][:, tiles, :], ALU.add).then_inc(chosen_s, 1)

                def rank(g):
                    tiles = GROUPS[g]
                    dve.wait_ge(ranked, g + 1)
                    for n in members(GROUPS[g]):
                        ch.link(dve.tensor_tensor(before_tile[:, n + 1, :], before_tile[:, n, :], total_ps[:, n, :], ALU.add))
                    ch.link(dve.tensor_tensor(pos[:, tiles, :], rank_ps[:, tiles, :], before_tile[:, tiles, :], ALU.add))

                def pick(out, values, tiles):
                    for q in range(TOPK):
                        dve.tensor_tensor(t[q][:, tiles, :], hot[q][:, tiles, :], values[:, tiles, :], ALU.mult).then_inc(ch_s, 1)
                    ch.n += TOPK
                    ch.hold()
                    for q in range(TOPK):
                        dve.tensor_reduce(out[:, q, tiles], t[q][:, tiles, :], AX.X, ALU.add).then_inc(ch_s, 1)
                    ch.n += TOPK
                    ch.hold()

                def place(tiles):
                    n = tiles.stop - tiles.start
                    if capped:
                        ch.link(dve.tensor_scalar(keep[:, tiles, :], pos[:, tiles, :], float(CAP), None, ALU.is_lt))
                        pick(kept, keep, tiles)
                    ch.link(dve.tensor_tensor(pos[:, tiles, :], pos[:, tiles, :], spread(ends[:, 0:E], n), ALU.add))
                    pick(slot, pos, tiles)
                    if not capped:
                        dve.tensor_copy(get_from[:, :, tiles], slot[:, :, tiles]).then_inc(placed, 1)
                        dve.tensor_copy(put_at[:, :, tiles], slot[:, :, tiles]).then_inc(placed, 1)
                        return
                    ch.link(dve.tensor_tensor(slot[:, :, tiles], slot[:, :, tiles], kept[:, :, tiles], ALU.mult))
                    ch.link(dve.tensor_scalar(far[:, :, tiles], kept[:, :, tiles], -FAR, FAR, ALU.mult, ALU.add))
                    ch.link(dve.tensor_tensor(far[:, :, tiles], far[:, :, tiles], slot[:, :, tiles], ALU.add))
                    dve.tensor_copy(put_at[:, :, tiles], far[:, :, tiles]).then_inc(placed, 1)
                    ch.link(dve.tensor_copy(get_from[:, :, tiles], slot[:, :, tiles]))

                for g in range(NG):
                    choose(g)
                    rank(g)
                    if capped:
                        place(GROUPS[g])
                dve.tensor_tensor(gap[:], best[:, :, 1], best[:, :, 0], ALU.subtract).then_inc(gapped, 1)
                if not capped:
                    ch.link(dve.tensor_tensor(cmp[:], before_tile[:, NT:NT + 1, :].rearrange("p a e -> p e a").to_broadcast([P, E, N // BR]),
                                              k.block_start[:].rearrange("p (a t) -> p a t", a=1).to_broadcast([P, E, N // BR]), ALU.is_gt))
                    ch.link(dve.tensor_reduce(blocks[:], cmp[:], AX.X, ALU.add))
                    ch.link(dve.memset(ends[:, 0:1], 0.0))
                    for e in range(E):
                        ch.link(dve.tensor_tensor(ends[:, e + 1:e + 2], ends[:, e:e + 1], blocks[:, e:e + 1], ALU.add))
                    ch.link(dve.tensor_tensor(cmpb[:], spread(ends[:, 1:E + 1], NB0),
                                              k.block_id[:].rearrange("p (b a) -> p b a", a=1).to_broadcast([P, NB0, E]), ALU.is_le))
                    ch.link(dve.tensor_reduce(blk[:], cmpb[:], AX.X, ALU.add))
                    ch.link(dve.tensor_scalar(block_expert[:], blk[:], float(E - 1), None, ALU.min))
                    ch.link(dve.tensor_scalar(ends[:], ends[:], float(BR), None, ALU.mult))
                    place(slice(0, NT))
                dve.wait_ge(exped, 1)
                ch.link(dve.tensor_scalar(gap[:], tail[:], 1.0, None, ALU.add))
                ch.link(dve.reciprocal(weight[:, 0, :], gap[:]))
                ch.link(dve.tensor_tensor(weight[:, 1, :], weight[:, 0, :], tail[:], ALU.mult))
                if capped:
                    ch.link(dve.tensor_tensor(weight[:], weight[:], kept[:], ALU.mult))


def dispatch(pool, xn, put_at, table, put, tiles):
    for n in tiles:
        for q in range(TOPK):
            pool.indirect_dma_start(out=table, out_offset=bass.IndirectOffsetOnAxis(ap=put_at[:, q, n:n + 1], axis=0),
                                    in_=xn[:, n, :], in_offset=None, bounds_check=table.shape[0] - 1,
                                    oob_is_err=False).then_inc(put, 16)


def gather_rows(pool, table, get_from, y, got, added, tiles):
    R = len(got)
    for n in range(TOPK * tiles.start, TOPK * tiles.stop):
        if n >= R:
            pool.wait_ge(added, n - R + 1)
        pool.indirect_dma_start(out=y[:, n % R, :], out_offset=None, in_=table,
                                in_offset=bass.IndirectOffsetOnAxis(ap=get_from[:, n % TOPK, n // TOPK:n // TOPK + 1], axis=0)
                                ).then_inc(got[n % R], 16)


def add_rows(dve, tile, y, got, added, weight, x_sb):
    R = len(got)
    for q in range(TOPK):
        n = TOPK * tile + q
        dve.wait_ge(got[n % R], 16 * (n // R + 1))
        if q:
            dve.wait_ge(added, n)
        dve.scalar_tensor_tensor(out=x_sb[:, tile, :], in0=y[:, n % R, :], scalar=weight[:, q, tile:tile + 1],
                                 in1=x_sb[:, tile, :], op0=ALU.mult, op1=ALU.add).then_inc(added, 1)


def combine_out(nc, tag, table, get_from, weight, x_sb, out):
    with ExitStack() as st:
        c = Ctx(nc, st, tag)
        R = 12
        y = c.sb("y", [P, R, D])
        got = [c.sem(f"got{r}") for r in range(R)]
        added, stored = c.sem("added"), c.sem("stored")
        with nc.Block() as block:
            @block.gpsimd
            def _(pool):
                gather_rows(pool, table, get_from, y, got, added, range(NT))

            @block.vector
            def _(dve):
                for tile in range(NT):
                    add_rows(dve, tile, y, got, added, weight, x_sb)

            @block.sync
            def _(sp):
                for first, last in ((0, 4), (4, 8), (8, 12), (12, 14), (14, 15), (15, 16)):
                    sp.wait_ge(added, TOPK * last)
                    sp.dma_start(out[first * P:last * P, :].rearrange("(t p) d -> p t d", p=P),
                                 x_sb[:, first:last, :]).then_inc(stored, 16)
                sp.wait_ge(stored, 96)


def experts_gated(nc, k, block_expert, xn, put_at, table, w_gate, w_up, w_down, returned):
    SB = BR // P
    with ExitStack() as st:
        c = Ctx(nc, st, "moe0")
        x, y = xn[:, 0:2 * SB, :], xn[:, 2 * SB:3 * SB, :]
        wg, wu = ([c.sb(f"{n}{r}", [P, KD, I0]) for r in range(2)] for n in ("wg", "wu"))
        wd = [c.sb(f"wd{r}", [P, KI, D]) for r in range(2)]
        wg_hi, wg_lo, wu_hi, wu_lo = ([c.sb(f"{n}{r}", [P, KD, I0], F32R) for r in range(2)]
                                      for n in ("wg_hi", "wg_lo", "wu_hi", "wu_lo"))
        wd_hi, wd_lo = ([c.sb(f"{n}{r}", [P, KI, D], F32R) for r in range(2)] for n in ("wd_hi", "wd_lo"))
        x_hi, x_lo = c.sb("x_hi", [P, KD, BR], F32R), c.sb("x_lo", [P, KD, BR], F32R)
        h_hi, h_lo = ([c.sb(f"{n}{m}", [P, BR], F32R) for m in range(KI)] for n in ("h_hi", "h_lo"))
        sg = c.sb("sg", [P, KI, BR])
        h = c.sb("h", [P, KI, BR])
        xT_ps = c.ps("xT_ps", [P, KD, BR])
        up_ps = [c.ps(f"up_ps{m}", [P, 2, BR]) for m in range(KI)]
        y_ps = [c.ps(f"y_ps{s}", [P, D]) for s in range(SB)]
        put = c.sem("put")
        w_in = [c.sem(f"w_in{r}") for r in range(2)]
        x_in = [c.sem(f"x_in{r}") for r in range(2)]
        stored = [c.sem(f"stored{s}") for s in range(SB)]
        w_high, w_low, turned, x_high, x_split, up, gated, hidden, h_high, h_split, down, evac = (
            c.sem(n) for n in ("w_high", "w_low", "turned", "x_high", "x_split", "up", "gated", "hidden",
                               "h_high", "h_split", "down", "evac"))
        passed_s = c.sem("passed_sp")
        raws = [[wg[r], wu[r], wd[r]] for r in range(2)]
        highs = [[wg_hi[r], wu_hi[r], wd_hi[r]] for r in range(2)]
        lows = [[wg_lo[r], wu_lo[r], wd_lo[r]] for r in range(2)]
        with nc.Block() as block:
            @block.sync
            def _(sp):
                for s in range(SB):
                    sp.sem_inc(stored[s], 16)

                def load_rows(p, r):
                    sp.dma_start(x[:, SB * r:SB * r + SB, :],
                                 table[bass.ds(p * BR, BR), :].rearrange("(s q) d -> q s d", q=P)).then_inc(x_in[r], 16)

                def load_weights(p, r):
                    ex = sp.value_load(block_expert[0:1, bass.ds(p, 1)], min_val=0, max_val=E - 1)
                    for dst, src in zip(raws[r], (w_gate, w_up, w_down)):
                        sp.dma_start(dst[:], src[bass.ds(ex, 1), :, :].rearrange("a (k q) i -> q (a k) i", q=P)).then_inc(w_in[r], 16)

                def store(b, s):
                    sp.wait_ge(evac, START + b + 1)
                    sp.sem_inc(passed_s, 1)
                    sp.dma_start(returned[bass.ds(b * P, P), :], y[:, s, :]).then_inc(stored[s], 16)

                load_weights(0, 0)
                load_weights(1, 1)
                sp.wait_ge(put, SENT)
                load_rows(0, 0)
                load_rows(1, 1)
                with sp.Fori(1, (NB0 - 1) // 2) as i:
                    for r in range(2):
                        sp.wait_ge(w_low, 3 * (2 * i + r - 1))
                        sp.sem_inc(passed_s, 1)
                        sp.wait_ge(turned, 2 * i + r - 1)
                        sp.sem_inc(passed_s, 1)
                        load_rows(2 * i + r, r)
                        load_weights(2 * i + r, r)
                        for s in range(SB):
                            store(SB * (2 * i + r - 2) + s, s)
                sp.wait_ge(w_low, 3 * (NB0 - 2))
                sp.wait_ge(turned, NB0 - 2)
                load_rows(NB0 - 1, 0)
                load_weights(NB0 - 1, 0)
                for b in range(SB * (NB0 - 3), SB * NB0):
                    store(b, b % SB)
                for s in range(SB):
                    sp.wait_ge(stored[s], 16 * (NB0 + 1))

            @block.gpsimd
            def _(pool):
                dispatch(pool, xn, put_at, table, put, range(NT))
                pool.wait_ge(put, SENT)

            @block.tensor
            def _(pe):
                def turn_x(r, fills):
                    pe.wait_ge(x_in[r], 16 * fills)
                    for s in range(SB):
                        for j in range(KD):
                            mm = pe.transpose(xT_ps[:, j, s * P:(s + 1) * P], x[:, SB * r + s, j * P:(j + 1) * P], k.ident[:])
                    mm.then_inc(turned, 1)

                def step(p, r, at, left):
                    pe.wait_ge(x_split, p + 1)
                    pe.wait_ge(w_low, 3 * p + 2)
                    for m in range(KI):
                        cols = slice(m * P, (m + 1) * P)
                        for q, (hi, lo) in enumerate(((wg_hi, wg_lo), (wu_hi, wu_lo))):
                            mm = three_pass(pe, up_ps[m][:, q, :], [(hi[r][:, j, cols], lo[r][:, j, cols], x_hi[:, j, :], x_lo[:, j, :])
                                                                    for j in range(KD)])
                        mm.then_inc(up, 1)
                    if left > 1:
                        turn_x((r + 1) % 2, at(2) + (r + 1) // 2 + 1)
                    pe.wait_ge(w_low, 3 * p + 3)
                    for m in range(KI):
                        pe.wait_ge(h_split, KI * p + m + 1)
                        for s in range(SB):
                            if m == 0:
                                pe.wait_ge(evac, START + SB * (p - 1) + s + 1)
                            rows = slice(s * P, (s + 1) * P)
                            for q, (a, b) in enumerate(((h_hi, wd_hi), (h_hi, wd_lo), (h_lo, wd_hi))):
                                mm = pe.matmul(y_ps[s][:], a[m][:, rows], b[r][:, m, :], start=(m == 0 and q == 0),
                                               stop=(m == KI - 1 and q == 2))
                            if m == KI - 1:
                                mm.then_inc(down, 1)
                turn_x(0, 1)
                rounds(pe, NB0, 2, step)

            @block.scalar
            def _(act):
                def split_w(n, r, fills):
                    act.wait_ge(w_in[r], 48 * fills)
                    act.copy(highs[r][n][:], raws[r][n][:]).then_inc(w_high, 1)

                def split_x(p):
                    act.wait_ge(turned, p + 1)
                    act.copy(x_hi[:], xT_ps[:]).then_inc(x_high, 1)

                def gate(p, m):
                    act.wait_ge(up, KI * p + m + 1)
                    act.activation(sg[:, m, :], up_ps[m][:, 0, :], ACT.Silu).then_inc(gated, 1)

                def split_h(p, m):
                    act.wait_ge(hidden, KI * p + m + 1)
                    act.copy(h_hi[m][:], h[:, m, :]).then_inc(h_high, 1)

                def step(p, r, at, left):
                    following = (r + 1) % 2, at(2) + (r + 1) // 2 + 1
                    gate(p, 0)
                    if left > 1:
                        split_w(0, *following)
                    gate(p, 1)
                    split_h(p, 0)
                    if left > 1:
                        split_w(1, *following)
                    gate(p, 2)
                    split_h(p, 1)
                    split_h(p, 2)
                    if left > 1:
                        split_x(p + 1)
                        split_w(2, *following)
                for n in range(3):
                    split_w(n, 0, 1)
                split_x(0)
                rounds(act, NB0, 2, step)

            @block.vector
            def _(dve):
                dve.sem_inc(evac, START)

                def split_w(p, n, r):
                    dve.wait_ge(w_high, 3 * p + n + 1)
                    dve.tensor_tensor(lows[r][n][:], raws[r][n][:], highs[r][n][:], ALU.subtract).then_inc(w_low, 1)

                def split_x(p):
                    dve.wait_ge(x_high, p + 1)
                    dve.tensor_tensor(x_lo[:], xT_ps[:], x_hi[:], ALU.subtract).then_inc(x_split, 1)

                def gate_up(p, m):
                    dve.wait_ge(gated, KI * p + m + 1)
                    dve.tensor_tensor(h[:, m, :], sg[:, m, :], up_ps[m][:, 1, :], ALU.mult).then_inc(hidden, 1)

                def split_h(p, m):
                    dve.wait_ge(h_high, KI * p + m + 1)
                    dve.tensor_tensor(h_lo[m][:], h[:, m, :], h_hi[m][:], ALU.subtract).then_inc(h_split, 1)

                def step(p, r, at, left):
                    gate_up(p, 0)
                    if left > 1:
                        split_w(p + 1, 0, (r + 1) % 2)
                    gate_up(p, 1)
                    split_h(p, 0)
                    if left > 1:
                        split_w(p + 1, 1, (r + 1) % 2)
                    gate_up(p, 2)
                    split_h(p, 1)
                    split_h(p, 2)
                    if left > 1:
                        split_x(p + 1)
                        split_w(p + 1, 2, (r + 1) % 2)
                    for s in range(SB):
                        dve.wait_ge(down, SB * p + s + 1)
                        dve.wait_ge(stored[s], 16 * (p + 1))
                        dve.tensor_copy(y[:, s, :], y_ps[s][:]).then_inc(evac, 1)
                for n in range(3):
                    split_w(0, n, 0)
                split_x(0)
                rounds(dve, NB0, 2, step)


def graph_product(nc, tag, adjT_dram, adj, src, gather, dinv, z_hi, z_lo, out, bn):
    HB = NT // 2
    HW = N // 2
    R = 4
    RY = 8
    with ExitStack() as st:
        c = Ctx(nc, st, tag)
        a = c.sb("a", [P, R, HW])
        at = c.sb("at", [P, R, HW], BF16)
        s = [c.sb(f"s{r}", [P, HW], F32R) for r in range(R)]
        acc = [c.ps(f"acc{b}", [P, D]) for b in range(HB)]
        loaded = [c.sem(f"loaded{r}") for r in range(R)]
        built, used, summed, read, stats = (c.sem(n) for n in ("built", "used", "summed", "read", "stats"))
        made, high, low, kept = (c.sem(n) for n in ("made", "high", "low", "kept"))
        if gather is not None:
            table, get_from, weight = gather
            y = c.sb("y", [P, RY, D])
            z = c.sb("z", [P, R, D])
            half_dinv, z_scale, mean, var, root, rstd, t = (
                c.sb(n, [P, NT]) for n in ("half_dinv", "z_scale", "mean", "var", "root", "rstd", "t"))
            mv = c.sb("mv", [P, NT, 2])
            got = [c.sem(f"got{r}") for r in range(RY)]
            added, varied, rooted, ch_s = (c.sem(n) for n in ("added", "varied", "rooted", "chain"))

        def z_tile(j):
            return z[:, j % R, :] if gather is not None else src[:, j, :]

        with nc.Block() as block:
            @block.sync
            def _(sp):
                for half in range(2):
                    for j in range(NT):
                        if half or j >= R:
                            sp.wait_ge(built, half * NT + j - R + 1)
                        cols = slice(half * HW, (half + 1) * HW)
                        sp.dma_start(at[:, j % R, :], adjT_dram[j * P:(j + 1) * P, cols]).then_inc(loaded[j % R], 16)
                        if gather is not None:
                            sp.dma_start(a[:, j % R, :], adj[j * P:(j + 1) * P, cols]).then_inc(loaded[j % R], 16)

            def build(eng, half, j):
                eng.wait_ge(used, half * NT + j + 1)
                per = 16 if gather is None else 32
                eng.wait_ge(loaded[j % R], per * (half * (NT // R) + j // R + 1))
                if gather is not None:
                    eng.tensor_tensor(s[j % R][:], a[:, j % R, :], at[:, j % R, :], ALU.add).then_inc(built, 1)
                else:
                    eng.copy(s[j % R][:], at[:, j % R, :]).then_inc(built, 1)

            if gather is not None:
                @block.gpsimd
                def _(pool):
                    for g in range(len(FOURS) + 1):
                        if g < len(FOURS):
                            gather_rows(pool, table, get_from, y, got, added, members(FOURS[g]))
                        for j in members(FOURS[g - 1]) if g else ():
                            build(pool, 0, j)
                    for j in range(NT):
                        build(pool, 1, j)

            @block.vector
            def _(dve):
                def make(j):
                    if j >= R:
                        dve.wait_ge(low, j - R + 1)
                        dve.wait_ge(kept, j - R + 1)
                    dve.tensor_scalar(z_tile(j), src[:, j, :], mean[:, j:j + 1], z_scale[:, j:j + 1],
                                      ALU.subtract, ALU.mult).then_inc(made, 1)

                def finish(half):
                    for b in range(HB):
                        o = out[:, half * HB + b, :]
                        dve.wait_ge(summed, half * HB + b + 1)
                        if gather is not None:
                            dve.scalar_tensor_tensor(out=o, in0=acc[b][:], scalar=half_dinv[:, half * HB + b:half * HB + b + 1],
                                                     in1=o, op0=ALU.mult, op1=ALU.add).then_inc(read, 1)
                        else:
                            dve.tensor_tensor(o, acc[b][:], o, ALU.add).then_inc(read, 1)
                    if gather is None:
                        dve.wait_ge(read, (half + 2) * HB)
                        for b in range(HB):
                            dve.bn_stats(bn[:, half * HB + b, :], out[:, half * HB + b, :]).then_inc(stats, 1)

                def split(j):
                    dve.wait_ge(high, j + 1)
                    dve.tensor_tensor(z_lo[:, j, :], z_tile(j), z_hi[:, j, :], ALU.subtract).then_inc(low, 1)

                if gather is None:
                    for j in range(NT):
                        split(j)
                else:
                    ch = Chain(dve, ch_s)
                    ch.link(dve.tensor_scalar(half_dinv[:], dinv[:], 0.5, None, ALU.mult))
                    for g, tiles in enumerate(FOURS):
                        for n in members(FOURS[g]):
                            add_rows(dve, n, y, got, added, weight, src)
                            dve.wait_ge(added, TOPK * n + TOPK)
                            ch.link(dve.bn_stats(bn[:, n, :], src[:, n, :]))
                        for n in members(FOURS[g]):
                            dve.bn_aggr(mv[:, n, :], bn[:, n, :]).then_inc(ch_s, 1)
                        ch.n += len(members(FOURS[g]))
                        ch.hold()
                        dve.tensor_scalar(var[:, tiles], mv[:, tiles, 1], EPS, None, ALU.add).then_inc(varied, 1)
                        ch.link(dve.tensor_copy(mean[:, tiles], mv[:, tiles, 0]))
                        dve.wait_ge(rooted, g + 1)
                        newton_rsqrt(ch, rstd[:, tiles], root[:, tiles], var[:, tiles], t[:, tiles])
                        ch.link(dve.tensor_tensor(z_scale[:, tiles], rstd[:, tiles], dinv[:, tiles], ALU.mult))
                        for j in members(FOURS[g]):
                            make(j)
                        for j in members(FOURS[g]):
                            split(j)
                    dve.wait_ge(kept, NT)
                finish(0)
                finish(1)

            @block.scalar
            def _(act):
                for j in range(NT):
                    if gather is not None:
                        if j % 4 == 0:
                            tiles = FOURS[j // 4]
                            act.wait_ge(varied, j // 4 + 1)
                            act.activation(root[:, tiles], var[:, tiles], ACT.Sqrt).then_inc(rooted, 1)
                        act.wait_ge(made, j + 1)
                    act.copy(z_hi[:, j, :], z_tile(j)).then_inc(high, 1)
                    if gather is not None:
                        act.activation(out[:, j, :], z_tile(j), ACT.Copy, scale=dinv[:, j:j + 1]).then_inc(kept, 1)
                    else:
                        build(act, 0, j)
                if gather is None:
                    for j in range(NT):
                        build(act, 1, j)

            @block.tensor
            def _(pe):
                pe.sem_inc(used, R)
                pe.sem_inc(read, HB)
                with pe.Fori(0, 2) as half:
                    for j in range(NT):
                        pe.wait_ge(built, half * NT + j + 1)
                        pe.wait_ge(low, j + 1)
                        for b in range(HB):
                            if j == 0:
                                pe.wait_ge(read, half * HB + b + 1)
                            lhs = s[j % R][:, b * P:(b + 1) * P]
                            pe.matmul(acc[b][:], lhs, z_hi[:, j, :], start=(j == 0), stop=False)
                            mm = pe.matmul(acc[b][:], lhs, z_lo[:, j, :], start=False, stop=(j == NT - 1))
                            if j == NT - 1:
                                mm.then_inc(summed, 1)
                        if j < NT - 1:
                            mm.then_inc(used, 1)
                    pe.wait_ge(summed, half * HB + HB)
                    pe.sem_inc(used, 1)


def experts_mlp(nc, k, x_sb, table, W1, b1, W2, b2, returned, x_from):
    MC = D // P
    NC = HID // 512
    R = 4
    with ExitStack() as st:
        c = Ctx(nc, st, "moe1")
        raw = c.sb("raw", [P, R, KD, 512])
        w_hi = [c.sb(f"w_hi{u}", [P, KD, 512], F32R) for u in range(2)]
        w_lo = [c.sb(f"w_lo{u}", [P, KD, 512], F32R) for u in range(2)]
        x = c.sb("x", [P, CT, D])
        x_hi = c.sb("x_hi", [P, KD, CAP], F32R)
        x_lo = c.sb("x_lo", [P, KD, CAP], F32R)
        hf = c.sb("hf", [P, 2, CAP])
        h_hi = [c.sb(f"h_hi{m}", [P, CAP], F32R) for m in range(HID // P)]
        h_lo = [c.sb(f"h_lo{m}", [P, CAP], F32R) for m in range(HID // P)]
        b1_rows = c.sb("b1_rows", [P, P])
        b1_col = c.sb("b1_col", [P, E, HID // P])
        b2_row = c.sb("b2_row", [P, D])
        y = c.sb("y", [P, CT, D])
        xT_ps = [c.ps(f"xT_ps{u}", [P, CAP]) for u in range(2)]
        h_ps = [c.ps(f"h_ps{u}", [P, CAP]) for u in range(2)]
        y_ps = [c.ps(f"y_ps{s}", [P, D]) for s in range(CT)]
        raw_in = [c.sem(f"raw_in{r}") for r in range(R)]
        b1_in, x_in, b2_in = c.sem("b1_in"), c.sem("x_in"), c.sem("b2_in")
        w_high, w_low = c.sem("w_high"), c.sem("w_low")
        turned, x_high, x_low, b1_turned, b1_ready = (c.sem(n) for n in ("turned", "x_high", "x_low", "b1_turned", "b1_ready"))
        up, act_done, h_high, h_low, down, y_done, stored = (
            c.sem(n) for n in ("up", "act_done", "h_high", "h_low", "down", "y_done", "stored"))
        passed_s, passed_p = c.sem("passed_sp"), c.sem("passed_pool")
        x_back = c.sem("x_back")
        with nc.Block() as block:
            @block.sync
            def _(sp):
                sp.sem_inc(stored, 16)
                sp.dma_start(b1_rows[:], b1.rearrange("e (m p) -> (e m) p", p=P)).then_inc(b1_in, 16)

                def chunk(e, n):
                    src = W1[bass.ds(e, 1), :, n * 512:(n + 1) * 512] if n < NC else \
                        W2[bass.ds(e, 1), (n - NC) * 512:(n - NC + 1) * 512, :]
                    sp.dma_start(raw[:, n % R], src.rearrange("a (k p) i -> p (a k) i", p=P)).then_inc(raw_in[n % R], 16)

                def store(e):
                    sp.wait_ge(y_done, START + CT * (e + 1))
                    sp.sem_inc(passed_s, 1)
                    sp.dma_start(returned[bass.ds(e * CAP, CAP), :].rearrange("(s p) d -> p s d", p=P), y[:]).then_inc(stored, 16)

                def rows(e):
                    sp.dma_start(x[:], table[bass.ds(e * CAP, CAP), :].rearrange("(s p) d -> p s d", p=P)).then_inc(x_in, 16)

                chunk(0, 0)
                rows(0)
                for n in range(1, R):
                    chunk(0, n)
                for q in range(4):
                    sp.dma_start(x_sb[:, 4 * q:4 * q + 4, :],
                                 x_from[512 * q:512 * q + 512, :].rearrange("(t p) d -> p t d", p=P)).then_inc(x_back, 16)
                with sp.Fori(0, E - 1) as e:
                    for n in range(R, 2 * NC):
                        sp.wait_ge(w_low, 2 * NC * e + n - R + 1)
                        sp.sem_inc(passed_s, 1)
                        chunk(e, n)
                    sp.wait_ge(turned, KD * (e + 1))
                    sp.sem_inc(passed_s, 1)
                    rows(e + 1)
                    for n in range(R):
                        sp.wait_ge(w_low, 2 * NC * e + 2 * NC + n - R + 1)
                        sp.sem_inc(passed_s, 1)
                        chunk(e + 1, n)
                    store(e)
                for n in range(R, 2 * NC):
                    sp.wait_ge(w_low, 2 * NC * (E - 1) + n - R + 1)
                    chunk(E - 1, n)
                store(E - 1)
                sp.wait_ge(stored, 16 * (E + 1))
                sp.wait_ge(x_back, 64)

            @block.tensor
            def _(pe):
                pe.sem_inc(h_low, START)
                pe.sem_inc(y_done, START)
                pe.sem_inc(act_done, 2)
                pe.wait_ge(b1_in, 16)
                pe.transpose(xT_ps[0][:, 0:P], b1_rows[:], k.ident[:]).then_inc(b1_turned, 1)
                pe.wait_ge(b1_ready, 1)

                def turn_rows(e):
                    pe.wait_ge(x_in, 16 * (e + 1))
                    for j in range(KD):
                        if j >= 2:
                            pe.wait_ge(x_low, KD * e + j - 1)
                        for s in range(CT):
                            mm = pe.transpose(xT_ps[j % 2][:, s * P:(s + 1) * P], x[:, s, j * P:(j + 1) * P], k.ident[:])
                        mm.then_inc(turned, 1)

                def up_chunk(e, n):
                    pe.wait_ge(w_low, 2 * NC * e + n + 1)
                    for m in range(MC):
                        pe.wait_ge(act_done, (HID // P) * e + n * MC + m + 1)
                        cols = slice(m * P, (m + 1) * P)
                        mm = three_pass(pe, h_ps[m % 2][:], [(w_hi[n % 2][:, j, cols], w_lo[n % 2][:, j, cols],
                                                             x_hi[:, j, :], x_lo[:, j, :]) for j in range(KD)])
                        mm.then_inc(up, 1)

                def down_chunk(e, n):
                    pe.wait_ge(w_low, 2 * NC * e + NC + n + 1)
                    for m in range(MC):
                        pe.wait_ge(h_low, START + (HID // P) * e + n * MC + m + 1)
                        for s in range(CT):
                            if n == 0 and m == 0:
                                pe.wait_ge(y_done, START + CT * e)
                            for q, (a, b) in enumerate(((h_hi, w_hi), (h_hi, w_lo), (h_lo, w_hi))):
                                mm = pe.matmul(y_ps[s][:], a[n * MC + m][:, s * P:(s + 1) * P], b[(NC + n) % 2][:, m, :],
                                               start=(n == 0 and m == 0 and q == 0), stop=(n == NC - 1 and m == MC - 1 and q == 2))
                    mm.then_inc(down, 1)

                def expert(e, last):
                    pe.wait_ge(x_low, KD * (e + 1))
                    for n in range(NC):
                        up_chunk(e, n)
                    for n in range(NC):
                        down_chunk(e, n)
                        if n == 1 and not last:
                            turn_rows(e + 1)

                turn_rows(0)
                with pe.Fori(0, E - 1) as e:
                    expert(e, False)
                expert(E - 1, True)

            @block.scalar
            def _(act):
                def w_part(e, n):
                    act.wait_ge(raw_in[n % R], 16 * (2 * e + n // R + 1))
                    if n >= NC + 2:
                        act.wait_ge(down, NC * e + n - NC - 1)
                    elif n >= 2:
                        act.wait_ge(up, (HID // P) * e + (n - 1) * MC)
                    elif not (isinstance(e, int) and e == 0):
                        act.wait_ge(down, NC * (e - 1) + NC + n - 1)
                    act.copy(w_hi[n % 2][:], raw[:, n % R]).then_inc(w_high, 1)

                def x_parts(e):
                    for j in range(KD):
                        act.wait_ge(turned, KD * e + j + 1)
                        act.copy(x_hi[:, j, :], xT_ps[j % 2][:]).then_inc(x_high, 1)

                def gelus(e, n):
                    for m in range(MC):
                        g = (HID // P) * e + n * MC + m
                        act.wait_ge(up, g + 1)
                        act.wait_ge(h_low, START + (HID // P) * e + max(n * MC + m - 1, 0))
                        act.activation(hf[:, m % 2, :], h_ps[m % 2][:], ACT.Gelu,
                                       bias=b1_col[:, bass.ds(e, 1), n * MC + m]).then_inc(act_done, 1)
                        act.wait_ge(act_done, g + 3)
                        act.copy(h_hi[n * MC + m][:], hf[:, m % 2, :]).then_inc(h_high, 1)

                w_part(0, 0)
                x_parts(0)
                w_part(0, 1)

                def expert_(e, last):
                    for n in range(NC):
                        gelus(e, n)
                        w_part(e, n + 2)
                    for n in range(NC):
                        if n == 1 and not last:
                            x_parts(e + 1)
                        if n < NC - 2:
                            w_part(e, NC + n + 2)
                        elif not last:
                            w_part(e + 1, n - NC + 2)
                with act.Fori(0, E - 1) as e:
                    expert_(e, False)
                expert_(E - 1, True)

            @block.vector
            def _(dve):
                dve.wait_ge(b1_turned, 1)
                dve.tensor_copy(b1_col[:].rearrange("p e m -> p (e m)"), xT_ps[0][:, 0:P]).then_inc(b1_ready, 1)

                def w_part(e, n):
                    dve.wait_ge(w_high, 2 * NC * e + n + 1)
                    dve.tensor_tensor(w_lo[n % 2][:], raw[:, n % R], w_hi[n % 2][:], ALU.subtract).then_inc(w_low, 1)

                def x_parts(e):
                    for j in range(KD):
                        dve.wait_ge(x_high, KD * e + j + 1)
                        dve.tensor_tensor(x_lo[:, j, :], xT_ps[j % 2][:], x_hi[:, j, :], ALU.subtract).then_inc(x_low, 1)

                def h_parts(e, n):
                    for m in range(MC):
                        dve.wait_ge(h_high, (HID // P) * e + n * MC + m + 1)
                        dve.tensor_tensor(h_lo[n * MC + m][:], hf[:, m % 2, :], h_hi[n * MC + m][:], ALU.subtract).then_inc(h_low, 1)

                def finish(e):
                    dve.wait_ge(down, NC * (e + 1))
                    dve.wait_ge(b2_in, 16 * (e + 1))
                    dve.wait_ge(stored, 16 * e + 16)
                    for s in range(CT):
                        dve.tensor_tensor(y[:, s, :], y_ps[s][:], b2_row[:], ALU.add).then_inc(y_done, 1)

                w_part(0, 0)
                x_parts(0)
                w_part(0, 1)

                def expert_(e, last):
                    for n in range(NC):
                        h_parts(e, n)
                        w_part(e, n + 2)
                    for n in range(NC):
                        if n == 1 and not last:
                            x_parts(e + 1)
                        if n < NC - 2:
                            w_part(e, NC + n + 2)
                        elif not last:
                            w_part(e + 1, n - NC + 2)
                    finish(e)
                with dve.Fori(0, E - 1) as e:
                    expert_(e, False)
                expert_(E - 1, True)

            @block.gpsimd
            def _(pool):
                with pool.Fori(0, E) as e:
                    pool.wait_ge(y_done, START + CT * e + 0)
                    pool.sem_inc(passed_p, 1)
                    pool.dma_start(b2_row[:], b2[bass.ds(e, 1), :].to_broadcast([P, D])).then_inc(b2_in, 16)


def graph_moe_kernel(nc, x, adj, W_seq, a1, a2, W_out, b_out, gate_w, w_gate, w_up, w_down, Wr, br, W1, b1, W2, b2, out):
    rows0, rows1 = NB0 * BR, E * CAP

    def scratch(name, shape):
        return nc.dram_tensor(name, shape, F32, kind="Internal").ap()
    s1_rows = scratch("s1_rows", [H, N])
    sent0, back0 = scratch("sent0", [rows0, D]), scratch("back0", [rows0, D])
    sent1, back1 = scratch("sent1", [rows1, D]), scratch("back1", [rows1, D])
    x3 = scratch("x3", [N, D])

    iso_row = nc.dram_tensor("iso_row", [1, N], BF16, kind="Internal").ap()
    adjT_dram = nc.dram_tensor("adjT_dram", [N, N], BF16, kind="Internal").ap()
    SPENT.clear()
    with ExitStack() as st:
        c = Ctx(nc, st, "all")
        k = make_constants(nc, c)
        mean, rstd, dinv = c.sb("mean", [P, NT]), c.sb("rstd", [P, NT]), c.sb("dinv", [P, NT])
        bn = c.sb("bn", [P, NT, 6])
        put_at, get_from = c.sb("put_at", [P, TOPK, NT], U32), c.sb("get_from", [P, TOPK, NT], U32)
        weight = c.sb("weight", [P, TOPK, NT])
        constants(nc, k)

        with ExitStack() as st1:
            c1 = Ctx(nc, st1, "one")
            seq = c1.sb("seq", [P, NT, D])
            with ExitStack() as st2:
                c2 = Ctx(nc, st2, "gat")
                adjT = c2.sb("adjT", [P, NT, N], BF16)
                isolated, rowsum, colsum = (c2.sb(n, [P, NT]) for n in ("isolated", "rowsum", "colsum"))
                s1, s2, ea, eb, g, ns2, big_s2 = (c2.sb(n, [P, NT, H]) for n in ("s1", "s2", "ea", "eb", "g", "ns2", "big_s2"))
                with ExitStack() as st3:
                    c3 = Ctx(nc, st3, "first")
                    x_in, w = c3.sb("x", [P, NT, D]), c3.sb("w", [P, KD, WC])
                    w_hi, w_lo = c3.sb("w_hi", [P, KD, WC], F32R), c3.sb("w_lo", [P, KD, WC], F32R)
                    transpose_adj(nc, k, adj, adjT, isolated, rowsum, colsum, x, x_in, bn, W_seq, a1, a2, w, w_hi, w_lo)
                    norm_stats(nc, "norm0", bn, mean, rstd)
                    project_heads(nc, k, x_in, mean, rstd, w_hi, w_lo, seq, s1, s2, adjT, adjT_dram, isolated, iso_row)
                softmax_factors(nc, k, s1, s2, ea, eb, g, ns2, big_s2, s1_rows, rowsum, colsum, dinv)
                attention(nc, k, adjT, seq, ea, eb, g, ns2, big_s2, s1_rows, [sent0, sent1])
            recycle(nc)
            with ExitStack() as st2:
                c2 = Ctx(nc, st2, "two")
                x_sb, block_expert = c2.sb("x", [P, NT, D]), c2.sb("block_expert", [P, NB0], I32)
                project_out(nc, k, seq, x, W_out, b_out, x_sb, bn)
                norm_stats(nc, "norm1", bn, mean, rstd)
                xn = seq
                route(nc, k, "route0", x_sb, mean, rstd, gate_w, None, xn, put_at, get_from, weight, block_expert)
                experts_gated(nc, k, block_expert, xn, put_at, sent0, w_gate, w_up, w_down, back0)
                recycle(nc)
                with ExitStack() as st3:
                    c3 = Ctx(nc, st3, "diffuse")
                    z_hi, z_lo = c3.sb("z_hi", [P, NT, D], F32R), c3.sb("z_lo", [P, NT, D], F32R)
                    graph_product(nc, "sym", adjT_dram, adj, x_sb, (back0, get_from, weight), dinv, z_hi, z_lo, seq, bn)
                    graph_product(nc, "prod", adjT_dram, None, seq, None, None, z_hi, z_lo, x_sb, bn)
                norm_stats(nc, "norm2", bn, mean, rstd)
                route(nc, k, "route1", x_sb, mean, rstd, Wr, br, xn, put_at, get_from, weight, None, table=sent1,
                      spill=x3)
            recycle(nc)
            experts_mlp(nc, k, xn, sent1, W1, b1, W2, b2, back1, x3)
            combine_out(nc, "combine", back1, get_from, weight, xn, out)


_INS = ['x', 'adj', 'L0_gnn_W_seq', 'L0_gnn_a1', 'L0_gnn_a2', 'L0_gnn_W_out', 'L0_gnn_b_out', 'L0_ffn_gate_w',
        'L0_ffn_w_gate', 'L0_ffn_w_up', 'L0_ffn_w_down', 'L1_ffn_Wr', 'L1_ffn_br', 'L1_ffn_W1', 'L1_ffn_b1',
        'L1_ffn_W2', 'L1_ffn_b2']
_OUTS = [((2048, 512), 'float32')]


def kernel(**inputs):
    import numpy as _np
    import concourse.bacc as _bacc
    from concourse import mybir as _mybir
    from concourse.bass_utils import run_bass_kernel_spmd as _run

    nc = _bacc.Bacc("TRN2", target_bir_lowering=False, num_devices=1)
    arrays, args = {}, []
    for name in _INS:
        a = _np.ascontiguousarray(inputs[name])
        arrays[f"in_{name}_dram"] = a
        args.append(nc.dram_tensor(f"in_{name}_dram", a.shape, _mybir.dt.from_np(a.dtype), kind="ExternalInput").ap())
    for i, (shape, dtype) in enumerate(_OUTS):
        dt = _mybir.dt.from_np(_np.dtype(dtype))
        args.append(nc.dram_tensor(f"out_{i}_dram", shape, dt, kind="ExternalOutput").ap())
    graph_moe_kernel(nc, *args)
    r = _run(nc, [arrays], core_ids=[0])
    got = tuple(r.results[0][f"out_{i}_dram"] for i in range(len(_OUTS)))
    return got[0]
```
